# Optimizing a Trainium2 kernel written in Bass

```python
import numpy as np
import jax
import jax.numpy as jnp

def _softmax(x, axis=-1):
    return jax.nn.softmax(x, axis=axis)

def _gelu(x):
    return jax.nn.gelu(x, approximate=True)

def _silu(x):
    return jax.nn.silu(x)

def _sigmoid(x):
    return jax.nn.sigmoid(x)

def _layernorm(x, axis=-1, eps=1e-05):
    m = jnp.mean(x, axis=axis, keepdims=True)
    v = jnp.var(x, axis=axis, keepdims=True)
    return (x - m) / jnp.sqrt(v + eps)

def _scatter_add(tgt, idx, src, axis=0):
    return tgt.at[idx].add(src)

def _segment_sum(src, seg, n):
    return jax.ops.segment_sum(src, seg, n)
kernel_name = 'mk_gnn_preln_d4_gnn_r64_4281f3'

def setup_inputs(seed: int=0):
    np.random.seed(seed)
    _w = jnp.asarray

    def _rec_inputs():
        import jax
        import jax.numpy as jnp
        _gk = jax.random.key(seed)
        x = -0.0005121 + 1.001 * jax.random.normal(jax.random.fold_in(_gk, 1), (100000, 64), jnp.float32)
        src = jax.random.randint(jax.random.fold_in(_gk, 2), (50000,), 0, 100000, jnp.int32)
        dst = jnp.minimum((100000 * jax.random.uniform(jax.random.fold_in(_gk, 3), (50000,)) ** 2.0).astype(jnp.int32), 99999)
        _o = jnp.argsort(dst, stable=True)
        src = src[_o]
        dst = dst[_o]
        edge_attr_16 = 0.000254156 + 0.999948 * jax.random.normal(jax.random.fold_in(_gk, 12), (50000, 16), jnp.float32)
        edge_type_4 = jax.random.randint(jax.random.fold_in(_gk, 14), (50000,), 0, 4, jnp.int32)
        edge_weight1 = 0.000614103 + 0.999867 * jax.random.normal(jax.random.fold_in(_gk, 15), (50000, 1), jnp.float32)
        node_type_2 = jax.random.randint(jax.random.fold_in(_gk, 16), (100000,), 0, 2, jnp.int32)
        return (x, src, dst, edge_attr_16, edge_type_4, edge_weight1, node_type_2)
    x, src, dst, edge_attr_16, edge_type_4, edge_weight1, node_type_2 = _rec_inputs()

    def _L0_gnn_setup():
        import jax, jax.numpy as jnp
        import numpy as np
        N, E = (50000, 12500)
        IN_D, HID, H1, OUT_D, H2, EDGE_D = (64, 16, 8, 64, 2, 1)
        NEG_SLOPE = 0.2

        def gatv2_layer(x, src, dst, edge_attr, Wl, Wr, We, att, bias, concat):
            n = x.shape[0]
            H, C = att.shape
            xl = (x @ Wl).reshape(n, H, C)
            xr = (x @ Wr).reshape(n, H, C)
            ee = (edge_attr @ We).reshape(-1, H, C)
            z = jax.nn.leaky_relu(xl[src] + xr[dst] + ee, NEG_SLOPE)
            score = jnp.einsum('ehc,hc->eh', z, att)
            m = jax.ops.segment_max(score, dst, num_segments=n)
            m = jnp.where(jnp.isfinite(m), m, 0.0)
            a = jnp.exp(score - m[dst])
            denom = jax.ops.segment_sum(a, dst, num_segments=n)
            alpha = a / (denom[dst] + 1e-16)
            msg = xl[src] * alpha[..., None]
            out = jax.ops.segment_sum(msg, dst, num_segments=n)
            if concat:
                return out.reshape(n, H * C) + bias
            return out.mean(axis=1) + bias

        def layer_norm(x, g, b):
            mu = x.mean(-1, keepdims=True)
            var = ((x - mu) ** 2).mean(-1, keepdims=True)
            return (x - mu) * jax.lax.rsqrt(var + 1e-05) * g + b
        key = jax.random.key(seed)
        ks = jax.random.split(key, 24)

        def w(k, *shape):
            fan_in = shape[0]
            return jax.random.normal(k, shape, dtype=jnp.float32) * (1.0 / np.sqrt(fan_in))
        inp = {'x': jax.random.normal(ks[0], (N, IN_D), dtype=jnp.float32), 'edge_index': jax.random.randint(ks[1], (2, E), 0, N, dtype=jnp.int64), 'edge_attr': jax.random.normal(ks[2], (E, EDGE_D), dtype=jnp.float32), 'w1_l': w(ks[3], IN_D, H1 * HID), 'w1_r': w(ks[4], IN_D, H1 * HID), 'w1_e': w(ks[5], EDGE_D, H1 * HID), 'att1': jax.random.normal(ks[6], (H1, HID), dtype=jnp.float32) * 0.1, 'b1': jnp.zeros((H1 * HID,), dtype=jnp.float32), 'w2_l': w(ks[7], H1 * HID, H2 * OUT_D), 'w2_r': w(ks[8], H1 * HID, H2 * OUT_D), 'w2_e': w(ks[9], EDGE_D, H2 * OUT_D), 'att2': jax.random.normal(ks[10], (H2, OUT_D), dtype=jnp.float32) * 0.1, 'b2': jnp.zeros((OUT_D,), dtype=jnp.float32), 'wc': w(ks[11], OUT_D, OUT_D), 'bc': jnp.zeros((OUT_D,), dtype=jnp.float32), 'ln_g': jnp.ones((OUT_D,), dtype=jnp.float32), 'ln_b': jnp.zeros((OUT_D,), dtype=jnp.float32), 'wr': w(ks[12], OUT_D, OUT_D), 'br': jnp.zeros((OUT_D,), dtype=jnp.float32), 'lnr_g': jnp.ones((OUT_D,), dtype=jnp.float32), 'lnr_b': jnp.zeros((OUT_D,), dtype=jnp.float32)}
        return inp
    _L0_gnn_all = _L0_gnn_setup()
    _L0_gnn_in = {k: v for k, v in _L0_gnn_all.items() if k in ('w1_l', 'w1_r', 'w1_e', 'att1', 'b1', 'w2_l', 'w2_r', 'w2_e', 'att2', 'b2', 'wc', 'bc', 'ln_g', 'ln_b', 'wr', 'br', 'lnr_g', 'lnr_b')}
    del _L0_gnn_all

    def _L1_gnn_setup():
        import jax, jax.numpy as jnp
        import numpy as np
        N_NODES = 50000
        N_EDGES = 12500
        IN_DIM = 64
        OUT_DIM = 64
        ALPHA = 0.2
        key = jax.random.key(seed)
        k1, k2, k3, k4 = jax.random.split(key, 4)
        x = jax.random.normal(k1, (N_NODES, IN_DIM), dtype=jnp.float32)
        edge_index = jax.random.randint(k2, (2, N_EDGES), 0, N_NODES, dtype=jnp.int64)
        W = jax.random.normal(k3, (OUT_DIM, IN_DIM), dtype=jnp.float32) * (1.0 / np.sqrt(IN_DIM))
        a = jax.random.normal(k4, (1, 2 * OUT_DIM), dtype=jnp.float32) * (1.0 / np.sqrt(2 * OUT_DIM))
        return {'x': x, 'edge_index': edge_index, 'W': W, 'a': a}
    _L1_gnn_all = _L1_gnn_setup()
    _L1_gnn_in = {k: v for k, v in _L1_gnn_all.items() if k in ('W', 'a')}
    del _L1_gnn_all

    def _L2_gnn_setup():
        import jax, jax.numpy as jnp
        import numpy as np
        NUM_NODE_TYPES = 2
        NUM_REL_TYPES = 4
        NUM_BASES = 8
        N_NODES = 100000
        N_EDGES = 25000
        IN_DIM = 64
        OUT_DIM = 64
        M = NUM_REL_TYPES * NUM_NODE_TYPES * NUM_NODE_TYPES
        key = jax.random.key(seed)
        ks = jax.random.split(key, 8)
        x = jax.random.normal(ks[0], (N_NODES, IN_DIM), dtype=jnp.float32)
        node_type = jax.random.randint(ks[1], (N_NODES,), 0, NUM_NODE_TYPES, dtype=jnp.int32)
        edge_src = jax.random.randint(ks[2], (N_EDGES,), 0, N_NODES, dtype=jnp.int32)
        edge_dst = jax.random.randint(ks[3], (N_EDGES,), 0, N_NODES, dtype=jnp.int32)
        edge_type = jax.random.randint(ks[4], (N_EDGES,), 0, NUM_REL_TYPES, dtype=jnp.int32)
        weight = jax.random.normal(ks[5], (NUM_BASES, IN_DIM, OUT_DIM), dtype=jnp.float32) * 0.05
        w_comp = jax.random.normal(ks[6], (M, NUM_BASES), dtype=jnp.float32) * 0.3
        bias = jax.random.normal(ks[7], (1, OUT_DIM), dtype=jnp.float32) * 0.1
        return {'x': x, 'node_type': node_type, 'edge_src': edge_src, 'edge_dst': edge_dst, 'edge_type': edge_type, 'weight': weight, 'w_comp': w_comp, 'bias': bias}
    _L2_gnn_all = _L2_gnn_setup()
    _L2_gnn_in = {k: v for k, v in _L2_gnn_all.items() if k in ('weight', 'w_comp', 'bias')}
    del _L2_gnn_all

    def _L3_gnn_setup():
        import jax, jax.numpy as jnp
        import numpy as np
        N, E = (50000, 12500)
        NODE_DIM, EDGE_DIM, HEADS = (64, 16, 4)
        C = NODE_DIM // HEADS
        NEG_SLOPE = 0.2
        BN_EPS = 1e-05
        key = jax.random.key(seed)
        ks = jax.random.split(key, 12)
        glorot = lambda k, shape: jax.random.normal(k, shape, jnp.float32) * np.sqrt(2.0 / (shape[0] + shape[-1]))
        return {'x': jax.random.normal(ks[0], (N, NODE_DIM), jnp.float32), 'edge_index': jax.random.randint(ks[1], (2, E), 0, N, jnp.int32), 'edge_attr': jax.random.normal(ks[2], (E, EDGE_DIM), jnp.float32), 'W_l': glorot(ks[3], (NODE_DIM, HEADS * C)), 'b_l': jnp.zeros((HEADS * C,), jnp.float32), 'W_r': glorot(ks[4], (NODE_DIM, HEADS * C)), 'b_r': jnp.zeros((HEADS * C,), jnp.float32), 'W_e': glorot(ks[5], (EDGE_DIM, HEADS * C)), 'att': glorot(ks[6], (HEADS, C)), 'bias': jnp.zeros((HEADS * C,), jnp.float32), 'gamma': jnp.ones((NODE_DIM,), jnp.float32), 'beta': jnp.zeros((NODE_DIM,), jnp.float32)}
    _L3_gnn_all = _L3_gnn_setup()
    _L3_gnn_in = {k: v for k, v in _L3_gnn_all.items() if k in ('W_l', 'b_l', 'W_r', 'b_r', 'W_e', 'att', 'bias', 'gamma', 'beta')}
    del _L3_gnn_all
    return {'x': x, 'src': src, 'dst': dst, 'edge_attr_16': edge_attr_16, 'edge_type_4': edge_type_4, 'edge_weight1': edge_weight1, 'node_type_2': node_type_2, 'L0_gnn_w1_l': _L0_gnn_in['w1_l'], 'L0_gnn_w1_r': _L0_gnn_in['w1_r'], 'L0_gnn_w1_e': _L0_gnn_in['w1_e'], 'L0_gnn_att1': _L0_gnn_in['att1'], 'L0_gnn_b1': _L0_gnn_in['b1'], 'L0_gnn_w2_l': _L0_gnn_in['w2_l'], 'L0_gnn_w2_r': _L0_gnn_in['w2_r'], 'L0_gnn_w2_e': _L0_gnn_in['w2_e'], 'L0_gnn_att2': _L0_gnn_in['att2'], 'L0_gnn_b2': _L0_gnn_in['b2'], 'L0_gnn_wc': _L0_gnn_in['wc'], 'L0_gnn_bc': _L0_gnn_in['bc'], 'L0_gnn_ln_g': _L0_gnn_in['ln_g'], 'L0_gnn_ln_b': _L0_gnn_in['ln_b'], 'L0_gnn_wr': _L0_gnn_in['wr'], 'L0_gnn_br': _L0_gnn_in['br'], 'L0_gnn_lnr_g': _L0_gnn_in['lnr_g'], 'L0_gnn_lnr_b': _L0_gnn_in['lnr_b'], 'L1_gnn_W': _L1_gnn_in['W'], 'L1_gnn_a': _L1_gnn_in['a'], 'L2_gnn_weight': _L2_gnn_in['weight'], 'L2_gnn_w_comp': _L2_gnn_in['w_comp'], 'L2_gnn_bias': _L2_gnn_in['bias'], 'L3_gnn_W_l': _L3_gnn_in['W_l'], 'L3_gnn_b_l': _L3_gnn_in['b_l'], 'L3_gnn_W_r': _L3_gnn_in['W_r'], 'L3_gnn_b_r': _L3_gnn_in['b_r'], 'L3_gnn_W_e': _L3_gnn_in['W_e'], 'L3_gnn_att': _L3_gnn_in['att'], 'L3_gnn_bias': _L3_gnn_in['bias'], 'L3_gnn_gamma': _L3_gnn_in['gamma'], 'L3_gnn_beta': _L3_gnn_in['beta']}

def reference(x, src, dst, edge_attr_16, edge_type_4, edge_weight1, node_type_2, L0_gnn_w1_l, L0_gnn_w1_r, L0_gnn_w1_e, L0_gnn_att1, L0_gnn_b1, L0_gnn_w2_l, L0_gnn_w2_r, L0_gnn_w2_e, L0_gnn_att2, L0_gnn_b2, L0_gnn_wc, L0_gnn_bc, L0_gnn_ln_g, L0_gnn_ln_b, L0_gnn_wr, L0_gnn_br, L0_gnn_lnr_g, L0_gnn_lnr_b, L1_gnn_W, L1_gnn_a, L2_gnn_weight, L2_gnn_w_comp, L2_gnn_bias, L3_gnn_W_l, L3_gnn_b_l, L3_gnn_W_r, L3_gnn_b_r, L3_gnn_W_e, L3_gnn_att, L3_gnn_bias, L3_gnn_gamma, L3_gnn_beta):
    import jax
    import jax.numpy as jnp

    def _L0_gnn_ref(x, edge_index, edge_attr, w1_l, w1_r, w1_e, att1, b1, w2_l, w2_r, w2_e, att2, b2, wc, bc, ln_g, ln_b, wr, br, lnr_g, lnr_b):
        import jax, jax.numpy as jnp
        import numpy as np
        N, E = (50000, 12500)
        IN_D, HID, H1, OUT_D, H2, EDGE_D = (64, 16, 8, 64, 2, 1)
        NEG_SLOPE = 0.2

        def gatv2_layer(x, src, dst, edge_attr, Wl, Wr, We, att, bias, concat):
            n = x.shape[0]
            H, C = att.shape
            xl = (x @ Wl).reshape(n, H, C)
            xr = (x @ Wr).reshape(n, H, C)
            ee = (edge_attr @ We).reshape(-1, H, C)
            z = jax.nn.leaky_relu(xl[src] + xr[dst] + ee, NEG_SLOPE)
            score = jnp.einsum('ehc,hc->eh', z, att)
            m = jax.ops.segment_max(score, dst, num_segments=n)
            m = jnp.where(jnp.isfinite(m), m, 0.0)
            a = jnp.exp(score - m[dst])
            denom = jax.ops.segment_sum(a, dst, num_segments=n)
            alpha = a / (denom[dst] + 1e-16)
            msg = xl[src] * alpha[..., None]
            out = jax.ops.segment_sum(msg, dst, num_segments=n)
            if concat:
                return out.reshape(n, H * C) + bias
            return out.mean(axis=1) + bias

        def layer_norm(x, g, b):
            mu = x.mean(-1, keepdims=True)
            var = ((x - mu) ** 2).mean(-1, keepdims=True)
            return (x - mu) * jax.lax.rsqrt(var + 1e-05) * g + b
        src, dst = (edge_index[0], edge_index[1])
        h = jax.nn.relu(gatv2_layer(x, src, dst, edge_attr, w1_l, w1_r, w1_e, att1, b1, True))
        h = jax.nn.relu(gatv2_layer(h, src, dst, edge_attr, w2_l, w2_r, w2_e, att2, b2, False))
        h = jax.nn.gelu(layer_norm(h @ wc + bc, ln_g, ln_b), approximate=False)
        h = h + jax.nn.gelu(layer_norm(h @ wr + br, lnr_g, lnr_b), approximate=False)
        return h

    def _L1_gnn_ref(x, edge_index, W, a):
        import jax, jax.numpy as jnp
        import numpy as np
        N_NODES = 50000
        N_EDGES = 12500
        IN_DIM = 64
        OUT_DIM = 64
        ALPHA = 0.2
        num_nodes = x.shape[0]
        h = x @ W.T
        src, dst = (edge_index[0], edge_index[1])
        a_src = a[0, :OUT_DIM]
        a_dst = a[0, OUT_DIM:]
        e = jax.nn.leaky_relu(h[src] @ a_src + h[dst] @ a_dst, ALPHA)
        seg_max = jax.ops.segment_max(e, src, num_segments=num_nodes)
        exp_e = jnp.exp(e - seg_max[src])
        denom = jax.ops.segment_sum(exp_e, src, num_segments=num_nodes)
        attention = exp_e / denom[src]
        h_prime = jax.ops.segment_sum(attention[:, None] * h[src], dst, num_segments=num_nodes)
        return jax.nn.elu(h_prime)

    def _L2_gnn_ref(x, node_type, edge_src, edge_dst, edge_type, weight, w_comp, bias):
        import jax, jax.numpy as jnp
        import numpy as np
        NUM_NODE_TYPES = 2
        NUM_REL_TYPES = 4
        NUM_BASES = 8
        N_NODES = 100000
        N_EDGES = 25000
        IN_DIM = 64
        OUT_DIM = 64
        M = NUM_REL_TYPES * NUM_NODE_TYPES * NUM_NODE_TYPES
        T, R = (NUM_NODE_TYPES, NUM_REL_TYPES)
        n_nodes = x.shape[0]
        w_flat = weight.reshape(OUT_DIM, NUM_BASES, IN_DIM)
        comb = jnp.matmul(w_comp, w_flat)
        W = comb.reshape(M, OUT_DIM, IN_DIM)
        rel = node_type[edge_src] * (T * R) + node_type[edge_dst] * R + edge_type
        all_msgs = jnp.einsum('ni,moi->nmo', x, W)
        msg = all_msgs[edge_src, rel]
        agg = jax.ops.segment_sum(msg, edge_dst, num_segments=n_nodes)
        out = agg + bias
        return out

    def _L3_gnn_ref(x, edge_index, edge_attr, W_l, b_l, W_r, b_r, W_e, att, bias, gamma, beta):
        import jax, jax.numpy as jnp
        import numpy as np
        N, E = (50000, 12500)
        NODE_DIM, EDGE_DIM, HEADS = (64, 16, 4)
        C = NODE_DIM // HEADS
        NEG_SLOPE = 0.2
        BN_EPS = 1e-05
        src, dst = (edge_index[0], edge_index[1])
        n = x.shape[0]
        xl = (x @ W_l + b_l).reshape(n, HEADS, C)
        xr = (x @ W_r + b_r).reshape(n, HEADS, C)
        e = (edge_attr @ W_e).reshape(-1, HEADS, C)
        g = jax.nn.leaky_relu(xl[src] + xr[dst] + e, NEG_SLOPE)
        logits = jnp.einsum('ehc,hc->eh', g, att)
        amax = jax.ops.segment_max(logits, dst, num_segments=n)
        ex = jnp.exp(logits - amax[dst])
        denom = jax.ops.segment_sum(ex, dst, num_segments=n)
        alpha = ex / (denom[dst] + 1e-16)
        msg = xl[src] * alpha[..., None]
        out = jax.ops.segment_sum(msg, dst, num_segments=n).reshape(n, HEADS * C) + bias
        mean = out.mean(axis=0)
        var = out.var(axis=0)
        out = (out - mean) * jax.lax.rsqrt(var + BN_EPS) * gamma + beta
        return jax.nn.gelu(out + x, approximate=False)
    edge_index = jnp.stack([src, dst])
    h = jnp.maximum(_layernorm(x, axis=-1), 0.0)
    x = x + _L0_gnn_ref(h, edge_index, edge_weight1, L0_gnn_w1_l, L0_gnn_w1_r, L0_gnn_w1_e, L0_gnn_att1, L0_gnn_b1, L0_gnn_w2_l, L0_gnn_w2_r, L0_gnn_w2_e, L0_gnn_att2, L0_gnn_b2, L0_gnn_wc, L0_gnn_bc, L0_gnn_ln_g, L0_gnn_ln_b, L0_gnn_wr, L0_gnn_br, L0_gnn_lnr_g, L0_gnn_lnr_b)
    h = jnp.maximum(_layernorm(x, axis=-1), 0.0)
    x = x + _L1_gnn_ref(h, edge_index, L1_gnn_W, L1_gnn_a)
    h = jnp.maximum(_layernorm(x, axis=-1), 0.0)
    x = x + _L2_gnn_ref(h, node_type_2, src, dst, edge_type_4, L2_gnn_weight, L2_gnn_w_comp, L2_gnn_bias)
    h = jnp.maximum(_layernorm(x, axis=-1), 0.0)
    x = x + _L3_gnn_ref(h, edge_index, edge_attr_16, L3_gnn_W_l, L3_gnn_b_l, L3_gnn_W_r, L3_gnn_b_r, L3_gnn_W_e, L3_gnn_att, L3_gnn_bias, L3_gnn_gamma, L3_gnn_beta)
    return x

_drawn_inputs = setup_inputs


def setup_inputs(seed=0):
    import zlib

    import numpy as np

    out = dict(_drawn_inputs(seed))
    spreads = {'L0_gnn_b1': (0.0, 0.1),
     'L0_gnn_b2': (0.0, 0.1),
     'L0_gnn_bc': (0.0, 0.1),
     'L0_gnn_ln_g': (1.0, 0.2),
     'L0_gnn_ln_b': (0.0, 0.1),
     'L0_gnn_br': (0.0, 0.1),
     'L0_gnn_lnr_g': (1.0, 0.2),
     'L0_gnn_lnr_b': (0.0, 0.1),
     'L3_gnn_b_l': (0.0, 0.1),
     'L3_gnn_b_r': (0.0, 2.0),
     'L3_gnn_bias': (0.0, 2.0),
     'L3_gnn_gamma': (1.0, 0.2),
     'L3_gnn_beta': (0.0, 0.306)}
    factors = {'L0_gnn_w1_r': 8.0,
     'L0_gnn_w1_e': 5.721,
     'L0_gnn_att1': 2.713,
     'L0_gnn_w2_r': 23.441,
     'L0_gnn_w2_e': 4.289,
     'L1_gnn_a': 4.828,
     'L3_gnn_W_r': 3.839}
    for name, (base, spread) in spreads.items():
        noise = np.random.default_rng([zlib.crc32(name.encode()), seed]).standard_normal(out[name].shape)
        drawn = base * np.exp(spread * noise) if base else spread * noise
        out[name] = jnp.asarray(drawn.astype(out[name].dtype))
    for name, factor in factors.items():
        out[name] = (out[name] * factor).astype(out[name].dtype)
    return out
```

```python
from contextlib import ExitStack

import concourse.bass as bass
from concourse import mybir

ALU = mybir.AluOpType
ACT = mybir.ActivationFunctionType
F32 = mybir.dt.float32
I32 = mybir.dt.int32
X = mybir.AxisListType.X

P = 128
N, D = 100000, 64
E = 50000
CH = 512
J = CH // P
NCH = -(-E // CH)
EP = NCH * CH
EF = EP // P
U = 2
NIT = NCH // U
SENT = EP - 1
BIG = 1.0e30
SKIP = 1 << 20
NTAB = -(-N // P)
EPS = 1e-5
SLOPE = 0.2
NEDGE_IDX = 4
SORTED = 1 << (E - 1).bit_length()
SF = SORTED // P
SLAST = E - (P - 1) * EF


class Chain:

    def __init__(self, eng, sem, per_step):
        self.eng, self.sem, self.per = eng, sem, per_step

    def at(self, it):
        self.base, self.n = it * self.per, 0

    def __call__(self, ins):
        self.n += 1
        ins.then_inc(self.sem, 1)
        self.eng.wait_ge(self.sem, self.base + self.n)

    def done(self):
        assert self.n == self.per, (self.n, self.per)


def steps(eng, body, last=NIT):
    body(0, True)
    with eng.Fori(1, last) as it:
        body(it, False)


def hold(eng, turn, *waits):
    for sem, value in waits:
        eng.wait_ge(sem, value)
        eng.sem_inc(turn, 1)


def rows(dram, it, k, width=None):
    v = dram[bass.ds((it * U + k) * CH, CH), :]
    return v.rearrange("(p j) d -> p j d", j=J)


def words(dram, it, k):
    return dram[bass.ds((it * U + k) * CH, CH)].rearrange("(p j) -> p j", j=J)


def cols(dram, it, k):
    return dram[:, bass.ds((it * U + k) * CH, CH)]


def line(dram, it, k, parts):
    return dram[bass.ds((it * U + k) * CH, CH)].unsqueeze(0).partition_broadcast(parts)


def bcast(ap, n):
    return ap.unsqueeze(2).to_broadcast([ap.shape[0], ap.shape[1], n])


class Mem:

    def __init__(self, nc, ctx, tag):
        self.nc, self.ctx, self.tag = nc, ctx, tag
        self.semaphores = []
        ctx.callback(self.close)

    def close(self):
        if self.semaphores:
            self.nc.clear_and_free_semaphores(self.semaphores)
            self.nc.all_engine_barrier()

    def sb(self, name, shape, dt=F32):
        return self.ctx.enter_context(self.nc.sbuf_tensor(f"{self.tag}_{name}", shape, dt))

    def ps(self, name, shape, dt=F32):
        return self.ctx.enter_context(self.nc.psum_tensor(f"{self.tag}_{name}", shape, dt))

    def sem(self, name):
        self.semaphores.append(self.nc.alloc_semaphore(f"{self.tag}_{name}"))
        return self.semaphores[-1]

    def sems(self, name, n=U):
        return [self.sem(f"{name}{i}") for i in range(n)]



def setup_block(nc, a, T, C):
    with ExitStack() as ctx:
        m = Mem(nc, ctx, "su")
        dstp = m.sb("dstp", [P, EF], I32)
        dstc = m.sb("dstc", [P, EF], I32)
        dstn = m.sb("dstn", [P, EF], I32)
        srci = m.sb("srci", [P, EF], I32)
        ewp = m.sb("ewp", [P, EF])
        etp = m.sb("etp", [P, EF], I32)
        fp = m.sb("fp", [P, EF])
        fc = m.sb("fc", [P, EF])
        fn = m.sb("fn", [P, EF])
        st = m.sb("st", [P, EF])
        keep = m.sb("keep", [P, EF])
        en = m.sb("en", [P, EF])
        t1 = m.sb("t1", [P, EF])
        dstg = m.sb("dstg", [P, EF], I32)
        scat = m.sb("scat", [P, EF], I32)
        etf = m.sb("etf", [P, EF])
        pos = m.sb("pos", [P, EF], I32)
        lp0 = m.sb("lp0", [P, NTAB], I32)
        eap = m.sb("eap", [18, EP - E])
        ones = m.sb("ones", [2, CH * 7])
        minus = m.sb("minus", [1, 1])
        zeros = m.sb("zeros", [P, (SORTED - EP) // P])
        pads, loads, stores = m.sem("pads"), m.sem("loads"), m.sem("stores")
        cst, dv, pl = m.sem("cst"), m.sem("dv"), m.sem("pl")
        wl = m.sem("wl")
        block = ctx.enter_context(nc.Block())
        NLOAD = [0]

        @block.vector
        def _(dve):
            nc.vector.memset(dstp[:, :], N + 1)
            nc.vector.memset(dstc[:, :], N)
            nc.vector.memset(dstn[:, :], N)
            nc.vector.memset(srci[:, :], 0)
            nc.vector.memset(ewp[:, :], 0.0)
            nc.vector.memset(etp[:, :], 0)
            nc.vector.memset(lp0[:, :], SENT)
            nc.vector.memset(eap[:, :], 0.0)
            nc.vector.memset(ones[:, :], 1.0)
            for t, v in ((C["ident"], 0.0), (C["sel8"], 1.0), (C["sel2"], 1.0), (C["sel4"], 1.0), (C["mean2"], 0.0), (C["att1b"], 0.0),
                         (C["att2b"], 0.0), (C["att3b"], 0.0), (C["cstk"], 0.0), (C["ones_sq"], 1.0), (minus, -1.0),
                         (zeros, 0.0)):
                nc.vector.memset(t[:, :], v)
            nc.vector.memset(C["ones_row"][:, :], 1.0).then_inc(pads, 1)
            dve.wait_ge(loads, 16 * 13)
            ch = Chain(dve, dv, 99)
            ch.at(0)
            nc.vector.tensor_copy(fp[:, :], dstp[:, :])
            nc.vector.tensor_copy(fc[:, :], dstc[:, :])
            nc.vector.tensor_copy(etf[:, :], etp[:, :])
            ch(nc.vector.tensor_copy(fn[:, :], dstn[:, :]))
            nc.vector.tensor_tensor(keep[:, :], fp[:, :], fc[:, :], ALU.is_equal)
            ch(nc.vector.tensor_tensor(en[:, :], fn[:, :], fc[:, :], ALU.is_equal))
            nc.vector.tensor_scalar(st[:, :], keep[:, :], -1.0, BIG, ALU.add, ALU.mult)
            nc.vector.scalar_tensor_tensor(t1[:, :], en[:, :], float(SKIP), fc[:, :], ALU.mult, ALU.add)
            ch(nc.vector.tensor_scalar(dstg[:, :], fc[:, :], float(N - 1), None, ALU.min))
            ch(nc.vector.tensor_copy(scat[:, :], t1[:, :]))
            nc.vector.tensor_scalar(en[:, :], en[:, :], -1.0, 1.0, ALU.mult, ALU.add)
            ch(nc.vector.tensor_scalar(t1[:, :], fc[:, :], float(N) - 0.5, None, ALU.is_lt))
            ch(nc.vector.tensor_tensor(en[:, :], en[:, :], t1[:, :], ALU.mult))

        @block.gpsimd
        def _(pool):
            nc.gpsimd.iota(pos[:, :], [[1, EF]], base=0, channel_multiplier=EF).then_inc(pl, 1)
            pool.wait_ge(pads, 1)
            nc.gpsimd.affine_select(out=C["ident"][:, :], in_=C["ident"][:, :], compare_op=ALU.not_equal, fill=1.0,
                                    base=0, pattern=[[-1, P]], channel_multiplier=1)
            n = 1
            for name, w in (("sel8", 16), ("sel2", 64), ("sel4", 16)):
                t = C[name]
                cols_ = t.shape[1]
                nc.gpsimd.affine_select(out=t[:, :], in_=t[:, :], compare_op=ALU.is_ge, fill=0.0, base=0,
                                        pattern=[[1, cols_]], channel_multiplier=-w).then_inc(pl, 1)
                n += 1
                pool.wait_ge(pl, n)
                nc.gpsimd.affine_select(out=t[:, :], in_=t[:, :], compare_op=ALU.is_ge, fill=0.0, base=w - 1,
                                        pattern=[[-1, cols_]], channel_multiplier=w).then_inc(pl, 1)
                n += 1
            for half in range(2):
                nc.gpsimd.affine_select(out=C["mean2"][:, :], in_=C["mean2"][:, :], compare_op=ALU.not_equal, fill=0.5,
                                        base=-D * half, pattern=[[-1, D]], channel_multiplier=1).then_inc(pl, 1)
                n += 1
                pool.wait_ge(pl, n)

        @block.sync
        def _(sp):
            sp.wait_ge(pads, 1)

            def padded(dst, src, before=0):
                lo = EF - before
                if before == 1:
                    sp.dma_start(dst[0:1, 1:EF], src[0:lo].unsqueeze(0)).then_inc(loads, 16)
                    sp.dma_start(dst[1:P - 1, :], src[lo:lo + (P - 2) * EF].rearrange("(p f) -> p f", f=EF)).then_inc(loads, 16)
                    left = E - lo - (P - 2) * EF
                    sp.dma_start(dst[P - 1:P, 0:left], src[E - left:E].unsqueeze(0)).then_inc(loads, 16)
                else:
                    full = (P - 1) * EF
                    s0 = -before
                    sp.dma_start(dst[0:P - 1, :], src[s0:s0 + full].rearrange("(p f) -> p f", f=EF)).then_inc(loads, 16)
                    left = E - s0 - full
                    sp.dma_start(dst[P - 1:P, 0:left], src[s0 + full:E].unsqueeze(0)).then_inc(loads, 16)

            padded(dstp, a["dst"], 1)
            padded(dstc, a["dst"])
            padded(dstn, a["dst"], -1)
            padded(srci, a["src"])
            padded(ewp, a["edge_weight1"].rearrange("e a -> (e a)"))

            padded(etp, a["edge_type_4"])
            sp.wait_ge(loads, 16 * 13)
            sp.wait_ge(dv, 6)
            sp.wait_ge(pl, 1)
            full = lambda t: t.rearrange("(p f) -> p f", f=EF)
            n = 0
            for dram, sbt in ((T["SRC"], srci), (T["DST"], dstg), (T["SCAT"], scat), (T["POS"], pos), (T["START"], st),
                              (T["KEEP"], keep), (T["ENDM"], en), (T["EW"], ewp), (T["ET"], etf)):
                sp.dma_start(full(dram), sbt[:, :]).then_inc(stores, 16)
                n += 16
            sp.dma_start(T["LP"].rearrange("(p f) -> p f", f=NTAB), lp0[:, :]).then_inc(stores, 16)
            sp.dma_start(T["EA"][0:16, 0:E], a["edge_attr_t"]).then_inc(stores, 16)
            sp.dma_start(T["EA"][0:16, E:EP], eap[0:16, :]).then_inc(stores, 16)
            n += 48
            sp.dma_start(T["EA"][16:18, :].rearrange("a (b c) -> a b c", c=CH * 7),
                         ones[:, :].unsqueeze(1).to_broadcast([2, NCH // 7, CH * 7])).then_inc(stores, 16)
            n += 16
            tail_of = lambda t: t[EP:SORTED].rearrange("(p f) -> p f", p=P)
            sp.dma_start(tail_of(T["EL"]), zeros[:, :]).then_inc(stores, 16)
            sp.dma_start(tail_of(T["AL"]), zeros[:, :]).then_inc(stores, 16)
            sp.dma_start(T["AL"][0:EP].rearrange("(p f) -> p f", f=EF), ewp[:, :]).then_inc(stores, 16)
            sp.dma_start(T["SSRC"][0:1].unsqueeze(0), minus[:, :]).then_inc(stores, 16)
            n += 64
            sp.wait_ge(stores, n)

        @block.scalar
        def _(act):
            act.wait_ge(pads, 1)
            n = 0

            def load(dst, src):
                act.dma_start(dst, src).then_inc(wl, 16)
                return 1
            n += load(C["wz1"][0:64, :], a["L0_gnn_w1_l"])
            n += load(C["wz1"][64:128, :], a["L0_gnn_w1_r"])
            n += load(C["we1"][:, :], a["L0_gnn_w1_e"])
            n += load(C["wl2"][:, :], a["L0_gnn_w2_l"])
            n += load(C["wr2"][:, :], a["L0_gnn_w2_r"])
            n += load(C["we2"][:, :], a["L0_gnn_w2_e"])
            n += load(C["wz3"][0:64, :], a["L3_gnn_W_l"])
            n += load(C["wz3"][64:128, :], a["L3_gnn_W_r"])
            n += load(C["we3"][0:16, :], a["L3_gnn_W_e"])
            n += load(C["we3"][16:17, :], a["L3_gnn_b_l"].unsqueeze(0))
            n += load(C["we3"][17:18, :], a["L3_gnn_b_r"].unsqueeze(0))
            n += load(C["b1"][:, :], a["L0_gnn_b1"].unsqueeze(1))
            n += load(C["b2"][:, :], a["L0_gnn_b2"].unsqueeze(1))
            n += load(C["bl3"][:, :], a["L3_gnn_b_l"].unsqueeze(1))
            n += load(C["b1row"][:, :], a["L0_gnn_b1"].unsqueeze(0))
            for name, key in (("lng", "L0_gnn_ln_g"), ("lnb", "L0_gnn_ln_b"), ("lrg", "L0_gnn_lnr_g"), ("lrb", "L0_gnn_lnr_b"),
                              ("gamma", "L3_gnn_gamma"), ("beta", "L3_gnn_beta"), ("bias3", "L3_gnn_bias")):
                n += load(C[name][:, :], a[key].unsqueeze(0).partition_broadcast(P))
            n += load(C["bias2"][:, :], a["L2_gnn_bias"].partition_broadcast(P))
            for name, w, b in (("wca", "L0_gnn_wc", "L0_gnn_bc"), ("wra", "L0_gnn_wr", "L0_gnn_br")):
                n += load(C[name][0:D, :], a[w])
                n += load(C[name][D:D + 1, :], a[b].unsqueeze(0))
            n += load(C["w1"][:, :], a["L1_gnn_W"])
            for q in range(2):
                n += load(C["a1"][:, q:q + 1], a["L1_gnn_a"][0, q * D:(q + 1) * D].unsqueeze(1))
            n += load(C["wflat"][:, :, :], a["L2_gnn_weight"].rearrange("b i o -> (b i o)").rearrange("(q p i) -> p q i", p=P, i=D))
            comp = a["w_comp_t"]
            for r in range(4):
                for q in range(4):
                    n += load(C["cstk"][32 * r + 8 * q:32 * r + 8 * q + 8, 16 * q:16 * q + 16], comp)
            for name, key, H, W in (("att1b", "L0_gnn_att1", 8, 16), ("att2b", "L0_gnn_att2", 2, 64), ("att3b", "L3_gnn_att", 4, 16)):
                for h in range(H):
                    n += load(C[name][h * W:(h + 1) * W, h:h + 1], a[key][h].unsqueeze(1))
            act.wait_ge(wl, 16 * n)


def index_block(nc, a, T, C):
    with ExitStack() as ctx:
        m = Mem(nc, ctx, "ix")
        si = [m.sb(f"si{k}", [P, J], I32) for k in range(U)]
        pv = [m.sb(f"pv{k}", [P, J], I32) for k in range(U)]
        s_in, s_sc = m.sems("in"), m.sems("sc")
        ii = [m.sb(f"ii{k}", [P, 2, J], I32) for k in range(U)]
        go = [m.sb(f"go{k}", [P, NEDGE_IDX, J], I32) for k in range(U)]
        s_ii, s_g, s_out = m.sems("ii"), m.sems("g"), m.sems("out")
        turn = m.sem("turn")
        key = [m.sb(f"key{i}", [P, SF]) for i in range(2)]
        pay = [m.sb(f"pay{i}", [P, SF]) for i in range(2)]
        tmp = [m.sb(f"tmp{i}", [P, SF // 2]) for i in range(3)]
        sign = m.sb("sign", [P, SF])
        bits = m.sb("bits", [P, SF], I32)
        place = m.sb("place", [P, SF], I32)
        srcs = m.sb("srcs", [P, SF], I32)
        eid = m.sb("eid", [P, SF], I32)
        bk, bp = m.ps("bk", [P, SF]), m.ps("bp", [P, SF])
        full = E // SF
        s_sort, s_seed, s_cl, s_ld, s_tq, s_tp, s_tr, sorted_, s_so = (
            m.sem(x) for x in "sort seed cl ld tq tp tr sorted so".split())
        lp = T["LP"].unsqueeze(1)
        nt = a["node_type_2"].unsqueeze(1)
        block = ctx.enter_context(nc.Block())

        @block.sync
        def _(sp):
            def positions(it, first):
                for k in range(U):
                    if not first:
                        sp.wait_ge(s_sc[k], 16 * J * it)
                    sp.dma_start(si[k][:, :], words(T["SCAT"], it, k)).then_inc(s_in[k], 16)
                    sp.dma_start(pv[k][:, :], words(T["POS"], it, k)).then_inc(s_in[k], 16)
            steps(sp, positions)

            def store(it, k):
                sp.wait_ge(s_g[k], 16 * J * NEDGE_IDX * (it + 1))
                for q, name in enumerate(("PSRC", "PDST", "NTS", "NTD")):
                    sp.dma_start(words(T[name], it, k), go[k][:, q, :]).then_inc(s_out[k], 16)

            def indices(it, first):
                for k in range(U):
                    if not first:
                        store(it - 1, k)
                    sp.dma_start(ii[k][:, 0, :], words(T["SRC"], it, k)).then_inc(s_ii[k], 16)
                    sp.dma_start(ii[k][:, 1, :], words(T["DST"], it, k)).then_inc(s_ii[k], 16)
            steps(sp, indices)
            for k in range(U):
                store(NIT - 1, k)
            for k in range(U):
                sp.wait_ge(s_out[k], 16 * NEDGE_IDX * NIT)
            sp.wait_ge(sorted_, 1)
            sp.dma_start(T["SSRC"][1:1 + SORTED].rearrange("(p f) -> p f", p=P), key[0][:, :]).then_inc(s_so, 16)
            sp.dma_start(T["EID"].rearrange("(p f) -> p f", p=P), eid[:, :]).then_inc(s_so, 16)
            sp.wait_ge(s_so, 32)

        @block.gpsimd
        def _(pool):
            nc.gpsimd.iota(place[:, :], [[1, SF]], base=0, channel_multiplier=SF).then_inc(s_seed, 1)

            def scatter(it, first):
                for k in range(U):
                    hold(pool, turn, (s_in[k], 32 * (it + 1)))
                    for j in range(J):
                        nc.gpsimd.indirect_dma_start(lp, bass.IndirectOffsetOnAxis(ap=si[k][:, j:j + 1], axis=0),
                                                     pv[k][:, j:j + 1], None, bounds_check=N - 1,
                                                     oob_is_err=False).then_inc(s_sc[k], 16)
            steps(pool, scatter)
            for k in range(U):
                pool.wait_ge(s_sc[k], 16 * J * NIT)

            def gather(it, first):
                for k in range(U):
                    hold(pool, turn, (s_ii[k], 32 * (it + 1)))
                    if not first:
                        hold(pool, turn, (s_out[k], 16 * NEDGE_IDX * it))
                    for q, (table, at) in enumerate(((lp, 0), (lp, 1), (nt, 0), (nt, 1))):
                        for j in range(J):
                            nc.gpsimd.indirect_dma_start(
                                go[k][:, q, j:j + 1], None, table,
                                bass.IndirectOffsetOnAxis(ap=ii[k][:, at, j:j + 1], axis=0)).then_inc(s_g[k], 16)
            steps(pool, gather)

        merges = range(1, SORTED.bit_length())
        inner = SF.bit_length() - 1
        turns = [k for k in merges if k > inner]

        @block.vector
        def _(dve):
            v = nc.vector
            ch = Chain(dve, s_sort, 0)
            ch.at(0)
            v.memset(sign[:, :], 1.0)
            v.memset(srcs[:, :], SKIP).then_inc(s_cl, 1)
            dve.wait_ge(s_seed, 1)
            ch(v.tensor_copy(pay[0][:, :], place[:, :]))
            dve.wait_ge(s_ld, 16 * 2)
            dve.wait_ge(s_cl, 1)
            ch(v.tensor_copy(key[0][:, :], srcs[:, :]))
            cur, nt_, half = 0, 0, SORTED // P // 2

            def exchange(cur, d):
                a_ = lambda t: t[:, :].rearrange("p (g two d) -> p g two d", two=2, d=d)
                h_ = lambda t: t[:, :].rearrange("p (g d) -> p g d", d=d)
                ka, kb = a_(key[cur])[:, :, 0, :], a_(key[cur])[:, :, 1, :]
                pa, pb = a_(pay[cur])[:, :, 0, :], a_(pay[cur])[:, :, 1, :]
                nk, np_ = a_(key[1 - cur]), a_(pay[1 - cur])
                v.tensor_tensor(h_(tmp[0]), ka, kb, ALU.is_gt)
                ch(v.tensor_tensor(h_(tmp[1]), pb, pa, ALU.subtract))
                v.tensor_tensor(nk[:, :, 0, :], ka, kb, ALU.min)
                v.tensor_tensor(nk[:, :, 1, :], ka, kb, ALU.max)
                ch(v.tensor_tensor(tmp[2][:, :], tmp[0][:, :], tmp[1][:, :], ALU.mult))
                v.tensor_tensor(np_[:, :, 0, :], pa, h_(tmp[2]), ALU.add)
                ch(v.tensor_tensor(np_[:, :, 1, :], pb, h_(tmp[2]), ALU.subtract))
                return 1 - cur

            def turn_tiles(cur, n):
                v.memset(tmp[0][:, 0:1], 0.0).then_inc(s_tq, 1)
                dve.wait_ge(s_tr, n + 1)
                return n + 1

            for k in merges:
                ch(v.tensor_scalar(bits[:, :], place[:, :], k, 1, ALU.logical_shift_right, ALU.bitwise_and))
                ch(v.tensor_tensor(key[cur][:, :], key[cur][:, :], sign[:, :], ALU.mult))
                ch(v.tensor_scalar(sign[:, :], bits[:, :], -2.0, 1.0, ALU.mult, ALU.add))
                ch(v.tensor_tensor(key[cur][:, :], key[cur][:, :], sign[:, :], ALU.mult))
                if k > inner:
                    nt_ = turn_tiles(cur, nt_)
                    for j in range(k - 1, inner - 1, -1):
                        cur = exchange(cur, 1 << (j - inner))
                    nt_ = turn_tiles(cur, nt_)
                for j in range(min(k, inner) - 1, -1, -1):
                    cur = exchange(cur, 1 << j)
            if cur:
                ch(v.tensor_copy(key[0][:, :], key[1][:, :]))
            v.tensor_copy(eid[:, :], pay[cur][:, :]).then_inc(sorted_, 1)

        def current_at_turns():
            cur, out = 0, []
            for k in merges:
                if k > inner:
                    out.append(cur)
                    cur = (cur + k - inner) % 2
                    out.append(cur)
                cur = (cur + min(k, inner)) % 2
            return out

        @block.tensor
        def _(pe):
            for n, cur in enumerate(current_at_turns()):
                pe.wait_ge(s_tq, n + 1)
                for tile_, bank in ((key[cur], bk), (pay[cur], bp)):
                    for b in range(SF // P):
                        last = nc.tensor.transpose(bank[:, b * P:(b + 1) * P], tile_[:, b * P:(b + 1) * P], C["ident"][:, :])
                last.then_inc(s_tp, 1)

        @block.scalar
        def _(act):
            act.wait_ge(s_cl, 1)
            act.dma_start(srcs[0:full, :], a["src"][0:full * SF].rearrange("(p f) -> p f", f=SF)).then_inc(s_ld, 16)
            act.dma_start(srcs[full:full + 1, 0:E - full * SF], a["src"][full * SF:E].unsqueeze(0)).then_inc(s_ld, 16)
            for n, cur in enumerate(current_at_turns()):
                act.wait_ge(s_tp, n + 1)
                nc.scalar.activation(key[cur][:, :], bk[:, :], ACT.Copy)
                nc.scalar.activation(pay[cur][:, :], bp[:, :], ACT.Copy).then_inc(s_tr, 1)



LN_OPS = 15
RSQRT_SEED = float(0x5F3759DF)


def row_moments(nc, x, bn):
    for g in range(x.shape[1]):
        last = nc.vector.bn_stats(bn[:, g, :], x[:, g, :])
    return last


def norm_factors(nc, ch, bn, sm, ready):
    v = nc.vector
    me, ve, mo, vo = (bn[:, :, i] for i in (1, 2, 4, 5))
    mean2, t1, t2, var, y = (sm[:, i, :] for i in range(5))
    v.tensor_tensor(mean2, me, mo, ALU.add)
    v.tensor_tensor(t2, ve, vo, ALU.add)
    ch(v.tensor_tensor(t1, me, mo, ALU.subtract))
    ch(v.tensor_tensor(var, t1, t1, ALU.mult))
    ch(v.scalar_tensor_tensor(t1, var, 16.0, t2, ALU.mult, ALU.add))
    ch(v.tensor_scalar(var, t1, 1.0 / D, EPS, ALU.mult, ALU.add))
    ch(v.tensor_scalar(t1.bitcast(I32), var.bitcast(I32), 1, None, ALU.logical_shift_right))
    ch(v.tensor_scalar(y.bitcast(I32), t1.bitcast(I32), -1.0, RSQRT_SEED, ALU.mult, ALU.add))
    for _ in range(3):
        ch(v.tensor_tensor(t1, y, y, ALU.mult))
        ch(v.scalar_tensor_tensor(t2, t1, -0.5, var, ALU.mult, ALU.mult))
        ch(v.scalar_tensor_tensor(y, t2, 1.5, y, ALU.add, ALU.mult))
    v.scalar_tensor_tensor(sm[:, 5, :], mean2, -0.5, y, ALU.mult, ALU.mult).then_inc(ready, 1)



def gat_block(nc, a, T, C, tag, H, R, wide):
    with ExitStack() as ctx:
        m = Mem(nc, ctx, tag)
        two = range(U)
        ix = [m.sb(f"ix{k}", [P, 2, J], I32) for k in two]
        W = P if wide else D
        xg = [m.sb(f"xg{k}", [P, J, 2, W]) for k in two]
        start = [m.sb(f"start{k}", [H, CH]) for k in two]
        NE = 18 if tag == "g" else 1
        ext = [m.sb(f"ext{k}", [NE, CH]) for k in two]
        hT = [m.sb(f"hT{k}", [P, CH]) for k in two]
        hT2 = [m.sb(f"hT2{k}", [P, CH]) for k in two] if wide else None
        zt = [m.sb(f"zt{k}", [R, CH]) for k in two]
        xl = [m.sb(f"xl{k}", [R, CH]) for k in two]
        r = [m.sb(f"r{k}", [H, CH + 1]) for k in two]
        ed = [m.sb(f"ed{k}", [H, 2, CH]) for k in two]
        ex = [m.sb(f"ex{k}", [H, 2, CH]) for k in two]
        rp = [m.sb(f"rp{k}", [H, CH]) for k in two]
        den = [m.sb(f"den{k}", [H, CH]) for k in two]
        rec = [m.sb(f"rec{k}", [H, CH]) for k in two]
        msg = [m.sb(f"msg{k}", [R, CH]) for k in two]
        num = [m.sb(f"num{k}", [R, CH]) for k in two]
        res = [m.sb(f"res{k}", [R, CH]) for k in two]
        rT = [m.sb(f"rT{k}", [R, CH]) for k in two]
        oE = [m.sb(f"oE{k}", [P, J, R]) for k in two]
        if not wide:
            bn = m.sb("bn", [P, U * J * 2, 6])
            sm = m.sb("sm", [P, 6, U * J * 2])
            hn = [m.sb(f"hn{k}", [P, J, 2, D]) for k in two]
        if tag == "g":
            xb = [m.sb(f"xb{k}", [P, J, 2, D]) for k in two]
        bank = [[m.ps(f"bank{k}_{b}", [P, CH]) for b in range(4)] for k in two]
        s_ix, s_g, s_ld, s_st = m.sems("ix"), m.sems("g"), m.sems("ld"), m.sems("st")
        s_xst = m.sems("xst")
        names = "ln hn hT h z zs zt xl s ed ex rec b b2 res rT o oE turn pturn chain_dve clear"
        S = {n: m.sem(n) for n in names.split()}
        block = ctx.enter_context(nc.Block())
        cnt = lambda it, k: it * U + k + 1

        if tag == "a":
            idx_names, table = ("SRC", "DST"), a["x"]
        elif tag == "b":
            idx_names, table = ("PSRC", "PDST"), T["H1"]
        else:
            idx_names, table = ("PSRC", "PDST"), T["D3"]
        NG = 16 * J * 2
        NXST = 16 if tag == "a" else 32
        NLD = 16 * {"a": 2, "b": 2, "g": 3}[tag]

        @block.sync
        def _(sp):
            def body(it, first):
                for k in two:
                    if not first:
                        sp.wait_ge(s_g[k], NG * it)
                    for q, name in enumerate(idx_names):
                        sp.dma_start(ix[k][:, q, :], words(T[name], it, k)).then_inc(s_ix[k], 16)
                    if not first:
                        sp.wait_ge(S["res"], cnt(it - 1, k))
                    if tag == "g":
                        sp.dma_start(xb[k][:, :, :, :], rows(T["XSD"], it, k).rearrange("p j (s d) -> p j s d", s=2)
                                     ).then_inc(s_ld[k], 16)
                    sp.dma_start(start[k][:, :], line(T["START"], it, k, H)).then_inc(s_ld[k], 16)
                    if tag == "g":
                        sp.dma_start(ext[k][:, :], cols(T["EA"], it, k)).then_inc(s_ld[k], 16)
                    else:
                        sp.dma_start(ext[k][:, :], line(T["EW"], it, k, 1)).then_inc(s_ld[k], 16)
            steps(sp, body)

        @block.gpsimd
        def _(pool):
            def body(it, first):
                for k in two:
                    hold(pool, S["turn"], (s_ix[k], 32 * (it + 1)))
                    if not first and wide:
                        hold(pool, S["turn"], (S["hT"], 2 * cnt(it - 1, k)))
                    elif not first:
                        hold(pool, S["turn"], (S["hn"], cnt(it - 1, k)),
                             (s_xst[k], NXST * it))
                    for q in range(2):
                        for j in range(J):
                            nc.gpsimd.indirect_dma_start(
                                xg[k][:, j, q, :], None, table,
                                bass.IndirectOffsetOnAxis(ap=ix[k][:, q, j:j + 1], axis=0)).then_inc(s_g[k], 16)
            steps(pool, body)

        @block.vector
        def _(dve):
            v = nc.vector
            nchain = U * ((1 if tag == "g" else 0) + 3 + 1 + 2) + (0 if wide else 1 + LN_OPS)
            ch = Chain(dve, S["chain_dve"], nchain)
            for k in two:
                v.memset(r[k][:, :], -BIG)
                v.memset(den[k][:, :], 0.0)
                last = v.memset(num[k][:, :], 0.0)
            last.then_inc(S["clear"], 1)
            dve.wait_ge(S["clear"], 1)

            def body(it, first):
                ch.at(it)
                for k in two:
                    if wide:
                        continue
                    dve.wait_ge(s_g[k], NG * (it + 1))
                    x = xg[k]
                    if tag == "g":
                        dve.wait_ge(s_ld[k], NLD * (it + 1))
                        ch(v.tensor_tensor(xg[k][:, :, :, :], xg[k][:, :, :, :], xb[k][:, :, :, :], ALU.add))
                    last = row_moments(nc, x[:, :, :, :].rearrange("p j s d -> p (j s) d"), bn[:, k * 2 * J:(k + 1) * 2 * J, :])
                if not wide:
                    ch(last)
                    if not first:
                        dve.wait_ge(S["hn"], cnt(it - 1, U - 1))
                    norm_factors(nc, ch, bn, sm, S["ln"])
                for k in two:
                    dve.wait_ge(S["zs"], cnt(it, k))
                    v.tensor_tensor(zt[k][:, :], zt[k][:, :], bank[k][1][0:R, :], ALU.max).then_inc(S["zt"], 1)
                for k in two:
                    dve.wait_ge(S["s"], cnt(it, k))
                    dve.wait_ge(s_ld[k], NLD * (it + 1))
                    before = r[(k - 1) % U]
                    sc = bank[k][3][0:H, :]
                    ch(v.tensor_copy(r[k][:, 0:1], before[:, CH:CH + 1]))
                    ch(v.tensor_tensor_scan(r[k][:, 1:CH + 1], start[k][:, :], sc, r[k][:, 0:1], ALU.add, ALU.max))
                    v.tensor_tensor(ed[k][:, 1, :], sc, r[k][:, 1:CH + 1], ALU.subtract)
                    ch(v.tensor_tensor(rp[k][:, :], r[k][:, 0:CH], start[k][:, :], ALU.add))
                    v.tensor_tensor(ed[k][:, 0, :], rp[k][:, :], r[k][:, 1:CH + 1], ALU.subtract).then_inc(S["ed"], 1)
                for k in two:
                    dve.wait_ge(S["ex"], cnt(it, k))
                    ch(v.tensor_tensor_scan(den[k][:, :], ex[k][:, 0, :], ex[k][:, 1, :], den[(k - 1) % U][:, CH - 1:CH],
                                            ALU.mult, ALU.add))
                    v.reciprocal(rec[k][:, :], den[k][:, :]).then_inc(S["rec"], 1)
                for k in two:
                    dve.wait_ge(S["xl"], cnt(it, k))
                    dve.wait_ge(S["b"], cnt(it, k))
                    ch(v.tensor_tensor(msg[k][:, :], bank[k][2][0:R, :], xl[k][:, :], ALU.mult))
                    ch(v.tensor_tensor_scan(num[k][:, :], bank[k][1][0:R, :], msg[k][:, :], num[(k - 1) % U][:, CH - 1:CH],
                                            ALU.mult, ALU.add))
                    dve.wait_ge(S["b2"], cnt(it, k))
                    v.tensor_tensor(res[k][:, :], num[k][:, :], bank[k][3][0:R, :], ALU.mult).then_inc(S["res"], 1)
                ch.done()
            steps(dve, body)

        @block.scalar
        def _(act):
            n = nc.scalar

            def body(it, first):
                for k in two:
                    if wide:
                        continue
                    act.wait_ge(S["ln"], it + 1)
                    if tag == "a":
                        act.dma_start(rows(T["XSD"], it, k).rearrange("p j (s d) -> p j s d", s=2), xg[k][:, :, :, :]
                                      ).then_inc(s_xst[k], 16)
                    if not first:
                        act.wait_ge(S["hT"], cnt(it - 1, k))
                        if tag == "g":
                            act.wait_ge(s_xst[k], NXST * it)
                    for g in range(2 * J):
                        last = n.activation(hn[k][:, g // 2, g % 2, :], xg[k][:, g // 2, g % 2, :], ACT.Relu,
                                            bias=sm[:, 5, k * 2 * J + g:k * 2 * J + g + 1],
                                            scale=sm[:, 4, k * 2 * J + g:k * 2 * J + g + 1])
                    last.then_inc(S["hn"], 1)
                    if tag == "g":
                        act.wait_ge(S["hn"], cnt(it, k))
                        act.dma_start(rows(T["X3"], it, k), xg[k][:, :, 1, :]).then_inc(s_xst[k], 16)
                        act.dma_start(rows(T["HN3"], it, k), hn[k][:, :, 1, :]).then_inc(s_xst[k], 16)
                for k in two:
                    if wide:
                        act.wait_ge(S["hT"], 2 * cnt(it, k) - 1)
                        n.activation(hT[k][:, :], bank[k][0][:, :], ACT.Copy)
                        act.wait_ge(S["hT"], 2 * cnt(it, k))
                        n.activation(hT2[k][:, :], bank[k][1][:, :], ACT.Copy).then_inc(S["h"], 1)
                    else:
                        act.wait_ge(S["hT"], cnt(it, k))
                        n.activation(hT[k][:, :], bank[k][0][:, :], ACT.Copy).then_inc(S["h"], 1)
                for k in two:
                    act.wait_ge(S["z"], cnt(it, k))
                    n.activation(zt[k][:, :], bank[k][1][0:R, :], ACT.Copy, scale=SLOPE).then_inc(S["zs"], 1)
                    if tag == "g":
                        n.activation(xl[k][:, :], bank[k][2][0:R, :], ACT.Identity, bias=C["bl3"][:, 0:1]).then_inc(S["xl"], 1)
                    else:
                        n.activation(xl[k][:, :], bank[k][2][0:R, :], ACT.Copy).then_inc(S["xl"], 1)
                for k in two:
                    act.wait_ge(S["ed"], cnt(it, k))
                    n.activation(ex[k][:, :, :], ed[k][:, :, :], ACT.Exp).then_inc(S["ex"], 1)
                for k in two:
                    act.wait_ge(S["res"], cnt(it, k))
                    if tag == "a":
                        n.activation(rT[k][:, :], res[k][:, :], ACT.Relu, bias=C["b1"][:, 0:1]).then_inc(S["rT"], 1)
                    elif tag == "g":
                        n.activation(rT[k][:, :], res[k][:, :], ACT.Copy).then_inc(S["rT"], 1)
                    act.wait_ge(S["o"], cnt(it, k))
                    if not first:
                        act.wait_ge(s_st[k], 16 * it)
                    if tag == "b":
                        n.activation(rT[k][0:D, :], bank[k][0][0:D, :], ACT.Relu, bias=C["b2"][:, 0:1]).then_inc(S["oE"], 1)
                        act.wait_ge(S["oE"], cnt(it, k))
                        act.dma_start(cols(T["H2T"], it, k), rT[k][0:D, :]).then_inc(s_st[k], 16)
                        continue
                    psO = bank[k][0][:, 0:J * R].rearrange("p (j d) -> p j d", j=J)
                    n.activation(oE[k][:, :, :], psO, ACT.Copy).then_inc(S["oE"], 1)
                    act.wait_ge(S["oE"], cnt(it, k))
                    act.dma_start(rows(T["H1" if tag == "a" else "AG"], it, k), oE[k][:, :, :]).then_inc(s_st[k], 16)
            steps(act, body)
            for k in two:
                act.wait_ge(s_st[k], 16 * NIT)
                if tag != "b":
                    act.wait_ge(s_xst[k], NXST * NIT)
            if tag == "a":
                n.activation(C["brow"][:, :], C["b1row"][:, :], ACT.Relu).then_inc(S["rT"], 1)
                act.wait_ge(S["rT"], NCH + 1)
                act.dma_start(T["H1"][SENT:SENT + 1, :], C["brow"][:, :]).then_inc(s_st[0], 16)
                act.wait_ge(s_st[0], 16 * NIT + 16)
            if tag == "b":
                n.activation(C["bcol"][:, :], C["b2"][:, 0:1].to_broadcast([D, EP - E]), ACT.Relu).then_inc(S["rT"], 1)
                act.wait_ge(S["rT"], 1)
                act.dma_start(T["H2T"][:, E:EP], C["bcol"][:, :]).then_inc(s_st[0], 16)
                act.wait_ge(s_st[0], 16 * NIT + 16)

        @block.tensor
        def _(pe):
            mm = nc.tensor.matmul
            tr = nc.tensor.transpose
            wz, we, att, sel = ((C["wz1"], C["we1"], C["att1b"], C["sel8"]) if tag == "a" else
                                (None, C["we2"], C["att2b"], C["sel2"]) if tag == "b" else
                                (C["wz3"], C["we3"], C["att3b"], C["sel4"]))
            split = lambda t: t.rearrange("r (p j) -> r p j", j=J)

            def body(it, first):
                for k in two:
                    if wide:
                        pe.wait_ge(s_g[k], NG * (it + 1))
                    else:
                        pe.wait_ge(S["hn"], cnt(it, k))
                    if not first:
                        pe.wait_ge(S["oE"], cnt(it - 1, k))
                        pe.wait_ge(S["res"], cnt(it - 1, k))
                    for q in range(2 if wide else 1):
                        for j in range(J):
                            src = xg[k][:, j, q, :] if wide else hn[k][:, j, :, :].rearrange("p s d -> p (s d)")
                            last = tr(split(bank[k][q][:, :])[:, :, j], src, C["ident"][:, :])
                        last.then_inc(S["hT"], 1)
                for k in two:
                    pe.wait_ge(S["h"], cnt(it, k))
                    pe.wait_ge(s_ld[k], NLD * (it + 1))
                    if wide:
                        mm(bank[k][1][0:R, :], C["wl2"][:, :], hT[k][:, :], start=True, stop=False)
                        mm(bank[k][1][0:R, :], C["wr2"][:, :], hT2[k][:, :], start=False, stop=False)
                    else:
                        mm(bank[k][1][0:R, :], wz[:, :], hT[k][:, :], start=True, stop=False)
                    mm(bank[k][1][0:R, :], we[:, :], ext[k][:, :], start=False, stop=True)
                    if wide:
                        last = mm(bank[k][2][0:R, :], C["wl2"][:, :], hT[k][:, :], start=True, stop=True)
                    else:
                        last = mm(bank[k][2][0:R, :], wz[0:D, :], hT[k][0:D, :], start=True, stop=True)
                    last.then_inc(S["z"], 1)
                for k in two:
                    hold(pe, S["pturn"], (S["zt"], cnt(it, k)))
                    mm(bank[k][3][0:H, :], att[:, :], zt[k][:, :], start=True, stop=True).then_inc(S["s"], 1)
                for k in two:
                    pe.wait_ge(S["ex"], cnt(it, k))
                    pe.wait_ge(S["xl"], cnt(it, k))
                    mm(bank[k][1][0:R, :], sel[:, :], ex[k][:, 0, :], start=True, stop=True)
                    mm(bank[k][2][0:R, :], sel[:, :], ex[k][:, 1, :], start=True, stop=True).then_inc(S["b"], 1)
                for k in two:
                    pe.wait_ge(S["rec"], cnt(it, k))
                    mm(bank[k][3][0:R, :], sel[:, :], rec[k][:, :], start=True, stop=True).then_inc(S["b2"], 1)
                for k in two:
                    if tag == "b":
                        pe.wait_ge(S["res"], cnt(it, k))
                        mm(bank[k][0][0:D, :], C["mean2"][:, :], res[k][:, :], start=True, stop=True).then_inc(S["o"], 1)
                        continue
                    hold(pe, S["pturn"], (S["rT"], cnt(it, k)))
                    for j in range(J):
                        last = tr(bank[k][0][:, j * R:(j + 1) * R], split(rT[k][:, :])[:, :, j], C["ident"][0:R, 0:R])
                    last.then_inc(S["o"], 1)
            steps(pe, body)



def weights_block(nc, T, C):
    with ExitStack() as ctx:
        m = Mem(nc, ctx, "we")
        ab = m.sb("ab", [D, 2, P])
        pi = m.sb("pi", [P, 1], I32)
        p5 = m.sb("p5", [P, 1], I32)
        s_ab, s_iota, s_p5, s_pe, s_end = (m.sem(x) for x in "ab iota p5 pe end".split())
        pw = m.ps("pw", [P, P])
        pt = m.ps("pt", [D, D])
        pf = m.ps("pf", [D, 4, P])
        block = ctx.enter_context(nc.Block())

        @block.gpsimd
        def _(pool):
            nc.gpsimd.iota(pi[:, :], [[1, 1]], base=0, channel_multiplier=1).then_inc(s_iota, 1)

        @block.vector
        def _(dve):
            v = nc.vector
            for q in range(2):
                last = v.tensor_copy(ab[:, q, :], C["a1"][:, q:q + 1].to_broadcast([D, P]))
            last.then_inc(s_ab, 1)
            dve.wait_ge(s_iota, 1)
            v.tensor_scalar(p5[:, :], pi[:, :], 5, None, ALU.logical_shift_right).then_inc(s_p5, 1)
            dve.wait_ge(s_p5, 1)
            for q in range(4):
                v.tensor_scalar(C["relp"][:, q:q + 1], p5[:, :], float(4 * q), None, ALU.add)
            dve.wait_ge(s_pe, 1)
            v.tensor_copy(C["wb"][:, :], pw[:, :])
            v.tensor_copy(C["w1t"][:, :], pt[:, :])
            v.tensor_copy(C["wft"][:, :, :], pf[:, :, :]).then_inc(s_end, 1)

        @block.tensor
        def _(pe):
            pe.wait_ge(s_ab, 1)
            for q in range(2):
                nc.tensor.matmul(pw[:, q * D:(q + 1) * D], ab[:, q, :], C["w1"][:, :], start=True, stop=True)
            nc.tensor.transpose(pt[:, :], C["w1"][:, :], C["ident"][0:D, 0:D])
            for q in range(4):
                last = nc.tensor.transpose(pf[:, q, :], C["wflat"][:, q, :], C["ident"][:, :])
            last.then_inc(s_pe, 1)



def mlp_block(nc, T, C):
    with ExitStack() as ctx:
        m = Mem(nc, ctx, "m")
        two = range(U)
        h = [m.sb(f"h{k}", [D + 1, CH]) for k in two]
        g1T = [m.sb(f"g1T{k}", [D + 1, CH]) for k in two]
        bn = [m.sb(f"bn{l}", [P, U * J, 6]) for l in range(2)]
        sm = [m.sb(f"sm{l}", [P, 6, U * J]) for l in range(2)]
        xn = [[m.sb(f"xn{l}{k}", [P, J, D]) for k in two] for l in range(2)]
        xs = [[m.sb(f"xs{l}{k}", [P, J, D]) for k in two] for l in range(2)]
        g = [[m.sb(f"g{l}{k}", [P, J, D]) for k in two] for l in range(2)]
        d1 = [m.sb(f"d1{k}", [P, J, D]) for k in two]
        pa = [[m.ps(f"pa{l}{k}", [P, J, D]) for k in two] for l in range(2)]
        pt = [m.ps(f"pt{k}", [D, CH]) for k in two]
        s_h, s_st = m.sems("h"), m.sems("st")
        s_mm, s_f, s_xn, s_sc, s_g = ([m.sem(f"{x}{l}") for l in range(2)] for x in "mm f xn sc g".split())
        s_t, s_gT, s_d1, s_ch, s_one, s_pturn = (m.sem(x) for x in "t gT d1 ch one pturn".split())
        block = ctx.enter_context(nc.Block())
        cnt = lambda it, k: it * U + k + 1
        gain = (("lng", "lnb"), ("lrg", "lrb"))

        @block.sync
        def _(sp):
            def body(it, first):
                for k in two:
                    if not first:
                        sp.wait_ge(s_mm[0], cnt(it - 1, k))
                    sp.dma_start(h[k][0:D, :], cols(T["H2T"], it, k)).then_inc(s_h[k], 16)
            steps(sp, body)

        @block.tensor
        def _(pe):
            pe.wait_ge(s_one, 1)

            def body(it, first):
                for k in two:
                    pe.wait_ge(s_h[k], 16 * (it + 1))
                    if not first:
                        pe.wait_ge(s_xn[0], cnt(it - 1, k))
                    for j in range(J):
                        last = nc.tensor.matmul(pa[0][k][:, j, :], h[k][:, :].rearrange("r (p j) -> r p j", j=J)[:, :, j],
                                                C["wca"][:, :], start=True, stop=True)
                    last.then_inc(s_mm[0], 1)
                for k in two:
                    hold(pe, s_pturn, (s_g[0], cnt(it, k)))
                    if not first:
                        hold(pe, s_pturn, (s_gT, cnt(it - 1, k)))
                    for j in range(J):
                        last = nc.tensor.transpose(pt[k][:, j * P:(j + 1) * P], g[0][k][:, j, :], C["ident"][:, :])
                    last.then_inc(s_t, 1)
                for k in two:
                    pe.wait_ge(s_gT, cnt(it, k))
                    if not first:
                        pe.wait_ge(s_xn[1], cnt(it - 1, k))
                    for j in range(J):
                        last = nc.tensor.matmul(pa[1][k][:, j, :], g1T[k][:, j * P:(j + 1) * P],
                                                C["wra"][:, :], start=True, stop=True)
                    last.then_inc(s_mm[1], 1)
            steps(pe, body)

        @block.vector
        def _(dve):
            v = nc.vector
            for k in two:
                v.memset(h[k][D:D + 1, :], 1.0)
                last = v.memset(g1T[k][D:D + 1, :], 1.0)
            last.then_inc(s_one, 1)
            ch = Chain(dve, s_ch, 2 * (1 + LN_OPS + U))

            def body(it, first):
                ch.at(it)
                for l in range(2):
                    for k in two:
                        dve.wait_ge(s_mm[l], cnt(it, k))
                        last = row_moments(nc, pa[l][k], bn[l][:, k * J:(k + 1) * J, :])
                    ch(last)
                    if not first:
                        dve.wait_ge(s_xn[l], cnt(it - 1, U - 1))
                    norm_factors(nc, ch, bn[l], sm[l], s_f[l])
                    gb, bb = (C[x][:, :].unsqueeze(1).to_broadcast([P, J, D]) for x in gain[l])
                    for k in two:
                        dve.wait_ge(s_xn[l], cnt(it, k))
                        ch(v.tensor_tensor(xs[l][k][:, :, :], xn[l][k][:, :, :], gb, ALU.mult))
                        v.tensor_tensor(xs[l][k][:, :, :], xs[l][k][:, :, :], bb, ALU.add).then_inc(s_sc[l], 1)
                for k in two:
                    dve.wait_ge(s_g[1], cnt(it, k))
                    if not first:
                        dve.wait_ge(s_st[k], 16 * it)
                    v.tensor_tensor(d1[k][:, :, :], g[0][k][:, :, :], g[1][k][:, :, :], ALU.add).then_inc(s_d1, 1)
                ch.done()
            steps(dve, body)

        @block.scalar
        def _(act):
            n = nc.scalar

            def body(it, first):
                for l in range(2):
                    act.wait_ge(s_f[l], it + 1)
                    for k in two:
                        for j in range(J):
                            c = k * J + j
                            last = n.activation(xn[l][k][:, j, :], pa[l][k][:, j, :], ACT.Identity,
                                                bias=sm[l][:, 5, c:c + 1], scale=sm[l][:, 4, c:c + 1])
                        last.then_inc(s_xn[l], 1)
                    for k in two:
                        act.wait_ge(s_sc[l], cnt(it, k))
                        if not first and l == 0:
                            act.wait_ge(s_d1, cnt(it - 1, k))
                        n.activation(g[l][k][:, :, :], xs[l][k][:, :, :], ACT.Gelu).then_inc(s_g[l], 1)
                    if l == 0:
                        for k in two:
                            act.wait_ge(s_t, cnt(it, k))
                            n.activation(g1T[k][0:D, :], pt[k][:, :], ACT.Copy).then_inc(s_gT, 1)
                for k in two:
                    act.wait_ge(s_d1, cnt(it, k))
                    act.dma_start(rows(T["D1"], it, k), d1[k][:, :, :]).then_inc(s_st[k], 16)
            steps(act, body)
            for k in two:
                act.wait_ge(s_st[k], 16 * NIT)



def logit_block(nc, T, C):
    with ExitStack() as ctx:
        m = Mem(nc, ctx, "l")
        two = range(U)
        ix = [m.sb(f"ix{k}", [P, 2, J], I32) for k in two]
        dg = [m.sb(f"dg{k}", [P, J, 2, D]) for k in two]
        xb = [m.sb(f"xb{k}", [P, J, 2, D]) for k in two]
        xs = [m.sb(f"xs{k}", [P, J, 2, D]) for k in two]
        hn = [m.sb(f"hn{k}", [P, J, 2 * D]) for k in two]
        pr = [m.sb(f"pr{k}", [P, J, 2 * D]) for k in two]
        raw = [m.sb(f"raw{k}", [P, J]) for k in two]
        e = [m.sb(f"e{k}", [P, J]) for k in two]
        bn = m.sb("bn", [P, U * J * 2, 6])
        sm = m.sb("sm", [P, 6, U * J * 2])
        s_ix, s_g, s_ld, s_dd, s_hs, s_es = (m.sems(x) for x in "ix g ld dd hs es".split())
        s_xs, s_f, s_hn, s_e, s_ch, s_turn = (m.sem(x) for x in "xs f hn e ch turn".split())
        block = ctx.enter_context(nc.Block())
        cnt = lambda it, k: it * U + k + 1
        NG = 16 * 2 * J

        @block.sync
        def _(sp):
            def body(it, first):
                for k in two:
                    if not first:
                        sp.wait_ge(s_g[k], NG * it)
                    sp.dma_start(ix[k][:, 0, :], words(T["PSRC"], it, k)).then_inc(s_ix[k], 16)
                    sp.dma_start(ix[k][:, 1, :], words(T["PDST"], it, k)).then_inc(s_ix[k], 16)
                    if not first:
                        sp.wait_ge(s_xs, cnt(it - 1, k))
                    sp.dma_start(xb[k][:, :, :, :], rows(T["XSD"], it, k).rearrange("p j (s d) -> p j s d", s=2)
                                 ).then_inc(s_ld[k], 16)
            steps(sp, body)

        @block.gpsimd
        def _(pool):
            def body(it, first):
                for k in two:
                    hold(pool, s_turn, (s_ix[k], 32 * (it + 1)))
                    if not first:
                        hold(pool, s_turn, (s_xs, cnt(it - 1, k)), (s_dd[k], 16 * it))
                    for q in range(2):
                        for j in range(J):
                            nc.gpsimd.indirect_dma_start(
                                dg[k][:, j, q, :], None, T["D1"],
                                bass.IndirectOffsetOnAxis(ap=ix[k][:, q, j:j + 1], axis=0)).then_inc(s_g[k], 16)
            steps(pool, body)

        @block.vector
        def _(dve):
            v = nc.vector
            ch = Chain(dve, s_ch, U + LN_OPS + 2 * U)
            wb = C["wb"][:, :].unsqueeze(1).to_broadcast([P, J, 2 * D])

            def body(it, first):
                ch.at(it)
                for k in two:
                    dve.wait_ge(s_g[k], NG * (it + 1))
                    dve.wait_ge(s_ld[k], 16 * (it + 1))
                    if not first:
                        dve.wait_ge(s_hn, cnt(it - 1, k))
                    v.tensor_tensor(xs[k][:, :, :, :], dg[k][:, :, :, :], xb[k][:, :, :, :], ALU.add).then_inc(s_xs, 1)
                    dve.wait_ge(s_xs, cnt(it, k))
                    last = row_moments(nc, xs[k][:, :, :, :].rearrange("p j s d -> p (j s) d"),
                                       bn[:, k * 2 * J:(k + 1) * 2 * J, :])
                    ch(last)
                if not first:
                    dve.wait_ge(s_hn, cnt(it - 1, U - 1))
                norm_factors(nc, ch, bn, sm, s_f)
                for k in two:
                    dve.wait_ge(s_hn, cnt(it, k))
                    ch(v.tensor_tensor(pr[k][:, :, :], hn[k][:, :, :], wb, ALU.mult))
                    ch(v.tensor_reduce(raw[k][:, :], pr[k][:, :, :], X, ALU.add))
                    if not first:
                        dve.wait_ge(s_es[k], 16 * it)
                    v.scalar_tensor_tensor(e[k][:, :], raw[k][:, :], SLOPE, raw[k][:, :], ALU.mult, ALU.max
                                           ).then_inc(s_e, 1)
                ch.done()
            steps(dve, body)

        @block.scalar
        def _(act):
            n = nc.scalar

            def body(it, first):
                for k in two:
                    act.wait_ge(s_g[k], NG * (it + 1))
                    act.dma_start(rows(T["D1D"], it, k), dg[k][:, :, 1, :]).then_inc(s_dd[k], 16)
                act.wait_ge(s_f, it + 1)
                for k in two:
                    if not first:
                        act.wait_ge(s_hs[k], 16 * it)
                        act.wait_ge(s_e, cnt(it - 1, k))
                    for g in range(2 * J):
                        c = k * 2 * J + g
                        last = n.activation(hn[k][:, g // 2, (g % 2) * D:(g % 2 + 1) * D], xs[k][:, g // 2, g % 2, :],
                                            ACT.Relu, bias=sm[:, 5, c:c + 1], scale=sm[:, 4, c:c + 1])
                    last.then_inc(s_hn, 1)
                    act.wait_ge(s_hn, cnt(it, k))
                    act.dma_start(rows(T["HS"], it, k), hn[k][:, :, 0:D]).then_inc(s_hs[k], 16)
                for k in two:
                    act.wait_ge(s_e, cnt(it, k))
                    act.dma_start(words(T["EL"], it, k), e[k][:, :]).then_inc(s_es[k], 16)
            steps(act, body)
            for k in two:
                for s in (s_dd, s_hs, s_es):
                    act.wait_ge(s[k], 16 * NIT)


def permute_block(nc, T, tag, gather):
    with ExitStack() as ctx:
        m = Mem(nc, ctx, tag)
        two = range(U)
        ix = [m.sb(f"ix{k}", [P, J], I32) for k in two]
        val = [m.sb(f"val{k}", [P, J]) for k in two]
        s_ix, s_g, s_st = (m.sems(x) for x in "ix g st".split())
        s_turn = m.sem("turn")
        block = ctx.enter_context(nc.Block())
        el, al = T["EL"].unsqueeze(1), T["AL"].unsqueeze(1)

        @block.sync
        def _(sp):
            def body(it, first):
                for k in two:
                    if not first:
                        sp.wait_ge(s_g[k], 16 * J * it)
                        if gather:
                            sp.dma_start(words(T["SE"], it - 1, k), val[k][:, :]).then_inc(s_st[k], 16)
                    sp.dma_start(ix[k][:, :], words(T["EID"], it, k)).then_inc(s_ix[k], 16)
                    if not gather:
                        sp.dma_start(val[k][:, :], words(T["SA"], it, k)).then_inc(s_ix[k], 16)
            steps(sp, body)
            if gather:
                for k in two:
                    sp.wait_ge(s_g[k], 16 * J * NIT)
                    sp.dma_start(words(T["SE"], NIT - 1, k), val[k][:, :]).then_inc(s_st[k], 16)
                    sp.wait_ge(s_st[k], 16 * NIT)

        @block.gpsimd
        def _(pool):
            def body(it, first):
                for k in two:
                    hold(pool, s_turn, (s_ix[k], (16 if gather else 32) * (it + 1)))
                    if gather and not first:
                        hold(pool, s_turn, (s_st[k], 16 * it))
                    for j in range(J):
                        at = bass.IndirectOffsetOnAxis(ap=ix[k][:, j:j + 1], axis=0)
                        if gather:
                            nc.gpsimd.indirect_dma_start(val[k][:, j:j + 1], None, el, at).then_inc(s_g[k], 16)
                        else:
                            nc.gpsimd.indirect_dma_start(al, at, val[k][:, j:j + 1], None).then_inc(s_g[k], 16)
            steps(pool, body)
            for k in two:
                pool.wait_ge(s_g[k], 16 * J * NIT)


def softmax_block(nc, T, C):
    with ExitStack() as ctx:
        m = Mem(nc, ctx, "sx")
        full = lambda t: t.rearrange("(p f) -> p f", f=EF)
        names = "se kp kc kn first last nfirst nlast r mx ex den a b al et relf"
        B = {x: m.sb(x, [P, EF]) for x in names.split()}
        ints = {x: m.sb(x, [P, EF], I32) for x in ("nts", "ntd")}
        col = m.sb("col", [P, 2])
        row = m.sb("row", [1, 2, P])
        carry = m.sb("carry", [1, P + 2])
        cin = m.sb("cin", [P, 1])
        prow = m.ps("prow", [1, 2, P])
        pcol = m.ps("pcol", [P, 1])
        s_ld, s_rel, s_st, s_ch, s_pe, s_up, s_ex, s_exd = (m.sem(x) for x in "ld rel st ch pe up ex exd".split())
        block = ctx.enter_context(nc.Block())

        @block.sync
        def _(sp):
            for t, src in ((B["se"], T["SE"]), (B["kp"], T["SSRC"][0:EP]), (B["kc"], T["SSRC"][1:EP + 1]),
                           (B["kn"], T["SSRC"][2:EP + 2])):
                sp.dma_start(t[:, :], full(src)).then_inc(s_ld, 16)
            for t, src in ((ints["nts"], T["NTS"]), (ints["ntd"], T["NTD"]), (B["et"], T["ET"])):
                sp.dma_start(t[:, :], full(src)).then_inc(s_rel, 16)
            sp.wait_ge(s_st, 1)
            sp.dma_start(full(T["REL"]), B["relf"][:, :]).then_inc(s_ld, 16)
            sp.wait_ge(s_st, 2)
            sp.dma_start(full(T["SA"]), B["al"][:, :]).then_inc(s_ld, 16)
            sp.wait_ge(s_ld, 16 * 6)

        @block.tensor
        def _(pe):
            for n in range(4):
                pe.wait_ge(s_up, 2 * n + 1)
                for q in range(2):
                    last = nc.tensor.transpose(prow[:, q, :], col[:, q:q + 1], C["ident"][:, :])
                last.then_inc(s_pe, 1)
                pe.wait_ge(s_up, 2 * n + 2)
                lo = 0 if n % 2 == 0 else 2
                nc.tensor.transpose(pcol[:, :], carry[:, lo:lo + P], C["ident"][0:1, 0:1]).then_inc(s_pe, 1)

        @block.scalar
        def _(act):
            act.wait_ge(s_ex, 1)
            nc.scalar.activation(B["ex"][:, :], B["b"][:, :], ACT.Exp).then_inc(s_exd, 1)

        @block.vector
        def _(dve):
            v = nc.vector
            ch = Chain(dve, s_ch, 0)
            ch.at(0)
            dve.wait_ge(s_rel, 48)
            ch(v.scalar_tensor_tensor(B["a"][:, :], ints["nts"][:, :], 8.0, B["et"][:, :], ALU.mult, ALU.add))
            v.scalar_tensor_tensor(B["relf"][:, :], ints["ntd"][:, :], 4.0, B["a"][:, :], ALU.mult, ALU.add).then_inc(s_st, 1)
            dve.wait_ge(s_ld, 64)
            v.tensor_tensor(B["nfirst"][:, :], B["kp"][:, :], B["kc"][:, :], ALU.is_equal)
            ch(v.tensor_tensor(B["nlast"][:, :], B["kn"][:, :], B["kc"][:, :], ALU.is_equal))
            v.tensor_scalar(B["first"][:, :], B["nfirst"][:, :], -1.0, BIG, ALU.add, ALU.mult)
            ch(v.tensor_scalar(B["last"][:, :], B["nlast"][:, :], -1.0, BIG, ALU.add, ALU.mult))
            passes = [0]

            def scan(out, d0, d1, op0, op1, empty, back):
                n = passes[0]
                passes[0] += 1
                rev = (lambda t: t[:, ::-1]) if back else (lambda t: t[:, :])
                edge = slice(0, 1) if back else slice(EF - 1, EF)
                ch(v.tensor_tensor_scan(rev(out), rev(d0), rev(d1), empty, op0, op1))
                v.tensor_copy(col[:, 0:1], out[:, edge])
                v.tensor_reduce(col[:, 1:2], d0[:, :], X, ALU.add if op0 == ALU.add else ALU.min).then_inc(s_up, 1)
                dve.wait_ge(s_pe, 2 * n + 1)
                v.memset(carry[:, :], empty)
                ch(v.tensor_copy(row[:, :, :], prow[:, :, :]))
                body, st, gate = carry[:, 1:P + 1], row[:, 0, :], row[:, 1, :]
                if back:
                    body, st, gate = body[:, ::-1], st[:, ::-1], gate[:, ::-1]
                v.tensor_tensor_scan(body, gate, st, empty, op0, op1).then_inc(s_up, 1)
                dve.wait_ge(s_pe, 2 * n + 2)
                ch(v.tensor_copy(cin[:, :], pcol[:, :]))
                ch(v.tensor_tensor_scan(rev(out), rev(d0), rev(d1), cin[:, 0:1], op0, op1))

            scan(B["r"], B["first"], B["se"], ALU.add, ALU.max, -BIG, False)
            scan(B["mx"], B["last"], B["r"], ALU.add, ALU.max, -BIG, True)
            v.tensor_tensor(B["b"][:, :], B["se"][:, :], B["mx"][:, :], ALU.subtract).then_inc(s_ex, 1)
            dve.wait_ge(s_exd, 1)
            scan(B["r"], B["nfirst"], B["ex"], ALU.mult, ALU.add, 0.0, False)
            ch(v.tensor_tensor(B["a"][:, :], B["r"][:, :], B["nlast"][:, :], ALU.mult))
            ch(v.tensor_tensor(B["a"][:, :], B["r"][:, :], B["a"][:, :], ALU.subtract))
            scan(B["den"], B["nlast"], B["a"], ALU.mult, ALU.add, 0.0, True)
            ch(v.tensor_scalar(B["den"][:, :], B["den"][:, :], 1.0, None, ALU.max))
            ch(v.reciprocal(B["b"][:, :], B["den"][:, :]))
            v.tensor_tensor(B["al"][:, :], B["ex"][:, :], B["b"][:, :], ALU.mult).then_inc(s_st, 1)



def mix_block(nc, T, C):
    with ExitStack() as ctx:
        m = Mem(nc, ctx, "e")
        two = range(U)
        hs = [m.sb(f"hs{k}", [P, J, D]) for k in two]
        al = [m.sb(f"al{k}", [P, J]) for k in two]
        kp = [m.sb(f"kp{k}", [D, CH]) for k in two]
        dd = [m.sb(f"dd{k}", [P, J, D]) for k in two]
        mg = [m.sb(f"mg{k}", [P, J, D]) for k in two]
        ag = [m.sb(f"ag{k}", [D, CH]) for k in two]
        ng = [m.sb(f"ng{k}", [P, J, D]) for k in two]
        ex = [m.sb(f"ex{k}", [P, J, D]) for k in two]
        t = [m.sb(f"t{k}", [P, J, D]) for k in two]
        o = [m.sb(f"o{k}", [P, J, D]) for k in two]
        pt = [m.ps(f"pt{k}", [D, CH]) for k in two]
        pw = [m.ps(f"pw{k}", [P, J, D]) for k in two]
        s_ld, s_st = m.sems("ld"), m.sems("st")
        s_mg, s_t, s_ag, s_w, s_ng, s_ex, s_o, s_ch, s_clear, s_pturn = (
            m.sem(x) for x in "mg t ag w ng ex o ch clear pturn".split())
        block = ctx.enter_context(nc.Block())
        cnt = lambda it, k: it * U + k + 1

        @block.sync
        def _(sp):
            def body(it, first):
                for k in two:
                    if not first:
                        sp.wait_ge(s_o, cnt(it - 1, k))
                    for dst, src in ((hs[k][:, :, :], rows(T["HS"], it, k)), (al[k][:, :], words(T["AL"], it, k)),
                                     (kp[k][:, :], line(T["KEEP"], it, k, D)), (dd[k][:, :, :], rows(T["D1D"], it, k))):
                        sp.dma_start(dst, src).then_inc(s_ld[k], 16)
            steps(sp, body)

        @block.vector
        def _(dve):
            v = nc.vector
            ch = Chain(dve, s_ch, U)
            for k in two:
                last = v.memset(ag[k][:, :], 0.0)
            last.then_inc(s_clear, 1)
            dve.wait_ge(s_clear, 1)

            def body(it, first):
                ch.at(it)
                for k in two:
                    dve.wait_ge(s_ld[k], 64 * (it + 1))
                    v.tensor_tensor(mg[k][:, :, :], hs[k][:, :, :], bcast(al[k][:, :], D), ALU.mult).then_inc(s_mg, 1)
                for k in two:
                    dve.wait_ge(s_t, cnt(it, k))
                    if k:
                        dve.wait_ge(s_ag, cnt(it, k - 1))
                    v.tensor_tensor_scan(ag[k][:, :], kp[k][:, :], pt[k][:, :], ag[(k - 1) % U][:, CH - 1:CH],
                                         ALU.mult, ALU.add).then_inc(s_ag, 1)
                for k in two:
                    dve.wait_ge(s_w, cnt(it, k))
                    v.tensor_scalar(ng[k][:, :, :], pw[k][:, :, :], 0.0, None, ALU.min).then_inc(s_ng, 1)
                for k in two:
                    dve.wait_ge(s_ex, cnt(it, k))
                    ch(v.scalar_tensor_tensor(t[k][:, :, :], pw[k][:, :, :], 0.0, ex[k][:, :, :], ALU.max, ALU.add))
                    if not first:
                        dve.wait_ge(s_st[k], 16 * it)
                    v.scalar_tensor_tensor(o[k][:, :, :], t[k][:, :, :], -1.0, dd[k][:, :, :], ALU.add, ALU.add
                                           ).then_inc(s_o, 1)
                ch.done()
            steps(dve, body)

        @block.tensor
        def _(pe):
            def body(it, first):
                for k in two:
                    hold(pe, s_pturn, (s_mg, cnt(it, k)))
                    for j in range(J):
                        last = nc.tensor.transpose(pt[k][:, :].rearrange("r (p j) -> r p j", j=J)[:, :, j],
                                                   mg[k][:, j, :], C["ident"][:, :])
                    last.then_inc(s_t, 1)
                for k in two:
                    pe.wait_ge(s_ag, cnt(it, k))
                    for j in range(J):
                        last = nc.tensor.matmul(pw[k][:, j, :], ag[k][:, :].rearrange("r (p j) -> r p j", j=J)[:, :, j],
                                                C["w1t"][:, :], start=True, stop=True)
                    last.then_inc(s_w, 1)
            steps(pe, body)

        @block.scalar
        def _(act):
            def body(it, first):
                for k in two:
                    act.wait_ge(s_ng, cnt(it, k))
                    nc.scalar.activation(ex[k][:, :, :], ng[k][:, :, :], ACT.Exp).then_inc(s_ex, 1)
                for k in two:
                    act.wait_ge(s_o, cnt(it, k))
                    act.dma_start(rows(T["D2"], it, k), o[k][:, :, :]).then_inc(s_st[k], 16)
            steps(act, body)
            for k in two:
                act.wait_ge(s_st[k], 16 * NIT)
            act.dma_start(T["D2"][SENT:SENT + 1, :], T["D1"][SENT:SENT + 1, :]).then_inc(s_st[0], 16)
            act.wait_ge(s_st[0], 16 * NIT + 16)


def relation_block(nc, T, C):
    with ExitStack() as ctx:
        m = Mem(nc, ctx, "f")
        two = range(U)
        ix = [m.sb(f"ix{k}", [P, J], I32) for k in two]
        dg = [m.sb(f"dg{k}", [P, J, D]) for k in two]
        xb = [m.sb(f"xb{k}", [P, J, D]) for k in two]
        xs = [m.sb(f"xs{k}", [P, J, D]) for k in two]
        hn = [m.sb(f"hn{k}", [P, J, D]) for k in two]
        hT = [m.sb(f"hT{k}", [D, CH]) for k in two]
        rl = [m.sb(f"rl{k}", [P, CH]) for k in two]
        kp = [m.sb(f"kp{k}", [D, CH]) for k in two]
        d2 = [m.sb(f"d2{k}", [P, J, D]) for k in two]
        d2b = [m.sb(f"d2b{k}", [P, J, D]) for k in two]
        sel = [[m.sb(f"sel{k}{q}", [P, CH]) for q in range(4)] for k in two]
        ag = [m.sb(f"ag{k}", [D, CH]) for k in two]
        o = [m.sb(f"o{k}", [P, J, D]) for k in two]
        srow = m.sb("srow", [1, D])
        bn = m.sb("bn", [P, U * J, 6])
        sm = m.sb("sm", [P, 6, U * J])
        bank = [[m.ps(f"bank{k}_{b}", [P, CH]) for b in range(4)] for k in two]
        s_ix, s_g, s_ld, s_st = (m.sems(x) for x in "ix g ld st".split())
        s_xs, s_f, s_hn, s_t, s_h, s_v, s_sel, s_m, s_ag, s_b, s_o, s_ch, s_turn, s_end, s_pturn = (
            m.sem(x) for x in "xs f hn t h v sel m ag b o ch turn end pturn".split())
        block = ctx.enter_context(nc.Block())
        cnt = lambda it, k: it * U + k + 1
        split = lambda t: t.rearrange("r (p j) -> r p j", j=J)

        @block.sync
        def _(sp):
            def body(it, first):
                for k in two:
                    if not first:
                        sp.wait_ge(s_g[k], 16 * J * it)
                    sp.dma_start(ix[k][:, :], words(T["PSRC"], it, k)).then_inc(s_ix[k], 16)
                    if not first:
                        sp.wait_ge(s_o, cnt(it - 1, k))
                    for dst, src in ((xb[k][:, :, :], rows(T["XSD"], it, k)[:, :, 0:D]),
                                     (rl[k][:, :], line(T["REL"], it, k, P)), (kp[k][:, :], line(T["KEEP"], it, k, D)),
                                     (d2[k][:, :, :], rows(T["D2"], it, k))):
                        sp.dma_start(dst, src).then_inc(s_ld[k], 16)
            steps(sp, body)

        @block.gpsimd
        def _(pool):
            def body(it, first):
                for k in two:
                    hold(pool, s_turn, (s_ix[k], 16 * (it + 1)))
                    if not first:
                        hold(pool, s_turn, (s_xs, cnt(it - 1, k)))
                    for j in range(J):
                        nc.gpsimd.indirect_dma_start(
                            dg[k][:, j, :], None, T["D2"],
                            bass.IndirectOffsetOnAxis(ap=ix[k][:, j:j + 1], axis=0)).then_inc(s_g[k], 16)
            steps(pool, body)

        @block.vector
        def _(dve):
            v = nc.vector
            for k in two:
                last = v.memset(ag[k][:, :], 0.0)
            last.then_inc(s_end, 1)
            dve.wait_ge(s_end, 1)
            ch = Chain(dve, s_ch, U + LN_OPS + U)
            b2 = C["bias2"][:, :].unsqueeze(1).to_broadcast([P, J, D])

            def body(it, first):
                ch.at(it)
                for k in two:
                    dve.wait_ge(s_g[k], 16 * J * (it + 1))
                    dve.wait_ge(s_ld[k], 64 * (it + 1))
                    if not first:
                        dve.wait_ge(s_hn, cnt(it - 1, U - 1))
                    v.tensor_tensor(xs[k][:, :, :], dg[k][:, :, :], xb[k][:, :, :], ALU.add).then_inc(s_xs, 1)
                    dve.wait_ge(s_xs, cnt(it, k))
                    ch(row_moments(nc, xs[k], bn[:, k * J:(k + 1) * J, :]))
                norm_factors(nc, ch, bn, sm, s_f)
                for q in range(4):
                    for k in two:
                        dve.wait_ge(s_v, it * 4 * U + q * U + k + 1)
                        v.scalar_tensor_tensor(sel[k][q][:, :], rl[k][:, :], C["relp"][:, q:q + 1],
                                               bank[k][1 + q % 2][:, :], ALU.is_equal, ALU.mult).then_inc(s_sel, 1)
                for k in two:
                    dve.wait_ge(s_m, cnt(it, k))
                    if k:
                        dve.wait_ge(s_ag, cnt(it, k - 1))
                    v.tensor_tensor_scan(ag[k][:, :], kp[k][:, :], bank[k][3][0:D, :], ag[(k - 1) % U][:, CH - 1:CH],
                                         ALU.mult, ALU.add).then_inc(s_ag, 1)
                for k in two:
                    ch(v.tensor_tensor(d2b[k][:, :, :], d2[k][:, :, :], b2, ALU.add))
                    dve.wait_ge(s_b, cnt(it, k))
                    if not first:
                        dve.wait_ge(s_st[k], 16 * it)
                    v.tensor_tensor(o[k][:, :, :], d2b[k][:, :, :],
                                    bank[k][0][:, 0:J * D].rearrange("p (j d) -> p j d", j=J), ALU.add).then_inc(s_o, 1)
                ch.done()
            steps(dve, body)

        @block.tensor
        def _(pe):
            def body(it, first):
                for k in two:
                    hold(pe, s_pturn, (s_hn, cnt(it, k)))
                    if not first:
                        hold(pe, s_pturn, (s_o, cnt(it - 1, k)))
                    for j in range(J):
                        last = nc.tensor.transpose(split(bank[k][0][0:D, :])[:, :, j], hn[k][:, j, :], C["ident"][:, :])
                    last.then_inc(s_t, 1)
                for q in range(4):
                    for k in two:
                        if q == 0:
                            pe.wait_ge(s_h, cnt(it, k))
                        if q >= 2:
                            pe.wait_ge(s_sel, it * 4 * U + (q - 2) * U + k + 1)
                        nc.tensor.matmul(bank[k][1 + q % 2][:, :], C["wft"][:, q, :], hT[k][:, :],
                                         start=True, stop=True).then_inc(s_v, 1)
                for k in two:
                    if not first:
                        pe.wait_ge(s_ag, cnt(it - 1, k))
                    for q in range(4):
                        pe.wait_ge(s_sel, it * 4 * U + q * U + k + 1)
                        last = nc.tensor.matmul(bank[k][3][0:D, :], C["cstk"][:, :], sel[k][q][:, :],
                                                start=(q == 0), stop=(q == 3))
                    last.then_inc(s_m, 1)
                for k in two:
                    hold(pe, s_pturn, (s_ag, cnt(it, k)))
                    for j in range(J):
                        last = nc.tensor.transpose(bank[k][0][:, j * D:(j + 1) * D], split(ag[k][:, :])[:, :, j],
                                                   C["ident"][0:D, 0:D])
                    last.then_inc(s_b, 1)
            steps(pe, body)

        @block.scalar
        def _(act):
            n = nc.scalar

            def body(it, first):
                act.wait_ge(s_f, it + 1)
                for k in two:
                    for j in range(J):
                        c = k * J + j
                        last = n.activation(hn[k][:, j, :], xs[k][:, j, :], ACT.Relu, bias=sm[:, 5, c:c + 1],
                                            scale=sm[:, 4, c:c + 1])
                    last.then_inc(s_hn, 1)
                for k in two:
                    act.wait_ge(s_t, cnt(it, k))
                    n.activation(hT[k][:, :], bank[k][0][0:D, :], ACT.Copy).then_inc(s_h, 1)
                for k in two:
                    act.wait_ge(s_o, cnt(it, k))
                    act.dma_start(rows(T["D3"], it, k), o[k][:, :, :]).then_inc(s_st[k], 16)
            steps(act, body)
            for k in two:
                act.wait_ge(s_st[k], 16 * NIT)
            act.dma_start(srow[:, :], T["D2"][SENT:SENT + 1, :]).then_inc(s_st[0], 16)
            act.wait_ge(s_st[0], 16 * NIT + 16)
            n.activation(C["c3row"][:, :], srow[:, :], ACT.Copy).then_inc(s_end, 1)
            act.wait_ge(s_end, 2)

    with ExitStack() as ctx:
        m = Mem(nc, ctx, "fs")
        s_a, s_d = m.sem("a"), m.sem("d")
        block = ctx.enter_context(nc.Block())

        @block.vector
        def _(dve):
            nc.vector.tensor_tensor(C["c3row"][:, :], C["c3row"][:, :], C["bias2"][0:1, :], ALU.add).then_inc(s_a, 1)

        @block.sync
        def _(sp):
            sp.wait_ge(s_a, 1)
            sp.dma_start(T["D3"][SENT:SENT + 1, :], C["c3row"][:, :]).then_inc(s_d, 16)
            sp.wait_ge(s_d, 16)
            sp.dma_start(C["c3"][:, :], T["D3"][SENT].unsqueeze(0).partition_broadcast(P)).then_inc(s_d, 16)
            sp.wait_ge(s_d, 32)



def batch_block(nc, T, C):
    F = 56
    NC = EF // F
    with ExitStack() as ctx:
        m = Mem(nc, ctx, "bn")
        em = m.sb("em", [P, EF])
        ag = [m.sb(f"ag{i}", [P, F, D]) for i in range(2)]
        q = [m.sb(f"q{i}", [P, F, D]) for i in range(2)]
        sq = [m.sb(f"sq{i}", [P, F, D]) for i in range(2)]
        part = m.sb("part", [P, 2, NC, D])
        tot = m.sb("tot", [P, 2, D])
        t = m.sb("t", [P, 6, D])
        ps = m.ps("ps", [P, 2 * D])
        s_em, s_q, s_sq, s_r, s_ch, s_pe = (m.sem(x) for x in "em q sq r ch pe".split())
        s_ld = m.sems("ld", 2)
        block = ctx.enter_context(nc.Block())
        ag_v = T["AG"].rearrange("(p f) d -> p f d", f=EF)

        @block.sync
        def _(sp):
            sp.dma_start(em[:, :], T["ENDM"].rearrange("(p f) -> p f", f=EF)).then_inc(s_em, 16)
            for c in range(NC):
                if c >= 2:
                    sp.wait_ge(s_q, c - 1)
                sp.dma_start(ag[c % 2][:, :, :], ag_v[:, c * F:(c + 1) * F, :]).then_inc(s_ld[c % 2], 16)

        @block.scalar
        def _(act):
            for c in range(NC):
                act.wait_ge(s_q, c + 1)
                if c >= 2:
                    act.wait_ge(s_r, c - 1)
                nc.scalar.activation(sq[c % 2][:, :, :], q[c % 2][:, :, :], ACT.Square).then_inc(s_sq, 1)

        @block.tensor
        def _(pe):
            pe.wait_ge(s_r, NC + 1)
            nc.tensor.matmul(ps[:, :], C["ones_sq"][:, :], tot[:, :, :].rearrange("p s d -> p (s d)"),
                             start=True, stop=True).then_inc(s_pe, 1)

        @block.vector
        def _(dve):
            v = nc.vector
            ch = Chain(dve, s_ch, 0)
            ch.at(0)
            dve.wait_ge(s_em, 16)
            by_d = lambda x: x.rearrange("p f d -> p d f")

            def squares(c):
                dve.wait_ge(s_sq, c + 1)
                v.tensor_reduce(part[:, 1, c, :], by_d(sq[c % 2][:, :, :]), X, ALU.add).then_inc(s_r, 1)

            for c in range(NC):
                dve.wait_ge(s_ld[c % 2], 16 * (c // 2 + 1))
                if c >= 2:
                    dve.wait_ge(s_sq, c - 1)
                v.tensor_tensor(q[c % 2][:, :, :], ag[c % 2][:, :, :], bcast(em[:, c * F:(c + 1) * F], D), ALU.mult
                                ).then_inc(s_q, 1)
                dve.wait_ge(s_q, c + 1)
                ch(v.tensor_reduce(part[:, 0, c, :], by_d(q[c % 2][:, :, :]), X, ALU.add))
                if c >= 1:
                    squares(c - 1)
            squares(NC - 1)
            dve.wait_ge(s_r, NC)
            v.tensor_reduce(tot[:, :, :], part[:, :, :, :].rearrange("p s c d -> p s d c"), X, ALU.add).then_inc(s_r, 1)
            dve.wait_ge(s_pe, 1)
            mean, ex2, var, y, t1, t2 = (t[:, i, :] for i in range(6))
            v.tensor_scalar(mean, ps[:, 0:D], 1.0 / N, None, ALU.mult)
            ch(v.tensor_scalar(ex2, ps[:, D:2 * D], 1.0 / N, EPS, ALU.mult, ALU.add))
            ch(v.tensor_tensor(t1, mean, mean, ALU.mult))
            ch(v.tensor_tensor(var, ex2, t1, ALU.subtract))
            ch(v.tensor_scalar(t1.bitcast(I32), var.bitcast(I32), 1, None, ALU.logical_shift_right))
            ch(v.tensor_scalar(y.bitcast(I32), t1.bitcast(I32), -1.0, RSQRT_SEED, ALU.mult, ALU.add))
            for _ in range(4):
                ch(v.tensor_tensor(t1, y, y, ALU.mult))
                ch(v.scalar_tensor_tensor(t2, t1, -0.5, var, ALU.mult, ALU.mult))
                ch(v.scalar_tensor_tensor(y, t2, 1.5, y, ALU.add, ALU.mult))
            ch(v.tensor_tensor(C["k1"][:, :], y, C["gamma"][:, :], ALU.mult))
            ch(v.tensor_tensor(t1, mean, C["bias3"][:, :], ALU.add))
            ch(v.tensor_tensor(t2, C["bias3"][:, :], t1, ALU.subtract))
            ch(v.tensor_tensor(t1, t2, C["k1"][:, :], ALU.mult))
            ch(v.tensor_tensor(C["k0"][:, :], t1, C["beta"][:, :], ALU.add))


def nodes_block(nc, a, out, C):
    G = 10
    NR = P * G
    NF = N // NR
    PT = (N - NF * NR) // G
    STEPS = NF // U
    assert NF % U == 0 and (NF * P + PT) * G == N
    with ExitStack() as ctx:
        m = Mem(nc, ctx, "n")
        two = range(U)
        x = [m.sb(f"x{k}", [P, G, D]) for k in two]
        x3 = [m.sb(f"x3{k}", [P, G, D]) for k in two]
        h = [m.sb(f"h{k}", [P, G, D]) for k in two]
        t = [m.sb(f"t{k}", [P, G, D]) for k in two]
        gl = [m.sb(f"gl{k}", [P, G, D]) for k in two]
        y = [m.sb(f"y{k}", [P, G, D]) for k in two]
        bn = m.sb("bn", [P, U * G, 6])
        sm = m.sb("sm", [P, 6, U * G])
        s_ld, s_st = m.sems("ld"), m.sems("st")
        s_x3, s_bn, s_f, s_h, s_t, s_gl, s_y, s_ch = (m.sem(q) for q in "x3 bn f h t gl y ch".split())
        block = ctx.enter_context(nc.Block())
        cnt = lambda it, k: it * U + k + 1

        def rows_of(dram, it, k, np_=P):
            return dram[bass.ds((it * U + k) * NR, np_ * G), :].rearrange("(p g) d -> p g d", g=G)

        def every(eng, body):
            body(0, True, two, P)
            with eng.Fori(1, STEPS) as it:
                body(it, False, two, P)
            body(STEPS, False, range(1), PT)

        @block.sync
        def _(sp):
            def body(it, first, slots, np_):
                for k in slots:
                    if not first:
                        sp.wait_ge(s_x3, cnt(it - 1, k))
                    sp.dma_start(x[k][0:np_, :, :], rows_of(a["x"], it, k, np_)).then_inc(s_ld[k], 16)
            every(sp, body)

        @block.gpsimd
        def _(pool):
            def body(it, first, slots, np_):
                bc = lambda w: w[0:np_, :].unsqueeze(1).to_broadcast([np_, G, D])
                for k in slots:
                    pool.wait_ge(s_ld[k], 16 * (it + 1))
                    if not first:
                        pool.wait_ge(s_y, cnt(it - 1, k))
                    nc.gpsimd.tensor_tensor(x3[k][0:np_, :, :], x[k][0:np_, :, :], bc(C["c3"]), ALU.add).then_inc(s_x3, 1)
            every(pool, body)

        @block.vector
        def _(dve):
            v = nc.vector
            ch = Chain(dve, s_ch, 1 + LN_OPS)

            def body(it, first, slots, np_):
                ch.at(it)
                bc = lambda w: w[0:np_, :].unsqueeze(1).to_broadcast([np_, G, D])
                ng = len(slots) * G
                for k in slots:
                    dve.wait_ge(s_x3, cnt(it, k))
                    last = row_moments(nc, x3[k][0:np_, :, :], bn[0:np_, k * G:(k + 1) * G, :])
                ch(last)
                if not first:
                    dve.wait_ge(s_h, cnt(it - 1, U - 1))
                norm_factors(nc, ch, bn[0:np_, 0:ng, :], sm[0:np_, :, 0:ng], s_f)
                for k in slots:
                    dve.wait_ge(s_h, cnt(it, k))
                    if not first:
                        dve.wait_ge(s_gl, cnt(it - 1, k))
                    v.tensor_tensor(t[k][0:np_, :, :], h[k][0:np_, :, :], bc(C["k0"]), ALU.add).then_inc(s_t, 1)
                for k in slots:
                    dve.wait_ge(s_gl, cnt(it, k))
                    if not first:
                        dve.wait_ge(s_st[k], 16 * it)
                    v.tensor_tensor(y[k][0:np_, :, :], gl[k][0:np_, :, :], x3[k][0:np_, :, :], ALU.add).then_inc(s_y, 1)
                ch.done()
            every(dve, body)

        @block.scalar
        def _(act):
            n = nc.scalar

            def body(it, first, slots, np_):
                act.wait_ge(s_f, it + 1)
                for k in slots:
                    if not first:
                        act.wait_ge(s_t, cnt(it - 1, k))
                    for g in range(G):
                        c = k * G + g
                        last = n.activation(h[k][0:np_, g, :], x3[k][0:np_, g, :], ACT.Relu,
                                            bias=sm[0:np_, 5, c:c + 1], scale=sm[0:np_, 4, c:c + 1])
                    last.then_inc(s_h, 1)
                for k in slots:
                    act.wait_ge(s_t, cnt(it, k))
                    if not first:
                        act.wait_ge(s_y, cnt(it - 1, k))
                    n.activation(gl[k][0:np_, :, :], t[k][0:np_, :, :], ACT.Gelu).then_inc(s_gl, 1)
                for k in slots:
                    act.wait_ge(s_y, cnt(it, k))
                    act.dma_start(rows_of(out, it, k, np_), y[k][0:np_, :, :]).then_inc(s_st[k], 16)
            every(act, body)
            act.wait_ge(s_st[0], 16 * (STEPS + 1))
            act.wait_ge(s_st[1], 16 * STEPS)


def targets_block(nc, T, out, C):
    with ExitStack() as ctx:
        m = Mem(nc, ctx, "o")
        two = range(U)
        ix = [m.sb(f"ix{k}", [P, J], I32) for k in two]
        ag, h, x3, t1, t2, t3, gl, y = ([m.sb(f"{n}{k}", [P, J, D]) for k in two] for n in
                                        "ag h x3 t1 t2 t3 gl y".split())
        s_ld, s_sc = m.sems("ld"), m.sems("sc")
        s_t, s_gl, s_y, s_ch, s_turn, s_spturn = (m.sem(q) for q in "t gl y ch turn spturn".split())
        block = ctx.enter_context(nc.Block())
        cnt = lambda it, k: it * U + k + 1

        @block.sync
        def _(sp):
            def body(it, first):
                for k in two:
                    if not first:
                        hold(sp, s_spturn, (s_y, cnt(it - 1, k)), (s_sc[k], 16 * J * it))
                    for dst, src in ((ix[k][:, :], words(T["SCAT"], it, k)), (ag[k][:, :, :], rows(T["AG"], it, k)),
                                     (h[k][:, :, :], rows(T["HN3"], it, k)), (x3[k][:, :, :], rows(T["X3"], it, k))):
                        sp.dma_start(dst, src).then_inc(s_ld[k], 16)
            steps(sp, body)

        @block.vector
        def _(dve):
            v = nc.vector
            ch = Chain(dve, s_ch, 2 * U)
            k1, k0 = (C[w][:, :].unsqueeze(1).to_broadcast([P, J, D]) for w in ("k1", "k0"))

            def body(it, first):
                ch.at(it)
                for k in two:
                    dve.wait_ge(s_ld[k], 64 * (it + 1))
                    ch(v.tensor_tensor(t1[k][:, :, :], ag[k][:, :, :], k1, ALU.mult))
                    ch(v.tensor_tensor(t2[k][:, :, :], t1[k][:, :, :], h[k][:, :, :], ALU.add))
                    v.tensor_tensor(t3[k][:, :, :], t2[k][:, :, :], k0, ALU.add).then_inc(s_t, 1)
                for k in two:
                    dve.wait_ge(s_gl, cnt(it, k))
                    if not first:
                        dve.wait_ge(s_sc[k], 16 * J * it)
                    v.tensor_tensor(y[k][:, :, :], gl[k][:, :, :], x3[k][:, :, :], ALU.add).then_inc(s_y, 1)
                ch.done()
            steps(dve, body)

        @block.scalar
        def _(act):
            def body(it, first):
                for k in two:
                    act.wait_ge(s_t, cnt(it, k))
                    nc.scalar.activation(gl[k][:, :, :], t3[k][:, :, :], ACT.Gelu).then_inc(s_gl, 1)
            steps(act, body)

        @block.gpsimd
        def _(pool):
            def body(it, first):
                for k in two:
                    hold(pool, s_turn, (s_y, cnt(it, k)), (s_ld[k], 64 * (it + 1)))
                    for j in range(J):
                        nc.gpsimd.indirect_dma_start(
                            out, bass.IndirectOffsetOnAxis(ap=ix[k][:, j:j + 1], axis=0), y[k][:, j, :], None,
                            bounds_check=N - 1, oob_is_err=False).then_inc(s_sc[k], 16)
            steps(pool, body)
            for k in two:
                pool.wait_ge(s_sc[k], 16 * J * NIT)



_INS = ['x', 'src', 'dst', 'edge_attr_t', 'w_comp_t', 'edge_type_4', 'edge_weight1', 'node_type_2',
        'L0_gnn_w1_l', 'L0_gnn_w1_r', 'L0_gnn_w1_e', 'L0_gnn_att1', 'L0_gnn_b1', 'L0_gnn_w2_l', 'L0_gnn_w2_r',
        'L0_gnn_w2_e', 'L0_gnn_att2', 'L0_gnn_b2', 'L0_gnn_wc', 'L0_gnn_bc', 'L0_gnn_ln_g', 'L0_gnn_ln_b',
        'L0_gnn_wr', 'L0_gnn_br', 'L0_gnn_lnr_g', 'L0_gnn_lnr_b', 'L1_gnn_W', 'L1_gnn_a', 'L2_gnn_weight',
        'L2_gnn_bias', 'L3_gnn_W_l', 'L3_gnn_b_l', 'L3_gnn_W_r', 'L3_gnn_b_r', 'L3_gnn_W_e',
        'L3_gnn_att', 'L3_gnn_bias', 'L3_gnn_gamma', 'L3_gnn_beta']



def program(nc, a, out):
    T = {}

    def table(name, shape, dt=F32):
        T[name] = nc.dram_tensor(f"t_{name}", shape, dt, kind="Internal").ap()

    for name in ("SRC", "DST", "SCAT", "POS", "PSRC", "PDST", "NTS", "NTD"):
        table(name, [EP], I32)
    for name in ("START", "KEEP", "ENDM", "EW", "ET"):
        table(name, [EP])
    table("LP", [P * NTAB], I32)
    table("EA", [18, EP])
    table("XSD", [EP, 2 * D])
    table("SSRC", [SORTED + 2])
    table("EID", [SORTED], I32)
    table("EL", [SORTED])
    table("AL", [SORTED])
    table("H1", [EP, P])
    table("H2T", [D, EP])
    for name in ("D1", "D2", "D3", "D1D", "HS", "AG", "X3", "HN3"):
        table(name, [EP, D])
    for name in ("SE", "SA", "REL"):
        table(name, [EP])
    with ExitStack() as ctx:
        m = Mem(nc, ctx, "c")
        C = {name: m.sb(name, shape) for name, shape in (
            ("ident", [P, P]), ("sel8", [8, P]), ("sel2", [2, P]), ("sel4", [4, D]), ("att1b", [P, 8]),
            ("att2b", [P, 2]), ("att3b", [D, 4]), ("ones_row", [1, P]), ("wz1", [P, P]), ("we1", [1, P]),
            ("wl2", [P, P]), ("wr2", [P, P]), ("we2", [1, P]), ("wz3", [P, D]), ("we3", [18, D]), ("b1", [P, 1]),
            ("b2", [D, 1]), ("mean2", [P, D]),
            ("b1row", [1, P]), ("brow", [1, P]), ("bcol", [D, EP - E]), ("cstk", [P, D]), ("ones_sq", [P, P]),
            ("lng", [P, D]), ("lnb", [P, D]), ("lrg", [P, D]), ("lrb", [P, D]), ("gamma", [P, D]), ("beta", [P, D]),
            ("bias3", [P, D]), ("bias2", [P, D]), ("wca", [D + 1, D]), ("wra", [D + 1, D]), ("w1", [D, D]),
            ("a1", [D, 2]), ("wflat", [P, 4, D]), ("w1t", [D, D]), ("wb", [P, P]), ("wft", [D, 4, P]),
            ("relp", [P, 4]), ("c3row", [1, D]), ("c3", [P, D]), ("k1", [P, D]), ("k0", [P, D]), ("bl3", [D, 1]))}
        setup_block(nc, a, T, C)
        weights_block(nc, T, C)
        index_block(nc, a, T, C)
        gat_block(nc, a, T, C, "a", 8, P, False)
        gat_block(nc, a, T, C, "b", 2, P, True)
        mlp_block(nc, T, C)
        logit_block(nc, T, C)
        permute_block(nc, T, "ps", True)
        softmax_block(nc, T, C)
        permute_block(nc, T, "pb", False)
        mix_block(nc, T, C)
        relation_block(nc, T, C)
        gat_block(nc, a, T, C, "g", 4, D, False)
        batch_block(nc, T, C)
        nodes_block(nc, a, out, C)
        targets_block(nc, T, out, C)


def kernel(**inputs):
    import numpy as _np
    import concourse.bacc as _bacc
    from concourse import mybir as _mybir
    from concourse.bass_utils import run_bass_kernel_spmd as _run

    nc = _bacc.Bacc("TRN2", target_bir_lowering=False, num_devices=1)
    inputs = dict(inputs)
    inputs["edge_attr_t"] = _np.asarray(inputs["edge_attr_16"]).T
    inputs["w_comp_t"] = _np.asarray(inputs["L2_gnn_w_comp"]).T
    arrays, args = {}, {}
    for name in _INS:
        v = _np.ascontiguousarray(inputs[name])
        arrays[f"in_{name}"] = v
        args[name] = nc.dram_tensor(f"in_{name}", v.shape, _mybir.dt.from_np(v.dtype), kind="ExternalInput").ap()
    out = nc.dram_tensor("out", (N, D), F32, kind="ExternalOutput").ap()
    program(nc, args, out)
    r = _run(nc, [arrays], core_ids=[0])
    return r.results[0]["out"]
```

```python
from contextlib import ExitStack

import concourse.bass as bass
from concourse import mybir

ALU = mybir.AluOpType
ACT = mybir.ActivationFunctionType
F32 = mybir.dt.float32
I32 = mybir.dt.int32
BF16 = mybir.dt.bfloat16
X = mybir.AxisListType.X

P = 128
N, D = 100000, 64
E = 50000
CH = 512
J = CH // P
NCH = -(-E // CH)
EP = NCH * CH
EF = EP // P
U = 2
NIT = NCH // U
SENT = EP - 1
BIG = 1.0e30
SKIP = 1 << 20
NTAB = -(-N // P)
EPS = 1e-5
SLOPE = 0.2
SORTED = 1 << (E - 1).bit_length()
SF = SORTED // P
SLAST = E - (P - 1) * EF


class Chain:

    def __init__(self, eng, sem, per_step):
        self.eng, self.sem, self.per = eng, sem, per_step

    def at(self, it):
        self.base, self.n = it * self.per, 0

    def __call__(self, ins):
        self.n += 1
        ins.then_inc(self.sem, 1)
        self.eng.wait_ge(self.sem, self.base + self.n)

    def done(self):
        assert self.n == self.per, (self.n, self.per)


def steps(eng, body, last=NIT):
    body(0, True)
    with eng.Fori(1, last) as it:
        body(it, False)


def hold(eng, turn, *waits):
    for sem, value in waits:
        eng.wait_ge(sem, value)
        eng.sem_inc(turn, 1)


def rows(dram, n):
    return dram[bass.ds(n * CH, CH), :].rearrange("(p j) d -> p j d", j=J)


def words(dram, n):
    return dram[bass.ds(n * CH, CH)].rearrange("(p j) -> p j", j=J)


def cols(dram, n):
    return dram[:, bass.ds(n * CH, CH)]


def line(dram, n, parts):
    return dram[bass.ds(n * CH, CH)].unsqueeze(0).partition_broadcast(parts)


def flow(eng, stages, total=NCH, slots=2):
    stages = [(s[0], s[1], total if len(s) < 3 else s[2]) for s in stages]
    lag = max(s for s, _, _ in stages)
    first = -(-(lag + slots) // slots) * slots
    last = total // slots * slots

    def step(t):
        for s, fn, chunks in stages:
            n = t - s
            if 0 <= n < chunks:
                fn(n, n % slots, n // slots, n >= slots)

    for t in range(first):
        step(t)
    with eng.Fori(first // slots, last // slots) as i:
        for u in range(slots):
            for s, fn, _ in stages:
                n = i * slots + (u - s)
                fn(n, (u - s) % slots, i + (u - s) // slots, True)
    for t in range(last, total + lag):
        step(t)


def later(n, least=1):
    return not isinstance(n, int) or n >= least


def chunks_of(k, slots, total=NCH):
    return len(range(k, total, slots))


def bcast(ap, n):
    return ap.unsqueeze(2).to_broadcast([ap.shape[0], ap.shape[1], n])


class Mem:

    def __init__(self, nc, ctx, tag):
        self.nc, self.ctx, self.tag = nc, ctx, tag
        self.semaphores = []
        ctx.callback(self.close)

    def close(self):
        if self.semaphores:
            self.nc.clear_and_free_semaphores(self.semaphores)
            self.nc.all_engine_barrier()

    def sb(self, name, shape, dt=F32):
        return self.ctx.enter_context(self.nc.sbuf_tensor(f"{self.tag}_{name}", shape, dt))

    def ps(self, name, shape, dt=F32):
        return self.ctx.enter_context(self.nc.psum_tensor(f"{self.tag}_{name}", shape, dt))

    def sem(self, name):
        self.semaphores.append(self.nc.alloc_semaphore(f"{self.tag}_{name}"))
        return self.semaphores[-1]

    def sems(self, name, n=U):
        return [self.sem(f"{name}{i}") for i in range(n)]



def setup_block(nc, a, T, C):
    with ExitStack() as ctx:
        m = Mem(nc, ctx, "su")
        dstp = m.sb("dstp", [P, EF], I32)
        dstc = m.sb("dstc", [P, EF], I32)
        dstn = m.sb("dstn", [P, EF], I32)
        srci = m.sb("srci", [P, EF], I32)
        ewp = m.sb("ewp", [P, EF])
        etp = m.sb("etp", [P, EF], I32)
        fp = m.sb("fp", [P, EF])
        fc = m.sb("fc", [P, EF])
        fn = m.sb("fn", [P, EF])
        st = m.sb("st", [P, EF])
        keep = m.sb("keep", [P, EF])
        en = m.sb("en", [P, EF])
        t1 = m.sb("t1", [P, EF])
        dstg = m.sb("dstg", [P, EF], I32)
        scat = m.sb("scat", [P, EF], I32)
        etf = m.sb("etf", [P, EF])
        pos = m.sb("pos", [P, EF], I32)
        lp0 = m.sb("lp0", [P, NTAB], I32)
        eap = m.sb("eap", [18, EP - E])
        ones = m.sb("ones", [2, CH * 7])
        minus = m.sb("minus", [1, 1])
        zeros = m.sb("zeros", [P, (SORTED - EP) // P])
        ewb = [m.sb(f"ewb{i}", [P, EF], BF16) for i in range(3)]
        rest = [m.sb(f"rest{i}", [P, EF]) for i in range(2)]
        pads, loads, stores = m.sem("pads"), m.sem("loads"), m.sem("stores")
        cst, dv, pl = m.sem("cst"), m.sem("dv"), m.sem("pl")
        wl = m.sem("wl")
        block = ctx.enter_context(nc.Block())
        NLOAD = [0]

        @block.vector
        def _(dve):
            nc.vector.memset(dstp[:, :], N + 1)
            nc.vector.memset(dstc[:, :], N)
            nc.vector.memset(dstn[:, :], N)
            nc.vector.memset(srci[:, :], 0)
            nc.vector.memset(ewp[:, :], 0.0)
            nc.vector.memset(etp[:, :], 0)
            nc.vector.memset(lp0[:, :], SENT)
            nc.vector.memset(eap[:, :], 0.0)
            nc.vector.memset(ones[:, :], 1.0)
            for t, v in ((C["ident"], 0.0), (C["sel8"], 1.0), (C["sel2"], 1.0), (C["sel4"], 1.0), (C["att1b"], 0.0),
                         (C["att2b"], 0.0), (C["att3b"], 0.0), (C["cstk"], 0.0), (C["ones_sq"], 1.0), (C["wz3"], 0.0), (C["we3"], 0.0), (minus, -1.0),
                         (zeros, 0.0)):
                nc.vector.memset(t[:, :], v)
            nc.vector.memset(C["ones_row"][:, :], 1.0).then_inc(pads, 1)
            dve.wait_ge(loads, 16 * 13)
            ch = Chain(dve, dv, 99)
            ch.at(0)
            nc.vector.tensor_copy(fp[:, :], dstp[:, :])
            nc.vector.tensor_copy(fc[:, :], dstc[:, :])
            nc.vector.tensor_copy(etf[:, :], etp[:, :])
            ch(nc.vector.tensor_copy(fn[:, :], dstn[:, :]))
            nc.vector.tensor_tensor(keep[:, :], fp[:, :], fc[:, :], ALU.is_equal)
            ch(nc.vector.tensor_tensor(en[:, :], fn[:, :], fc[:, :], ALU.is_equal))
            nc.vector.tensor_scalar(st[:, :], keep[:, :], -1.0, BIG, ALU.add, ALU.mult)
            nc.vector.scalar_tensor_tensor(t1[:, :], en[:, :], float(SKIP), fc[:, :], ALU.mult, ALU.add)
            ch(nc.vector.tensor_scalar(dstg[:, :], fc[:, :], float(N - 1), None, ALU.min))
            ch(nc.vector.tensor_copy(scat[:, :], t1[:, :]))
            nc.vector.tensor_scalar(en[:, :], en[:, :], -1.0, 1.0, ALU.mult, ALU.add)
            ch(nc.vector.tensor_scalar(t1[:, :], fc[:, :], float(N) - 0.5, None, ALU.is_lt))
            ch(nc.vector.tensor_tensor(en[:, :], en[:, :], t1[:, :], ALU.mult))
            three_parts(nc, ch, ewp, ewb, rest)

        @block.gpsimd
        def _(pool):
            nc.gpsimd.iota(pos[:, :], [[1, EF]], base=0, channel_multiplier=EF).then_inc(pl, 1)
            pool.wait_ge(pads, 1)
            nc.gpsimd.affine_select(out=C["ident"][:, :], in_=C["ident"][:, :], compare_op=ALU.not_equal, fill=1.0,
                                    base=0, pattern=[[-1, P]], channel_multiplier=1)
            n = 1
            for name, w in (("sel8", 16), ("sel2", 64), ("sel4", 16)):
                t = C[name]
                cols_ = t.shape[1]
                nc.gpsimd.affine_select(out=t[:, :], in_=t[:, :], compare_op=ALU.is_ge, fill=0.0, base=0,
                                        pattern=[[1, cols_]], channel_multiplier=-w).then_inc(pl, 1)
                n += 1
                pool.wait_ge(pl, n)
                nc.gpsimd.affine_select(out=t[:, :], in_=t[:, :], compare_op=ALU.is_ge, fill=0.0, base=w - 1,
                                        pattern=[[-1, cols_]], channel_multiplier=w).then_inc(pl, 1)
                n += 1

        @block.sync
        def _(sp):
            sp.wait_ge(pads, 1)

            def padded(dst, src, before=0):
                lo = EF - before
                if before == 1:
                    sp.dma_start(dst[0:1, 1:EF], src[0:lo].unsqueeze(0)).then_inc(loads, 16)
                    sp.dma_start(dst[1:P - 1, :], src[lo:lo + (P - 2) * EF].rearrange("(p f) -> p f", f=EF)).then_inc(loads, 16)
                    left = E - lo - (P - 2) * EF
                    sp.dma_start(dst[P - 1:P, 0:left], src[E - left:E].unsqueeze(0)).then_inc(loads, 16)
                else:
                    full = (P - 1) * EF
                    s0 = -before
                    sp.dma_start(dst[0:P - 1, :], src[s0:s0 + full].rearrange("(p f) -> p f", f=EF)).then_inc(loads, 16)
                    left = E - s0 - full
                    sp.dma_start(dst[P - 1:P, 0:left], src[s0 + full:E].unsqueeze(0)).then_inc(loads, 16)

            padded(dstp, a["dst"], 1)
            padded(dstc, a["dst"])
            padded(dstn, a["dst"], -1)
            padded(srci, a["src"])
            padded(ewp, a["edge_weight1"].rearrange("e a -> (e a)"))

            padded(etp, a["edge_type_4"])
            sp.wait_ge(loads, 16 * 13)
            sp.wait_ge(dv, 6 + PART_OPS)
            sp.wait_ge(pl, 1)
            full = lambda t: t.rearrange("(p f) -> p f", f=EF)
            n = 0
            for dram, sbt in ((T["SRC"], srci), (T["DST"], dstg), (T["SCAT"], scat), (T["POS"], pos), (T["START"], st),
                              (T["KEEP"], keep), (T["ENDM"], en), (T["ET"], etf)):
                sp.dma_start(full(dram), sbt[:, :]).then_inc(stores, 16)
                n += 16
            for row in range(9):
                sp.dma_start(full(T["EWP"][row]), ewb[row % 3][:, :]).then_inc(stores, 16)
                n += 16
            sp.dma_start(T["LP"].rearrange("(p f) -> p f", f=NTAB), lp0[:, :]).then_inc(stores, 16)
            sp.dma_start(T["EA"][0:16, 0:E], a["edge_attr_t"]).then_inc(stores, 16)
            sp.dma_start(T["EA"][0:16, E:EP], eap[0:16, :]).then_inc(stores, 16)
            n += 48
            sp.dma_start(T["EA"][16:18, :].rearrange("a (b c) -> a b c", c=CH * 7),
                         ones[:, :].unsqueeze(1).to_broadcast([2, NCH // 7, CH * 7])).then_inc(stores, 16)
            n += 16
            tail_of = lambda t: t[EP:SORTED].rearrange("(p f) -> p f", p=P)
            sp.dma_start(tail_of(T["EL"]), zeros[:, :]).then_inc(stores, 16)
            sp.dma_start(tail_of(T["AL"]), zeros[:, :]).then_inc(stores, 16)
            sp.dma_start(T["AL"][0:EP].rearrange("(p f) -> p f", f=EF), ewp[:, :]).then_inc(stores, 16)
            sp.dma_start(T["SSRC"][0:1].unsqueeze(0), minus[:, :]).then_inc(stores, 16)
            n += 64
            sp.wait_ge(stores, n)

        @block.scalar
        def _(act):
            act.wait_ge(pads, 1)
            n = 0

            def load(dst, src):
                act.dma_start(dst, src).then_inc(wl, 16)
                return 1
            n += load(C["wz1"][0:64, :], a["L0_gnn_w1_l"])
            n += load(C["wz1"][64:128, :], a["L0_gnn_w1_r"])
            n += load(C["we1"][:, :], a["L0_gnn_w1_e"])
            n += load(C["wl2"][:, :], a["L0_gnn_w2_l"])
            n += load(C["wr2"][:, :], a["L0_gnn_w2_r"])
            n += load(C["we2"][:, :], a["L0_gnn_w2_e"])
            n += load(C["wz3"][0:64, 0:D], a["L3_gnn_W_l"])
            n += load(C["wz3"][0:64, D:P], a["L3_gnn_W_l"])
            n += load(C["wz3"][64:128, 0:D], a["L3_gnn_W_r"])
            n += load(C["we3"][0:16, 0:D], a["L3_gnn_W_e"])
            n += load(C["we3"][16:17, 0:D], a["L3_gnn_b_l"].unsqueeze(0))
            n += load(C["we3"][17:18, 0:D], a["L3_gnn_b_r"].unsqueeze(0))
            n += load(C["b1"][:, :], a["L0_gnn_b1"].unsqueeze(1))
            n += load(C["b2"][:, :], a["L0_gnn_b2"].unsqueeze(1))
            n += load(C["bl3"][:, :], a["L3_gnn_b_l"].unsqueeze(1))
            n += load(C["b1row"][:, :], a["L0_gnn_b1"].unsqueeze(0))
            for name, key in (("lng", "L0_gnn_ln_g"), ("lnb", "L0_gnn_ln_b"), ("lrg", "L0_gnn_lnr_g"), ("lrb", "L0_gnn_lnr_b"),
                              ("gamma", "L3_gnn_gamma"), ("beta", "L3_gnn_beta"), ("bias3", "L3_gnn_bias")):
                n += load(C[name][:, :], a[key].unsqueeze(0).partition_broadcast(P))
            n += load(C["bias2"][:, :], a["L2_gnn_bias"].partition_broadcast(P))
            for name, w, b in (("wca", "L0_gnn_wc", "L0_gnn_bc"), ("wra", "L0_gnn_wr", "L0_gnn_br")):
                n += load(C[name][0:D, :], a[w])
                n += load(C[name][D:D + 1, :], a[b].unsqueeze(0))
            n += load(C["w1"][:, :], a["L1_gnn_W"])
            for q in range(2):
                n += load(C["a1"][:, q:q + 1], a["L1_gnn_a"][0, q * D:(q + 1) * D].unsqueeze(1))
            n += load(C["wflat"][:, :, :], a["L2_gnn_weight"].rearrange("b i o -> (b i o)").rearrange("(q p i) -> p q i", p=P, i=D))
            comp = a["w_comp_t"]
            for r in range(4):
                for q in range(4):
                    n += load(C["cstk"][32 * r + 8 * q:32 * r + 8 * q + 8, 16 * q:16 * q + 16], comp)
            for name, key, H, W in (("att1b", "L0_gnn_att1", 8, 16), ("att2b", "L0_gnn_att2", 2, 64), ("att3b", "L3_gnn_att", 4, 16)):
                for h in range(H):
                    n += load(C[name][h * W:(h + 1) * W, h:h + 1], a[key][h].unsqueeze(1))
            act.wait_ge(wl, 16 * n)


PART_OPS = 5


def three_parts(nc, ch, x, parts, rest):
    v = nc.vector
    ch(v.tensor_copy(parts[0][:, :], x[:, :]))
    ch(v.tensor_tensor(rest[0][:, :], x[:, :], parts[0][:, :], ALU.subtract))
    ch(v.tensor_copy(parts[1][:, :], rest[0][:, :]))
    ch(v.tensor_tensor(rest[1][:, :], rest[0][:, :], parts[1][:, :], ALU.subtract))
    ch(v.tensor_copy(parts[2][:, :], rest[1][:, :]))


def index_block(nc, a, T, C):
    with ExitStack() as ctx:
        m = Mem(nc, ctx, "ix")
        si = [m.sb(f"si{k}", [P, J], I32) for k in range(U)]
        pv = [m.sb(f"pv{k}", [P, J], I32) for k in range(U)]
        s_in, s_sc = m.sems("in"), m.sems("sc")
        lpt, ntt, tab = (m.sb(x, [P, NTAB], I32) for x in ("lpt", "ntt", "tab"))
        s_nt, s_tl, s_tc, s_tab, s_clr = (m.sem(x) for x in "nt tl tc tab clr".split())
        NTF = N // NTAB
        turn = m.sem("turn")
        key = [m.sb(f"key{i}", [P, SF]) for i in range(2)]
        pay = [m.sb(f"pay{i}", [P, SF]) for i in range(2)]
        tmp = [m.sb(f"tmp{i}", [P, SF // 2]) for i in range(3)]
        sign = m.sb("sign", [P, SF])
        bits = m.sb("bits", [P, SF], I32)
        place = m.sb("place", [P, SF], I32)
        srcs = m.sb("srcs", [P, SF], I32)
        eid = m.sb("eid", [P, SF], I32)
        bk, bp = m.ps("bk", [P, SF]), m.ps("bp", [P, SF])
        full = E // SF
        s_sort, s_seed, s_cl, s_ld, s_tq, s_tp, s_tr, sorted_, s_so = (
            m.sem(x) for x in "sort seed cl ld tq tp tr sorted so".split())
        lp = T["LP"].unsqueeze(1)
        block = ctx.enter_context(nc.Block())

        @block.sync
        def _(sp):
            def positions(it, first):
                for k in range(U):
                    if not first:
                        sp.wait_ge(s_sc[k], 16 * J * it)
                    sp.dma_start(si[k][:, :], words(T["SCAT"], it * U + k)).then_inc(s_in[k], 16)
                    sp.dma_start(pv[k][:, :], words(T["POS"], it * U + k)).then_inc(s_in[k], 16)
            sp.wait_ge(s_clr, 1)
            sp.dma_start(ntt[0:NTF, :], a["node_type_2"][0:NTF * NTAB].rearrange("(p f) -> p f", f=NTAB)).then_inc(s_nt, 16)
            sp.dma_start(ntt[NTF:NTF + 1, 0:N - NTF * NTAB], a["node_type_2"][NTF * NTAB:N].unsqueeze(0)).then_inc(s_nt, 16)
            steps(sp, positions)
            for k in range(U):
                sp.wait_ge(s_sc[k], 16 * J * NIT)
            sp.dma_start(lpt[:, :], T["LP"].rearrange("(p f) -> p f", f=NTAB)).then_inc(s_tl, 16)
            sp.wait_ge(s_tc, 1)
            sp.dma_start(T["LPT"].rearrange("(p f) -> p f", f=NTAB), tab[:, :]).then_inc(s_tab, 16)

            sp.wait_ge(sorted_, 1)
            sp.dma_start(T["SSRC"][1:1 + SORTED].rearrange("(p f) -> p f", p=P), key[0][:, :]).then_inc(s_so, 16)
            sp.dma_start(T["EID"].rearrange("(p f) -> p f", p=P), eid[:, :]).then_inc(s_so, 16)
            sp.wait_ge(s_so, 32)
            sp.wait_ge(s_tab, 16)

        @block.gpsimd
        def _(pool):
            nc.gpsimd.iota(place[:, :], [[1, SF]], base=0, channel_multiplier=SF).then_inc(s_seed, 1)

            def scatter(it, first):
                for k in range(U):
                    hold(pool, turn, (s_in[k], 32 * (it + 1)))
                    for j in range(J):
                        nc.gpsimd.indirect_dma_start(lp, bass.IndirectOffsetOnAxis(ap=si[k][:, j:j + 1], axis=0),
                                                     pv[k][:, j:j + 1], None, bounds_check=N - 1,
                                                     oob_is_err=False).then_inc(s_sc[k], 16)
            steps(pool, scatter)
            for k in range(U):
                pool.wait_ge(s_sc[k], 16 * J * NIT)

        merges = range(1, SORTED.bit_length())
        inner = SF.bit_length() - 1
        turns = [k for k in merges if k > inner]

        @block.vector
        def _(dve):
            v = nc.vector
            ch = Chain(dve, s_sort, 0)
            ch.at(0)
            v.memset(sign[:, :], 1.0)
            v.memset(ntt[:, :], 0).then_inc(s_clr, 1)
            v.memset(srcs[:, :], SKIP).then_inc(s_cl, 1)
            dve.wait_ge(s_seed, 1)
            ch(v.tensor_copy(pay[0][:, :], place[:, :]))
            dve.wait_ge(s_ld, 16 * 2)
            dve.wait_ge(s_cl, 1)
            ch(v.tensor_copy(key[0][:, :], srcs[:, :]))
            cur, nt_, half = 0, 0, SORTED // P // 2

            def exchange(cur, d):
                a_ = lambda t: t[:, :].rearrange("p (g two d) -> p g two d", two=2, d=d)
                h_ = lambda t: t[:, :].rearrange("p (g d) -> p g d", d=d)
                ka, kb = a_(key[cur])[:, :, 0, :], a_(key[cur])[:, :, 1, :]
                pa, pb = a_(pay[cur])[:, :, 0, :], a_(pay[cur])[:, :, 1, :]
                nk, np_ = a_(key[1 - cur]), a_(pay[1 - cur])
                v.tensor_tensor(h_(tmp[0]), ka, kb, ALU.is_gt)
                ch(v.tensor_tensor(h_(tmp[1]), pb, pa, ALU.subtract))
                v.tensor_tensor(nk[:, :, 0, :], ka, kb, ALU.min)
                v.tensor_tensor(nk[:, :, 1, :], ka, kb, ALU.max)
                ch(v.tensor_tensor(tmp[2][:, :], tmp[0][:, :], tmp[1][:, :], ALU.mult))
                v.tensor_tensor(np_[:, :, 0, :], pa, h_(tmp[2]), ALU.add)
                ch(v.tensor_tensor(np_[:, :, 1, :], pb, h_(tmp[2]), ALU.subtract))
                return 1 - cur

            def turn_tiles(cur, n):
                v.memset(tmp[0][:, 0:1], 0.0).then_inc(s_tq, 1)
                dve.wait_ge(s_tr, n + 1)
                return n + 1

            for k in merges:
                ch(v.tensor_scalar(bits[:, :], place[:, :], k, 1, ALU.logical_shift_right, ALU.bitwise_and))
                ch(v.tensor_tensor(key[cur][:, :], key[cur][:, :], sign[:, :], ALU.mult))
                ch(v.tensor_scalar(sign[:, :], bits[:, :], -2.0, 1.0, ALU.mult, ALU.add))
                ch(v.tensor_tensor(key[cur][:, :], key[cur][:, :], sign[:, :], ALU.mult))
                if k > inner:
                    nt_ = turn_tiles(cur, nt_)
                    for j in range(k - 1, inner - 1, -1):
                        cur = exchange(cur, 1 << (j - inner))
                    nt_ = turn_tiles(cur, nt_)
                for j in range(min(k, inner) - 1, -1, -1):
                    cur = exchange(cur, 1 << j)
            if cur:
                ch(v.tensor_copy(key[0][:, :], key[1][:, :]))
            v.tensor_copy(eid[:, :], pay[cur][:, :]).then_inc(sorted_, 1)
            dve.wait_ge(s_nt, 32)
            dve.wait_ge(s_tl, 16)
            v.scalar_tensor_tensor(tab[:, :], lpt[:, :], 2.0, ntt[:, :], ALU.mult, ALU.add).then_inc(s_tc, 1)

        def current_at_turns():
            cur, out = 0, []
            for k in merges:
                if k > inner:
                    out.append(cur)
                    cur = (cur + k - inner) % 2
                    out.append(cur)
                cur = (cur + min(k, inner)) % 2
            return out

        @block.tensor
        def _(pe):
            for n, cur in enumerate(current_at_turns()):
                pe.wait_ge(s_tq, n + 1)
                for tile_, bank in ((key[cur], bk), (pay[cur], bp)):
                    for b in range(SF // P):
                        last = nc.tensor.transpose(bank[:, b * P:(b + 1) * P], tile_[:, b * P:(b + 1) * P], C["ident"][:, :])
                last.then_inc(s_tp, 1)

        @block.scalar
        def _(act):
            act.wait_ge(s_cl, 1)
            act.dma_start(srcs[0:full, :], a["src"][0:full * SF].rearrange("(p f) -> p f", f=SF)).then_inc(s_ld, 16)
            act.dma_start(srcs[full:full + 1, 0:E - full * SF], a["src"][full * SF:E].unsqueeze(0)).then_inc(s_ld, 16)
            for n, cur in enumerate(current_at_turns()):
                act.wait_ge(s_tp, n + 1)
                nc.scalar.activation(key[cur][:, :], bk[:, :], ACT.Copy)
                nc.scalar.activation(pay[cur][:, :], bp[:, :], ACT.Copy).then_inc(s_tr, 1)


def positions_block(nc, T):
    with ExitStack() as ctx:
        m = Mem(nc, ctx, "po")
        full = lambda t: t.rearrange("(p f) -> p f", f=EF)
        raw = [m.sb(f"raw{i}", [P, EF], I32) for i in range(2)]
        at = [m.sb(f"at{i}", [P, EF], I32) for i in range(2)]
        kind = [m.sb(f"kind{i}", [P, EF], I32) for i in range(2)]
        et, part, rel = (m.sb(x, [P, EF]) for x in ("et", "part", "rel"))
        s_ld, s_ch, s_done, s_st = (m.sem(x) for x in "ld ch done st".split())
        block = ctx.enter_context(nc.Block())

        @block.sync
        def _(sp):
            for t, name in ((raw[0], "VSRC"), (raw[1], "VDST"), (et, "ET")):
                sp.dma_start(t[:, :], full(T[name])).then_inc(s_ld, 16)
            sp.wait_ge(s_done, 1)
            for t, name in ((at[0], "PSRC"), (at[1], "PDST"), (rel, "REL")):
                sp.dma_start(full(T[name]), t[:, :]).then_inc(s_st, 16)
            sp.wait_ge(s_st, 48)

        @block.vector
        def _(dve):
            v = nc.vector
            ch = Chain(dve, s_ch, 2)
            ch.at(0)
            dve.wait_ge(s_ld, 48)
            for i in range(2):
                v.tensor_scalar(at[i][:, :], raw[i][:, :], 1, None, ALU.logical_shift_right)
                last = v.tensor_scalar(kind[i][:, :], raw[i][:, :], 1, None, ALU.bitwise_and)
            ch(last)
            ch(v.scalar_tensor_tensor(part[:, :], kind[0][:, :], 8.0, et[:, :], ALU.mult, ALU.add))
            v.scalar_tensor_tensor(rel[:, :], kind[1][:, :], 4.0, part[:, :], ALU.mult, ALU.add).then_inc(s_done, 1)
            ch.done()



LN_OPS = 15
RSQRT_SEED = float(0x5F3759DF)


def row_moments(nc, x, bn):
    for g in range(x.shape[1]):
        last = nc.vector.bn_stats(bn[:, g, :], x[:, g, :])
    return last


def norm_factors(nc, ch, bn, sm, ready):
    v = nc.vector
    me, ve, mo, vo = (bn[:, :, i] for i in (1, 2, 4, 5))
    mean2, t1, t2, var, y = (sm[:, i, :] for i in range(5))
    v.tensor_tensor(mean2, me, mo, ALU.add)
    v.tensor_tensor(t2, ve, vo, ALU.add)
    ch(v.tensor_tensor(t1, me, mo, ALU.subtract))
    ch(v.tensor_tensor(var, t1, t1, ALU.mult))
    ch(v.scalar_tensor_tensor(t1, var, 16.0, t2, ALU.mult, ALU.add))
    ch(v.tensor_scalar(var, t1, 1.0 / D, EPS, ALU.mult, ALU.add))
    ch(v.tensor_scalar(t1.bitcast(I32), var.bitcast(I32), 1, None, ALU.logical_shift_right))
    ch(v.tensor_scalar(y.bitcast(I32), t1.bitcast(I32), -1.0, RSQRT_SEED, ALU.mult, ALU.add))
    for _ in range(3):
        ch(v.tensor_tensor(t1, y, y, ALU.mult))
        ch(v.scalar_tensor_tensor(t2, t1, -0.5, var, ALU.mult, ALU.mult))
        ch(v.scalar_tensor_tensor(y, t2, 1.5, y, ALU.add, ALU.mult))
    v.scalar_tensor_tensor(sm[:, 5, :], mean2, -0.5, y, ALU.mult, ALU.mult).then_inc(ready, 1)



def gat_block(nc, a, T, C, tag, H, R, wide):
    with ExitStack() as ctx:
        m = Mem(nc, ctx, tag)
        W = P if wide else D
        SL = 4
        L = 2 if wide else 3
        slots = range(SL)
        NE = 18 if tag == "g" else 9
        ix = [m.sb(f"ix{k}", [P, 2, J], I32) for k in slots]
        xg = [m.sb(f"xg{k}", [P, J, 2, W]) for k in slots]
        start = [m.sb(f"start{k}", [H, CH]) for k in slots]
        ext = [m.sb(f"ext{k}", [NE, CH], F32 if tag == "g" else BF16) for k in slots]
        hT = [m.sb(f"hT{k}", [P, CH]) for k in slots]
        hT2 = [m.sb(f"hT2{k}", [P, CH]) for k in slots] if wide else None
        zt = [m.sb(f"zt{k}", [R, CH]) for k in slots]
        xl = [m.sb(f"xl{k}", [R, CH]) for k in slots]
        r = [m.sb(f"r{k}", [H, CH + 1]) for k in slots]
        ed = [m.sb(f"ed{k}", [H, 2, CH]) for k in slots]
        ex = [m.sb(f"ex{k}", [H, 2, CH]) for k in slots]
        rp = m.sb("rp", [H, CH])
        den = [m.sb(f"den{k}", [H, CH]) for k in slots]
        recT = [m.sb(f"recT{k}", [P, J * H]) for k in slots]
        msg = m.sb("msg", [R, CH])
        num = [m.sb(f"num{k}", [R, CH]) for k in slots]
        if wide:
            heads = [m.sb(f"heads{k}", [P, J, H, D]) for k in slots]
        oE = [m.sb(f"oE{k}", [P, J, D if wide else R]) for k in slots]
        if not wide:
            bn = m.sb("bn", [P, J * 2, 6])
            sm = m.sb("sm", [P, 6, J * 2])
            hn = [m.sb(f"hn{k}", [P, J, 2, D]) for k in slots]
        if tag == "a":
            go = [m.sb(f"go{k}", [P, 2, J], I32) for k in slots]
            s_go, s_gst = m.sems("go", SL), m.sems("gst", SL)
        if tag == "g":
            xb = [m.sb(f"xb{k}", [P, J, 2, D]) for k in slots]
        bT, bZ, bX, bS, bF0, bF1, bF2, bO = (m.ps(f"bank{b}", [P, CH]) for b in range(8))
        s_ix, s_g, s_xb, s_ext, s_start, s_st, s_xst = (m.sems(x, SL) for x in "ix g xb ext start st xst".split())
        names = "ln hn hT h z zs zt xl s ed ex den rec b sum o div oE turn pturn spturn clear chz ch1 ch3 ch4 tail"
        S = {n: m.sem(n) for n in names.split()}
        block = ctx.enter_context(nc.Block())
        split = lambda t: t.rearrange("r (p j) -> r p j", j=J)

        if tag == "a":
            idx_names, table = ("SRC", "DST"), a["x"]
        elif tag == "b":
            idx_names, table = ("PSRC", "PDST"), T["H1"]
        else:
            idx_names, table = ("PSRC", "PDST"), T["D3"]
        NG = 16 * J * 2
        NXST = 16 if tag == "a" else 32
        stored_rows = not wide

        @block.sync
        def _(sp):
            def indices(n, k, q, old):
                if old:
                    hold(sp, S["spturn"], (s_g[k], NG * q))
                    if tag == "a":
                        hold(sp, S["spturn"], (s_go[k], NG * q))
                for i, name in enumerate(idx_names):
                    sp.dma_start(ix[k][:, i, :], words(T[name], n)).then_inc(s_ix[k], 16)
                if tag == "g":
                    if old:
                        sp.wait_ge(S["hn"], n - SL + 1)
                    sp.dma_start(xb[k][:, :, :, :], rows(T["XSD"], n).rearrange("p j (s d) -> p j s d", s=2)
                                 ).then_inc(s_xb[k], 16)

            def extras(n, k, q, old):
                if old:
                    hold(sp, S["spturn"], (S["z"], n - SL + 1))
                src = cols(T["EA" if tag == "g" else "EWP"], n)
                sp.dma_start(ext[k][:, :], src).then_inc(s_ext[k], 16)
                if tag == "a":
                    hold(sp, S["spturn"], (s_go[k], NG * (q + 1)))
                    sp.dma_start(words(T["VSRC"], n), go[k][:, 0, :]).then_inc(s_gst[k], 16)
                    sp.dma_start(words(T["VDST"], n), go[k][:, 1, :]).then_inc(s_gst[k], 16)
                    hold(sp, S["spturn"], (s_g[k], NG * (q + 1)))
                    sp.dma_start(rows(T["XSD"], n).rearrange("p j (s d) -> p j s d", s=2), xg[k][:, :, :, :]
                                 ).then_inc(s_xst[k], 16)

            def starts(n, k, q, old):
                if old:
                    hold(sp, S["spturn"], (S["ed"], n - SL + 1))
                sp.dma_start(start[k][:, :], line(T["START"], n, H)).then_inc(s_start[k], 16)
            flow(sp, [(0, indices), (1, extras), (1, starts)], slots=SL)
            if tag == "a":
                for k in slots:
                    sp.wait_ge(s_gst[k], 32 * chunks_of(k, SL))

        @block.gpsimd
        def _(pool):
            def gather(n, k, q, old):
                hold(pool, S["turn"], (s_ix[k], 32 * (q + 1)))
                if old and wide:
                    hold(pool, S["turn"], (S["hT"], n - SL + 1))
                elif old:
                    hold(pool, S["turn"], (S["hn"], n - SL + 1), (s_xst[k], NXST * q))
                for i in range(2):
                    for j in range(J):
                        nc.gpsimd.indirect_dma_start(
                            xg[k][:, j, i, :], None, table,
                            bass.IndirectOffsetOnAxis(ap=ix[k][:, i, j:j + 1], axis=0)).then_inc(s_g[k], 16)
                if tag == "a":
                    if old:
                        hold(pool, S["turn"], (s_gst[k], 32 * q))
                    for i in range(2):
                        for j in range(J):
                            nc.gpsimd.indirect_dma_start(
                                go[k][:, i, j:j + 1], None, T["LPT"].unsqueeze(1),
                                bass.IndirectOffsetOnAxis(ap=ix[k][:, i, j:j + 1], axis=0)).then_inc(s_go[k], 16)
            flow(pool, [(0, gather)], slots=SL)

        @block.vector
        def _(dve):
            v = nc.vector
            for k in slots:
                v.memset(r[k][:, :], -BIG)
                v.memset(den[k][:, :], 0.0)
                last = v.memset(num[k][:, :], 0.0)
            last.then_inc(S["clear"], 1)
            dve.wait_ge(S["clear"], 1)
            ch1 = Chain(dve, S["ch1"], 1 + LN_OPS + (tag == "g"))
            chz = Chain(dve, S["chz"], 1)
            ch3, ch4 = Chain(dve, S["ch3"], 3), Chain(dve, S["ch4"], 1)

            def norm(n, k, q, old):
                ch1.at(n)
                dve.wait_ge(s_g[k], NG * (q + 1))
                if tag == "g":
                    dve.wait_ge(s_xb[k], 16 * (q + 1))
                    ch1(v.tensor_tensor(xg[k][:, :, :, :], xg[k][:, :, :, :], xb[k][:, :, :, :], ALU.add))
                ch1(row_moments(nc, xg[k][:, :, :, :].rearrange("p j s d -> p (j s) d"), bn))
                if later(n):
                    dve.wait_ge(S["hn"], n)
                norm_factors(nc, ch1, bn, sm, S["ln"])
                ch1.done()

            def leaky(n, k, q, old):
                if wide:
                    chz.at(n)
                    dve.wait_ge(S["xl"], n + 1)
                    dve.wait_ge(S["z"], n + 1)
                    if old:
                        dve.wait_ge(S["s"], n - SL + 1)
                    chz(v.tensor_tensor(zt[k][:, :], xl[k][:, :], bZ[0:R, :], ALU.add))
                    v.scalar_tensor_tensor(zt[k][:, :], zt[k][:, :], SLOPE, zt[k][:, :], ALU.mult, ALU.max
                                           ).then_inc(S["zt"], 1)
                    return
                dve.wait_ge(S["zs"], n + 1)
                v.tensor_tensor(zt[k][:, :], zt[k][:, :], bZ[0:R, :], ALU.max).then_inc(S["zt"], 1)

            def maximum(n, k, q, old):
                ch3.at(n)
                dve.wait_ge(S["s"], n + 1)
                dve.wait_ge(s_start[k], 16 * (q + 1))
                if old:
                    dve.wait_ge(S["ex"], n - SL + 1)
                sc = bS[0:H, :]
                ch3(v.tensor_copy(r[k][:, 0:1], r[(k - 1) % SL][:, CH:CH + 1]))
                ch3(v.tensor_tensor_scan(r[k][:, 1:CH + 1], start[k][:, :], sc, r[k][:, 0:1], ALU.add, ALU.max))
                v.tensor_tensor(ed[k][:, 1, :], sc, r[k][:, 1:CH + 1], ALU.subtract)
                ch3(v.tensor_tensor(rp[:, :], r[k][:, 0:CH], start[k][:, :], ALU.add))
                v.tensor_tensor(ed[k][:, 0, :], rp[:, :], r[k][:, 1:CH + 1], ALU.subtract).then_inc(S["ed"], 1)
                ch3.done()

            def denominator(n, k, q, old):
                dve.wait_ge(S["ex"], n + 1)
                if later(n):
                    dve.wait_ge(S["den"], n)
                if old:
                    dve.wait_ge(S["o"], n - SL + 1)
                v.tensor_tensor_scan(den[k][:, :], ex[k][:, 0, :], ex[k][:, 1, :], den[(k - 1) % SL][:, CH - 1:CH],
                                     ALU.mult, ALU.add).then_inc(S["den"], 1)

            def sums(n, k, q, old):
                ch4.at(n)
                dve.wait_ge(S["b"], n + 1)
                dve.wait_ge(S["xl"], n + 1)
                ch4(v.tensor_tensor(msg[:, :], bF1[0:R, :], xl[k][:, :], ALU.mult))
                if later(n):
                    dve.wait_ge(S["sum"], n)
                if old:
                    dve.wait_ge(S["o"], n - SL + 1)
                v.tensor_tensor_scan(num[k][:, :], bF0[0:R, :], msg[:, :], num[(k - 1) % SL][:, CH - 1:CH],
                                     ALU.mult, ALU.add).then_inc(S["sum"], 1)
                ch4.done()

            def quotients(n, k, q, old):
                dve.wait_ge(S["o"], n + 1)
                v.reciprocal(recT[k][:, :], bF2[:, 0:J * H]).then_inc(S["rec"], 1)
                dve.wait_ge(S["rec"], n + 1)
                if old:
                    dve.wait_ge(s_st[k], 16 * q)
                by_head = lambda t: t.rearrange("p (g c) -> p g c", c=R // H)
                if wide:
                    v.tensor_tensor(heads[k][:, :, :, :].rearrange("p j h d -> p (j h) d"), by_head(bO[:, :]),
                                    bcast(recT[k][:, :], D), ALU.mult).then_inc(S["div"], 1)
                    dve.wait_ge(S["div"], n + 1)
                    v.tensor_tensor(oE[k][:, :, :], heads[k][:, :, 0, :], heads[k][:, :, 1, :], ALU.add
                                    ).then_inc(S["oE"], 1)
                    return
                to, of = by_head(oE[k][:, :, :].rearrange("p j r -> p (j r)")), by_head(bO[:, 0:J * R])
                if tag == "a":
                    v.scalar_tensor_tensor(to, of, 0.0, bcast(recT[k][:, :], R // H), ALU.max, ALU.mult
                                           ).then_inc(S["oE"], 1)
                else:
                    v.tensor_tensor(to, of, bcast(recT[k][:, :], R // H), ALU.mult).then_inc(S["oE"], 1)
            if wide:
                stages = [(L, leaky), (L + 2, quotients), (L + 1, denominator), (L + 1, sums), (L, maximum)]
            else:
                stages = [(L, leaky), (L + 2, quotients), (L + 1, denominator), (L + 1, sums), (L, maximum), (L - 2, norm)]
            flow(dve, stages, slots=SL)

        @block.scalar
        def _(act):
            f = nc.scalar.activation

            def normed(n, k, q, old):
                act.wait_ge(S["ln"], n + 1)
                if old:
                    act.wait_ge(S["hT"], n - SL + 1)
                    if tag == "g":
                        act.wait_ge(s_xst[k], NXST * q)
                for g in range(2 * J):
                    last = f(hn[k][:, g // 2, g % 2, :], xg[k][:, g // 2, g % 2, :], ACT.Relu,
                             bias=sm[:, 5, g:g + 1], scale=sm[:, 4, g:g + 1])
                last.then_inc(S["hn"], 1)
                if tag == "g":
                    act.wait_ge(S["hn"], n + 1)
                    act.dma_start(rows(T["X3"], n), xg[k][:, :, 1, :]).then_inc(s_xst[k], 16)
                    act.dma_start(rows(T["HN3"], n), hn[k][:, :, 1, :]).then_inc(s_xst[k], 16)

            def turned(n, k, q, old):
                act.wait_ge(S["hT"], n + 1)
                if old:
                    act.wait_ge(S["z"], n - SL + 1)
                if wide:
                    f(hT2[k][:, :], bF2[:, :], ACT.Copy)
                f(hT[k][:, :], bT[:, :], ACT.Copy).then_inc(S["h"], 1)

            def features(n, k, q, old):
                act.wait_ge(S["z"], n + 1)
                if old:
                    act.wait_ge(S["sum"], n - SL + 1)
                if wide:
                    f(xl[k][:, :], bX[0:R, :], ACT.Copy).then_inc(S["xl"], 1)
                else:
                    f(xl[k][:, :], bZ[D:P, :] if tag == "g" else bX[:, :], ACT.Identity,
                      bias=C["bl3" if tag == "g" else "b1"][:, 0:1]).then_inc(S["xl"], 1)

            def values(n, k, q, old):
                act.wait_ge(S["z"], n + 1)
                if old:
                    act.wait_ge(S["s"], n - SL + 1)
                f(zt[k][:, :], bZ[0:R, :], ACT.Copy, scale=SLOPE).then_inc(S["zs"], 1)

            def exponents(n, k, q, old):
                act.wait_ge(S["ed"], n + 1)
                if old:
                    act.wait_ge(S["b"], n - SL + 1)
                    act.wait_ge(S["den"], n - SL + 1)
                f(ex[k][:, :, :], ed[k][:, :, :], ACT.Exp).then_inc(S["ex"], 1)

            def results(n, k, q, old):
                act.wait_ge(S["oE"], n + 1)
                act.dma_start(rows(T[{"a": "H1", "b": "HR", "g": "AG"}[tag]], n), oE[k][:, :, :]).then_inc(s_st[k], 16)
            if wide:
                stages = [(L, features), (L - 1, turned), (L, exponents), (L + 2, results)]
            else:
                stages = [(L, values), (L, features), (L - 1, normed), (L - 1, turned), (L, exponents), (L + 2, results)]
            flow(act, stages, slots=SL)
            for k in slots:
                act.wait_ge(s_st[k], 16 * chunks_of(k, SL))
                if stored_rows:
                    act.wait_ge(s_xst[k], NXST * chunks_of(k, SL))
            if tag == "a":
                f(C["brow"][:, :], C["b1row"][:, :], ACT.Relu).then_inc(S["tail"], 1)
                act.wait_ge(S["tail"], 1)
                act.dma_start(T["H1"][SENT:SENT + 1, :], C["brow"][:, :]).then_inc(s_st[0], 16)
                act.wait_ge(s_st[0], 16 * chunks_of(0, SL) + 16)
            if tag == "b":
                f(C["brow"][:, 0:D], C["b1row"][:, 0:D], ACT.Copy, scale=0.0).then_inc(S["tail"], 1)
                act.wait_ge(S["tail"], 1)
                act.dma_start(T["HR"][SENT:SENT + 1, :], C["brow"][:, 0:D]).then_inc(s_st[0], 16)
                act.wait_ge(s_st[0], 16 * chunks_of(0, SL) + 16)

        @block.tensor
        def _(pe):
            mm, tr = nc.tensor.matmul, nc.tensor.transpose
            wz, we, att, sel = ((C["wz1"], C["we1p"], C["att1b"], C["sel8"]) if tag == "a" else
                                (None, C["we2p"], C["att2b"], C["sel2"]) if tag == "b" else
                                (C["wz3"], C["we3"], C["att3b"], C["sel4"]))

            def turn(n, k, q, old):
                if wide:
                    pe.wait_ge(s_g[k], NG * (q + 1))
                else:
                    pe.wait_ge(S["hn"], n + 1)
                if later(n):
                    pe.wait_ge(S["h"], n)
                if wide and later(n, 3):
                    pe.wait_ge(S["rec"], n - 2)
                if wide:
                    for j in range(J):
                        tr(split(bF2[:, :])[:, :, j], xg[k][:, j, 1, :], C["ident"][:, :])
                for j in range(J):
                    src = xg[k][:, j, 0, :] if wide else hn[k][:, j, :, :].rearrange("p s d -> p (s d)")
                    last = tr(split(bT[:, :])[:, :, j], src, C["ident"][:, :])
                last.then_inc(S["hT"], 1)

            def project(n, k, q, old):
                pe.wait_ge(s_ext[k], 16 * (q + 1))
                pe.wait_ge(S["h"], n + 1)
                if later(n):
                    pe.wait_ge(S["zt"], n)
                    pe.wait_ge(S["xl"], n)
                wx, hx = (C["wl2"][:, :], hT[k][:, :]) if wide else (wz[0:D, :], hT[k][0:D, :])
                wr, hr = (C["wr2"][:, :], hT2[k][:, :]) if wide else (wz[:, :], hT[k][:, :])
                if tag == "g":
                    mm(bZ[:, :], C["wz3"][:, :], hr, start=True, stop=False)
                    mm(bZ[:, :], we[:, :], ext[k][:, :], start=False, stop=True).then_inc(S["z"], 1)
                    return
                mm(bZ[0:R, :], wr, hr, start=True, stop=False)
                mm(bZ[0:R, :], we[:, :], ext[k][:, :], start=False, stop=True)
                mm(bX[0:R, :], wx, hx, start=True, stop=True).then_inc(S["z"], 1)

            def scores(n, k, q, old):
                hold(pe, S["pturn"], (S["zt"], n + 1))
                if later(n):
                    hold(pe, S["pturn"], (S["ed"], n))
                mm(bS[0:H, :], att[:, :], zt[k][:, :], start=True, stop=True).then_inc(S["s"], 1)

            def factors(n, k, q, old):
                pe.wait_ge(S["ex"], n + 1)
                if later(n):
                    pe.wait_ge(S["sum"], n)
                mm(bF0[0:R, :], sel[:, :], ex[k][:, 0, :], start=True, stop=True)
                mm(bF1[0:R, :], sel[:, :], ex[k][:, 1, :], start=True, stop=True).then_inc(S["b"], 1)

            def results(n, k, q, old):
                hold(pe, S["pturn"], (S["sum"], n + 1), (S["den"], n + 1))
                if later(n):
                    hold(pe, S["pturn"], (S["oE"], n))
                for j in range(J):
                    tr(bO[:, j * R:(j + 1) * R], split(num[k][:, :])[:, :, j], C["ident"][0:R, 0:R])
                if wide:
                    hold(pe, S["pturn"], (S["h"], min(n + 3, NCH) if isinstance(n, int) else n + 3))
                for j in range(J):
                    last = mm(bF2[:, j * H:(j + 1) * H], split(den[k][:, :])[:, :, j], C["ident"][0:H, 0:H],
                              start=True, stop=True)
                last.then_inc(S["o"], 1)
            stages = [(L, project), (L + 1, factors), (L, scores), (L - 1, turn), (L + 1, results)]
            flow(pe, stages, slots=SL)



def weights_block(nc, T, C):
    with ExitStack() as ctx:
        m = Mem(nc, ctx, "we")
        ab = m.sb("ab", [D, 2, P])
        pi = m.sb("pi", [P, 1], I32)
        p5 = m.sb("p5", [P, 1], I32)
        s_ab, s_iota, s_p5, s_pe, s_end = (m.sem(x) for x in "ab iota p5 pe end".split())
        pw = m.ps("pw", [P, P])
        pt = m.ps("pt", [D, D])
        pf = m.ps("pf", [D, 4, P])
        wrow = m.sb("wrow", [1, 2 * P])
        parts = [m.sb(f"part{i}", [1, 2 * P], BF16) for i in range(3)]
        rest = [m.sb(f"rest{i}", [1, 2 * P]) for i in range(2)]
        s_ch, s_parts = m.sem("ch"), m.sem("parts")
        block = ctx.enter_context(nc.Block())

        @block.sync
        def _(sp):
            sp.wait_ge(s_ch, 1 + PART_OPS)
            for l, name in enumerate(("we1p", "we2p")):
                for row in range(9):
                    sp.dma_start(C[name][row:row + 1, :], parts[row // 3][0:1, l * P:(l + 1) * P]).then_inc(s_parts, 16)
            sp.wait_ge(s_parts, 16 * 18)

        @block.gpsimd
        def _(pool):
            nc.gpsimd.iota(pi[:, :], [[1, 1]], base=0, channel_multiplier=1).then_inc(s_iota, 1)

        @block.vector
        def _(dve):
            v = nc.vector
            ch = Chain(dve, s_ch, 1 + PART_OPS)
            ch.at(0)
            v.tensor_copy(wrow[:, 0:P], C["we1"][:, :])
            ch(v.tensor_copy(wrow[:, P:2 * P], C["we2"][:, :]))
            three_parts(nc, ch, wrow, parts, rest)
            for q in range(2):
                last = v.tensor_copy(ab[:, q, :], C["a1"][:, q:q + 1].to_broadcast([D, P]))
            last.then_inc(s_ab, 1)
            dve.wait_ge(s_iota, 1)
            v.tensor_scalar(p5[:, :], pi[:, :], 5, None, ALU.logical_shift_right).then_inc(s_p5, 1)
            dve.wait_ge(s_p5, 1)
            for q in range(4):
                v.tensor_scalar(C["relp"][:, q:q + 1], p5[:, :], float(4 * q), None, ALU.add)
            dve.wait_ge(s_pe, 1)
            v.tensor_copy(C["wb"][:, :], pw[:, :])
            v.tensor_copy(C["w1t"][:, :], pt[:, :])
            v.tensor_copy(C["wft"][:, :, :], pf[:, :, :]).then_inc(s_end, 1)

        @block.tensor
        def _(pe):
            pe.wait_ge(s_ab, 1)
            for q in range(2):
                nc.tensor.matmul(pw[:, q * D:(q + 1) * D], ab[:, q, :], C["w1"][:, :], start=True, stop=True)
            nc.tensor.transpose(pt[:, :], C["w1"][:, :], C["ident"][0:D, 0:D])
            for q in range(4):
                last = nc.tensor.transpose(pf[:, q, :], C["wflat"][:, q, :], C["ident"][:, :])
            last.then_inc(s_pe, 1)



def mlp_block(nc, T, C):
    with ExitStack() as ctx:
        m = Mem(nc, ctx, "m")
        SL = 4
        four, two = range(SL), range(2)
        hr = [m.sb(f"hr{k}", [P, J, D]) for k in four]
        h = [m.sb(f"h{k}", [D + 1, CH]) for k in four]
        g1T = [m.sb(f"g1T{k}", [D + 1, CH]) for k in four]
        bn = m.sb("bn", [P, 2 * J, 6])
        sm = m.sb("sm", [P, 6, 2 * J])
        xn = [[m.sb(f"xn{l}{k}", [P, J, D]) for k in four] for l in two]
        xs = [[m.sb(f"xs{l}{k}", [P, J, D]) for k in four] for l in two]
        g = [[m.sb(f"g{l}{k}", [P, J, D]) for k in four] for l in two]
        d1 = [m.sb(f"d1{k}", [P, J, D]) for k in four]
        pa = [[m.ps(f"pa{l}{b}", [P, J, D]) for b in two] for l in two]
        pt = [m.ps(f"pt{b}", [D, CH]) for b in two]
        ph = [m.ps(f"ph{b}", [D, CH]) for b in two]
        s_hr, s_st = m.sems("hr", SL), m.sems("st", SL)
        s_th, s_h = m.sem("th"), m.sem("h")
        s_mm, s_xn, s_sc, s_g, s_bn = ([m.sem(f"{x}{l}") for l in two] for x in "mm xn sc g bn".split())
        s_t, s_gT, s_d1, s_one, s_pturn, s_f, s_chn = (m.sem(x) for x in "t gT d1 one pturn f chn".split())
        s_chs = [m.sem(f"chs{l}") for l in two]
        block = ctx.enter_context(nc.Block())
        gain = (("lng", "lnb"), ("lrg", "lrb"))

        @block.sync
        def _(sp):
            def load(n, k, q, old):
                if old:
                    sp.wait_ge(s_th, n - SL + 1)
                sp.dma_start(hr[k][:, :, :], rows(T["HR"], n)).then_inc(s_hr[k], 16)
            flow(sp, [(0, load)], slots=SL)

        @block.tensor
        def _(pe):
            pe.wait_ge(s_one, 1)

            def input_turn(n, k, q, old):
                hold(pe, s_pturn, (s_hr[k], 16 * (q + 1)))
                if later(n, 2):
                    hold(pe, s_pturn, (s_h, n - 1))
                for j in range(J):
                    last = nc.tensor.transpose(ph[k % 2][:, j * P:(j + 1) * P], hr[k][:, j, :], C["ident"][:, :])
                last.then_inc(s_th, 1)

            def first(n, k, q, old):
                pe.wait_ge(s_h, n + 1)
                if later(n, 2):
                    pe.wait_ge(s_xn[0], n - 1)
                for j in range(J):
                    last = nc.tensor.matmul(pa[0][k % 2][:, j, :], h[k][:, j * P:(j + 1) * P], C["wca"][:, :],
                                            start=True, stop=True)
                last.then_inc(s_mm[0], 1)

            def turn(n, k, q, old):
                hold(pe, s_pturn, (s_g[0], n + 1))
                if later(n, 2):
                    hold(pe, s_pturn, (s_gT, n - 1))
                for j in range(J):
                    last = nc.tensor.transpose(pt[k % 2][:, j * P:(j + 1) * P], g[0][k][:, j, :], C["ident"][:, :])
                last.then_inc(s_t, 1)

            def second(n, k, q, old):
                pe.wait_ge(s_gT, n + 1)
                if later(n, 2):
                    pe.wait_ge(s_xn[1], n - 1)
                for j in range(J):
                    last = nc.tensor.matmul(pa[1][k % 2][:, j, :], g1T[k][:, j * P:(j + 1) * P], C["wra"][:, :],
                                            start=True, stop=True)
                last.then_inc(s_mm[1], 1)
            flow(pe, [(1, first), (4, turn), (4, second), (0, input_turn)], slots=SL)

        @block.vector
        def _(dve):
            v = nc.vector
            v.memset(bn[:, :, :], 1.0)
            for k in four:
                v.memset(h[k][D:D + 1, :], 1.0)
                last = v.memset(g1T[k][D:D + 1, :], 1.0)
            last.then_inc(s_one, 1)
            dve.wait_ge(s_one, 1)
            chn = Chain(dve, s_chn, LN_OPS)
            gains = [Chain(dve, s_chs[l], 1) for l in two]

            def moments(l):
                def fn(n, k, q, old):
                    dve.wait_ge(s_mm[l], n + 1)
                    row_moments(nc, pa[l][k % 2], bn[:, l * J:(l + 1) * J, :]).then_inc(s_bn[l], 1)
                    dve.wait_ge(s_bn[l], n + 1)
                return fn

            def factors(n, k, q, old):
                chn.at(n)
                whole = not isinstance(n, int)
                if later(n):
                    dve.wait_ge(s_xn[0], n if whole else min(n, NCH))
                if later(n, 4):
                    dve.wait_ge(s_xn[1], n - 3)
                norm_factors(nc, chn, bn, sm, s_f)
                chn.done()

            def scale(l):
                gb, bb = (C[x][:, :].unsqueeze(1).to_broadcast([P, J, D]) for x in gain[l])

                def fn(n, k, q, old):
                    gains[l].at(n)
                    dve.wait_ge(s_xn[l], n + 1)
                    if old:
                        dve.wait_ge(s_g[l], n - SL + 1)
                    gains[l](v.tensor_tensor(xs[l][k][:, :, :], xn[l][k][:, :, :], gb, ALU.mult))
                    v.tensor_tensor(xs[l][k][:, :, :], xs[l][k][:, :, :], bb, ALU.add).then_inc(s_sc[l], 1)
                    gains[l].done()
                return fn

            def add(n, k, q, old):
                dve.wait_ge(s_g[1], n + 1)
                if old:
                    dve.wait_ge(s_st[k], 16 * q)
                v.tensor_tensor(d1[k][:, :, :], g[0][k][:, :, :], g[1][k][:, :, :], ALU.add).then_inc(s_d1, 1)
            flow(dve, [(2, factors, NCH + 3), (3, scale(0)), (6, scale(1)), (7, add), (1, moments(0)), (4, moments(1))],
                 slots=SL)

        @block.scalar
        def _(act):
            f = nc.scalar.activation

            def inputs(n, k, q, old):
                act.wait_ge(s_th, n + 1)
                if old:
                    act.wait_ge(s_mm[0], n - SL + 1)
                f(h[k][0:D, :], ph[k % 2][:, :], ACT.Relu, bias=C["b2"][:, 0:1], scale=0.5).then_inc(s_h, 1)

            def normed(l):
                def fn(n, k, q, old):
                    act.wait_ge(s_f, n + 1 + 3 * l)
                    if old:
                        act.wait_ge(s_sc[l], n - SL + 1)
                    for j in range(J):
                        last = f(xn[l][k][:, j, :], pa[l][k % 2][:, j, :], ACT.Identity,
                                 bias=sm[:, 5, l * J + j:l * J + j + 1], scale=sm[:, 4, l * J + j:l * J + j + 1])
                    last.then_inc(s_xn[l], 1)
                return fn

            def gelu(l):
                def fn(n, k, q, old):
                    act.wait_ge(s_sc[l], n + 1)
                    if old:
                        act.wait_ge(s_d1, n - SL + 1)
                    f(g[l][k][:, :, :], xs[l][k][:, :, :], ACT.Gelu).then_inc(s_g[l], 1)
                return fn

            def turned(n, k, q, old):
                act.wait_ge(s_t, n + 1)
                if old:
                    act.wait_ge(s_mm[1], n - SL + 1)
                f(g1T[k][0:D, :], pt[k % 2][:, :], ACT.Copy).then_inc(s_gT, 1)

            def store(n, k, q, old):
                act.wait_ge(s_d1, n + 1)
                act.dma_start(rows(T["D1"], n), d1[k][:, :, :]).then_inc(s_st[k], 16)
            flow(act, [(4, gelu(0)), (7, gelu(1)), (4, turned), (2, normed(0)), (5, normed(1)), (7, store), (0, inputs)],
                 slots=SL)
            for k in four:
                act.wait_ge(s_st[k], 16 * chunks_of(k, SL))



def logit_block(nc, T, C):
    with ExitStack() as ctx:
        m = Mem(nc, ctx, "l")
        two = range(2)
        ix = [m.sb(f"ix{k}", [P, 2, J], I32) for k in two]
        dg = [m.sb(f"dg{k}", [P, J, 2, D]) for k in two]
        xb = [m.sb(f"xb{k}", [P, J, 2, D]) for k in two]
        xs = [m.sb(f"xs{k}", [P, J, 2, D]) for k in two]
        hn = [m.sb(f"hn{k}", [P, J, 2 * D]) for k in two]
        pr = [m.sb(f"pr{k}", [P, J, 2 * D]) for k in two]
        raw = [m.sb(f"raw{k}", [P, J]) for k in two]
        e = [m.sb(f"e{k}", [P, J]) for k in two]
        bn = m.sb("bn", [P, J * 2, 6])
        sm = m.sb("sm", [P, 6, J * 2])
        s_ix, s_g, s_ld, s_dd, s_hs, s_es = (m.sems(x, 2) for x in "ix g ld dd hs es".split())
        s_xs, s_f, s_hn, s_e, s_ch, s_che, s_turn = (m.sem(x) for x in "xs f hn e ch che turn".split())
        block = ctx.enter_context(nc.Block())
        NG = 16 * 2 * J

        @block.sync
        def _(sp):
            def load(n, k, q, old):
                if old:
                    sp.wait_ge(s_g[k], NG * q)
                sp.dma_start(ix[k][:, 0, :], words(T["PSRC"], n)).then_inc(s_ix[k], 16)
                sp.dma_start(ix[k][:, 1, :], words(T["PDST"], n)).then_inc(s_ix[k], 16)
                if old:
                    sp.wait_ge(s_xs, n - 1)
                sp.dma_start(xb[k][:, :, :, :], rows(T["XSD"], n).rearrange("p j (s d) -> p j s d", s=2)
                             ).then_inc(s_ld[k], 16)
            flow(sp, [(0, load)])

        @block.gpsimd
        def _(pool):
            def gather(n, k, q, old):
                hold(pool, s_turn, (s_ix[k], 32 * (q + 1)))
                if old:
                    hold(pool, s_turn, (s_xs, n - 1), (s_dd[k], 16 * q))
                for i in range(2):
                    for j in range(J):
                        nc.gpsimd.indirect_dma_start(
                            dg[k][:, j, i, :], None, T["D1"],
                            bass.IndirectOffsetOnAxis(ap=ix[k][:, i, j:j + 1], axis=0)).then_inc(s_g[k], 16)
            flow(pool, [(0, gather)])

        @block.vector
        def _(dve):
            v = nc.vector
            ch, che = Chain(dve, s_ch, 1 + LN_OPS), Chain(dve, s_che, 2)
            wb = C["wb"][:, :].unsqueeze(1).to_broadcast([P, J, 2 * D])

            def norm(n, k, q, old):
                ch.at(n)
                dve.wait_ge(s_g[k], NG * (q + 1))
                dve.wait_ge(s_ld[k], 16 * (q + 1))
                if old:
                    dve.wait_ge(s_hn, n - 1)
                v.tensor_tensor(xs[k][:, :, :, :], dg[k][:, :, :, :], xb[k][:, :, :, :], ALU.add).then_inc(s_xs, 1)
                dve.wait_ge(s_xs, n + 1)
                ch(row_moments(nc, xs[k][:, :, :, :].rearrange("p j s d -> p (j s) d"), bn))
                if later(n):
                    dve.wait_ge(s_hn, n)
                norm_factors(nc, ch, bn, sm, s_f)
                ch.done()

            def logits(n, k, q, old):
                che.at(n)
                dve.wait_ge(s_hn, n + 1)
                che(v.tensor_tensor(pr[k][:, :, :], hn[k][:, :, :], wb, ALU.mult))
                che(v.tensor_reduce(raw[k][:, :], pr[k][:, :, :], X, ALU.add))
                if old:
                    dve.wait_ge(s_es[k], 16 * q)
                v.scalar_tensor_tensor(e[k][:, :], raw[k][:, :], SLOPE, raw[k][:, :], ALU.mult, ALU.max).then_inc(s_e, 1)
                che.done()
            flow(dve, [(3, logits), (1, norm)])

        @block.scalar
        def _(act):
            def dst_rows(n, k, q, old):
                act.wait_ge(s_g[k], NG * (q + 1))
                act.dma_start(rows(T["D1D"], n), dg[k][:, :, 1, :]).then_inc(s_dd[k], 16)

            def normed(n, k, q, old):
                act.wait_ge(s_f, n + 1)
                if old:
                    act.wait_ge(s_hs[k], 16 * q)
                    act.wait_ge(s_e, n - 1)
                for g in range(2 * J):
                    last = nc.scalar.activation(hn[k][:, g // 2, (g % 2) * D:(g % 2 + 1) * D], xs[k][:, g // 2, g % 2, :],
                                                ACT.Relu, bias=sm[:, 5, g:g + 1], scale=sm[:, 4, g:g + 1])
                last.then_inc(s_hn, 1)
                act.wait_ge(s_hn, n + 1)
                act.dma_start(rows(T["HS"], n), hn[k][:, :, 0:D]).then_inc(s_hs[k], 16)

            def store(n, k, q, old):
                act.wait_ge(s_e, n + 1)
                act.dma_start(words(T["EL"], n), e[k][:, :]).then_inc(s_es[k], 16)
            flow(act, [(1, dst_rows), (3, store), (1, normed)])
            for k in two:
                for s in (s_dd, s_hs, s_es):
                    act.wait_ge(s[k], 16 * (NCH // 2))


def permute_block(nc, T, tag, gather):
    with ExitStack() as ctx:
        m = Mem(nc, ctx, tag)
        SL = 4
        ix = [m.sb(f"ix{k}", [P, J], I32) for k in range(SL)]
        val = [m.sb(f"val{k}", [P, J]) for k in range(SL)]
        s_ix, s_g, s_st = (m.sems(x, SL) for x in "ix g st".split())
        s_turn = m.sem("turn")
        block = ctx.enter_context(nc.Block())
        el, al = T["EL"].unsqueeze(1), T["AL"].unsqueeze(1)

        @block.sync
        def _(sp):
            def load(n, k, q, old):
                if old:
                    sp.wait_ge(s_g[k], 16 * J * q)
                sp.dma_start(ix[k][:, :], words(T["EID"], n)).then_inc(s_ix[k], 16)
                if not gather:
                    sp.dma_start(val[k][:, :], words(T["SA"], n)).then_inc(s_ix[k], 16)
            flow(sp, [(0, load)], slots=SL)

        @block.gpsimd
        def _(pool):
            def move(n, k, q, old):
                hold(pool, s_turn, (s_ix[k], (16 if gather else 32) * (q + 1)))
                if gather and old:
                    hold(pool, s_turn, (s_st[k], 16 * q))
                for j in range(J):
                    at = bass.IndirectOffsetOnAxis(ap=ix[k][:, j:j + 1], axis=0)
                    if gather:
                        nc.gpsimd.indirect_dma_start(val[k][:, j:j + 1], None, el, at).then_inc(s_g[k], 16)
                    else:
                        nc.gpsimd.indirect_dma_start(al, at, val[k][:, j:j + 1], None).then_inc(s_g[k], 16)
            flow(pool, [(0, move)], slots=SL)
            for k in range(SL):
                pool.wait_ge(s_g[k], 16 * J * chunks_of(k, SL))

        if gather:
            @block.scalar
            def _(act):
                def store(n, k, q, old):
                    act.wait_ge(s_g[k], 16 * J * (q + 1))
                    act.dma_start(words(T["SE"], n), val[k][:, :]).then_inc(s_st[k], 16)
                flow(act, [(0, store)], slots=SL)
                for k in range(SL):
                    act.wait_ge(s_st[k], 16 * chunks_of(k, SL))


def softmax_block(nc, T, C):
    with ExitStack() as ctx:
        m = Mem(nc, ctx, "sx")
        full = lambda t: t.rearrange("(p f) -> p f", f=EF)
        names = "se kp kc kn first last nfirst nlast r mx ex den a b al"
        B = {x: m.sb(x, [P, EF]) for x in names.split()}
        col = m.sb("col", [P, 2])
        row = m.sb("row", [1, 2, P])
        carry = m.sb("carry", [1, P + 2])
        cin = m.sb("cin", [P, 1])
        prow = m.ps("prow", [1, 2, P])
        pcol = m.ps("pcol", [P, 1])
        s_ld, s_st, s_ch, s_pe, s_up, s_ex, s_exd = (m.sem(x) for x in "ld st ch pe up ex exd".split())
        block = ctx.enter_context(nc.Block())

        @block.sync
        def _(sp):
            for t, src in ((B["se"], T["SE"]), (B["kp"], T["SSRC"][0:EP]), (B["kc"], T["SSRC"][1:EP + 1]),
                           (B["kn"], T["SSRC"][2:EP + 2])):
                sp.dma_start(t[:, :], full(src)).then_inc(s_ld, 16)
            sp.wait_ge(s_st, 1)
            sp.dma_start(full(T["SA"]), B["al"][:, :]).then_inc(s_ld, 16)
            sp.wait_ge(s_ld, 16 * 5)

        @block.tensor
        def _(pe):
            for n in range(4):
                pe.wait_ge(s_up, 2 * n + 1)
                for q in range(2):
                    last = nc.tensor.transpose(prow[:, q, :], col[:, q:q + 1], C["ident"][:, :])
                last.then_inc(s_pe, 1)
                pe.wait_ge(s_up, 2 * n + 2)
                lo = 0 if n % 2 == 0 else 2
                nc.tensor.transpose(pcol[:, :], carry[:, lo:lo + P], C["ident"][0:1, 0:1]).then_inc(s_pe, 1)

        @block.scalar
        def _(act):
            act.wait_ge(s_ex, 1)
            nc.scalar.activation(B["ex"][:, :], B["b"][:, :], ACT.Exp).then_inc(s_exd, 1)

        @block.vector
        def _(dve):
            v = nc.vector
            ch = Chain(dve, s_ch, 0)
            ch.at(0)
            dve.wait_ge(s_ld, 64)
            v.tensor_tensor(B["nfirst"][:, :], B["kp"][:, :], B["kc"][:, :], ALU.is_equal)
            ch(v.tensor_tensor(B["nlast"][:, :], B["kn"][:, :], B["kc"][:, :], ALU.is_equal))
            v.tensor_scalar(B["first"][:, :], B["nfirst"][:, :], -1.0, BIG, ALU.add, ALU.mult)
            ch(v.tensor_scalar(B["last"][:, :], B["nlast"][:, :], -1.0, BIG, ALU.add, ALU.mult))
            passes = [0]

            def scan(out, d0, d1, op0, op1, empty, back):
                n = passes[0]
                passes[0] += 1
                rev = (lambda t: t[:, ::-1]) if back else (lambda t: t[:, :])
                edge = slice(0, 1) if back else slice(EF - 1, EF)
                ch(v.tensor_tensor_scan(rev(out), rev(d0), rev(d1), empty, op0, op1))
                v.tensor_copy(col[:, 0:1], out[:, edge])
                v.tensor_reduce(col[:, 1:2], d0[:, :], X, ALU.add if op0 == ALU.add else ALU.min).then_inc(s_up, 1)
                dve.wait_ge(s_pe, 2 * n + 1)
                v.memset(carry[:, :], empty)
                ch(v.tensor_copy(row[:, :, :], prow[:, :, :]))
                body, st, gate = carry[:, 1:P + 1], row[:, 0, :], row[:, 1, :]
                if back:
                    body, st, gate = body[:, ::-1], st[:, ::-1], gate[:, ::-1]
                v.tensor_tensor_scan(body, gate, st, empty, op0, op1).then_inc(s_up, 1)
                dve.wait_ge(s_pe, 2 * n + 2)
                ch(v.tensor_copy(cin[:, :], pcol[:, :]))
                ch(v.tensor_tensor_scan(rev(out), rev(d0), rev(d1), cin[:, 0:1], op0, op1))

            scan(B["r"], B["first"], B["se"], ALU.add, ALU.max, -BIG, False)
            scan(B["mx"], B["last"], B["r"], ALU.add, ALU.max, -BIG, True)
            v.tensor_tensor(B["b"][:, :], B["se"][:, :], B["mx"][:, :], ALU.subtract).then_inc(s_ex, 1)
            dve.wait_ge(s_exd, 1)
            scan(B["r"], B["nfirst"], B["ex"], ALU.mult, ALU.add, 0.0, False)
            ch(v.tensor_tensor(B["a"][:, :], B["r"][:, :], B["nlast"][:, :], ALU.mult))
            ch(v.tensor_tensor(B["a"][:, :], B["r"][:, :], B["a"][:, :], ALU.subtract))
            scan(B["den"], B["nlast"], B["a"], ALU.mult, ALU.add, 0.0, True)
            ch(v.tensor_scalar(B["den"][:, :], B["den"][:, :], 1.0, None, ALU.max))
            ch(v.reciprocal(B["b"][:, :], B["den"][:, :]))
            v.tensor_tensor(B["al"][:, :], B["ex"][:, :], B["b"][:, :], ALU.mult).then_inc(s_st, 1)



def mix_block(nc, T, C):
    with ExitStack() as ctx:
        m = Mem(nc, ctx, "e")
        SL = 4
        four = range(SL)
        hs = [m.sb(f"hs{k}", [P, J, D]) for k in four]
        al = [m.sb(f"al{k}", [P, J]) for k in four]
        kp = [m.sb(f"kp{k}", [D, CH]) for k in four]
        dd = [m.sb(f"dd{k}", [P, J, D]) for k in four]
        mg = [m.sb(f"mg{k}", [P, J, D]) for k in four]
        ag = [m.sb(f"ag{k}", [D, CH]) for k in four]
        ng = [m.sb(f"ng{k}", [P, J, D]) for k in four]
        ex = [m.sb(f"ex{k}", [P, J, D]) for k in four]
        t = [m.sb(f"t{k}", [P, J, D]) for k in four]
        o = [m.sb(f"o{k}", [P, J, D]) for k in four]
        pt = [m.ps(f"pt{b}", [D, CH]) for b in range(2)]
        pw = [m.ps(f"pw{k}", [P, J, D]) for k in four]
        s_ld, s_st = m.sems("ld", SL), m.sems("st", SL)
        s_mg, s_t, s_ag, s_w, s_ng, s_ex, s_o, s_ch, s_clear, s_pturn = (
            m.sem(x) for x in "mg t ag w ng ex o ch clear pturn".split())
        block = ctx.enter_context(nc.Block())
        split = lambda t: t.rearrange("r (p j) -> r p j", j=J)

        @block.sync
        def _(sp):
            def load(n, k, q, old):
                if old:
                    sp.wait_ge(s_o, n - SL + 1)
                for dst, src in ((hs[k][:, :, :], rows(T["HS"], n)), (al[k][:, :], words(T["AL"], n)),
                                 (kp[k][:, :], line(T["KEEP"], n, D)), (dd[k][:, :, :], rows(T["D1D"], n))):
                    sp.dma_start(dst, src).then_inc(s_ld[k], 16)
            flow(sp, [(0, load)], slots=SL)

        @block.vector
        def _(dve):
            v = nc.vector
            ch = Chain(dve, s_ch, 1)
            for k in four:
                last = v.memset(ag[k][:, :], 0.0)
            last.then_inc(s_clear, 1)
            dve.wait_ge(s_clear, 1)

            def product(n, k, q, old):
                dve.wait_ge(s_ld[k], 64 * (q + 1))
                if old:
                    dve.wait_ge(s_t, n - SL + 1)
                v.tensor_tensor(mg[k][:, :, :], hs[k][:, :, :], bcast(al[k][:, :], D), ALU.mult).then_inc(s_mg, 1)

            def sums(n, k, q, old):
                dve.wait_ge(s_t, n + 1)
                if later(n):
                    dve.wait_ge(s_ag, n)
                if old:
                    dve.wait_ge(s_w, n - SL + 1)
                v.tensor_tensor_scan(ag[k][:, :], kp[k][:, :], pt[k % 2][:, :], ag[(k - 1) % SL][:, CH - 1:CH],
                                     ALU.mult, ALU.add).then_inc(s_ag, 1)

            def negative(n, k, q, old):
                dve.wait_ge(s_w, n + 1)
                v.tensor_scalar(ng[k][:, :, :], pw[k][:, :, :], 0.0, None, ALU.min).then_inc(s_ng, 1)

            def result(n, k, q, old):
                ch.at(n)
                dve.wait_ge(s_ex, n + 1)
                ch(v.scalar_tensor_tensor(t[k][:, :, :], pw[k][:, :, :], 0.0, ex[k][:, :, :], ALU.max, ALU.add))
                if old:
                    dve.wait_ge(s_st[k], 16 * q)
                v.scalar_tensor_tensor(o[k][:, :, :], t[k][:, :, :], -1.0, dd[k][:, :, :], ALU.add, ALU.add
                                       ).then_inc(s_o, 1)
                ch.done()
            flow(dve, [(4, result), (2, sums), (1, product), (3, negative)], slots=SL)

        @block.tensor
        def _(pe):
            def turn(n, k, q, old):
                hold(pe, s_pturn, (s_mg, n + 1))
                if later(n, 2):
                    hold(pe, s_pturn, (s_ag, n - 1))
                for j in range(J):
                    last = nc.tensor.transpose(split(pt[k % 2][:, :])[:, :, j], mg[k][:, j, :], C["ident"][:, :])
                last.then_inc(s_t, 1)

            def project(n, k, q, old):
                pe.wait_ge(s_ag, n + 1)
                if old:
                    pe.wait_ge(s_o, n - SL + 1)
                for j in range(J):
                    last = nc.tensor.matmul(pw[k][:, j, :], split(ag[k][:, :])[:, :, j], C["w1t"][:, :],
                                            start=True, stop=True)
                last.then_inc(s_w, 1)
            flow(pe, [(1, turn), (2, project)], slots=SL)

        @block.scalar
        def _(act):
            def exponents(n, k, q, old):
                act.wait_ge(s_ng, n + 1)
                nc.scalar.activation(ex[k][:, :, :], ng[k][:, :, :], ACT.Exp).then_inc(s_ex, 1)

            def store(n, k, q, old):
                act.wait_ge(s_o, n + 1)
                act.dma_start(rows(T["D2"], n), o[k][:, :, :]).then_inc(s_st[k], 16)
            flow(act, [(4, store), (3, exponents)], slots=SL)
            for k in four:
                act.wait_ge(s_st[k], 16 * chunks_of(k, SL))
            act.dma_start(T["D2"][SENT:SENT + 1, :], T["D1"][SENT:SENT + 1, :]).then_inc(s_st[0], 16)
            act.wait_ge(s_st[0], 16 * chunks_of(0, SL) + 16)


def relation_block(nc, T, C):
    with ExitStack() as ctx:
        m = Mem(nc, ctx, "f")
        two = range(2)
        ix = [m.sb(f"ix{k}", [P, J], I32) for k in two]
        dg = [m.sb(f"dg{k}", [P, J, D]) for k in two]
        xb = [m.sb(f"xb{k}", [P, J, D]) for k in two]
        xs = [m.sb(f"xs{k}", [P, J, D]) for k in two]
        hn = [m.sb(f"hn{k}", [P, J, D]) for k in two]
        hT = [m.sb(f"hT{k}", [D, CH]) for k in two]
        rl = [m.sb(f"rl{k}", [P, CH]) for k in two]
        kp = [m.sb(f"kp{k}", [D, CH]) for k in two]
        d2 = [m.sb(f"d2{k}", [P, J, D]) for k in two]
        d2b = [m.sb(f"d2b{k}", [P, J, D]) for k in two]
        sel = [[m.sb(f"sel{k}{g}", [P, CH]) for g in range(4)] for k in two]
        ag = [m.sb(f"ag{k}", [D, CH]) for k in two]
        o = [m.sb(f"o{k}", [P, J, D]) for k in two]
        srow = m.sb("srow", [1, D])
        bn = m.sb("bn", [P, J, 6])
        sm = m.sb("sm", [P, 6, J])
        b_turn = m.ps("turn", [P, CH])
        b_v = [m.ps(f"v{g}", [P, CH]) for g in range(4)]
        b_m = [m.ps(f"m{k}", [P, CH]) for k in two]
        b_back = m.ps("back", [P, CH])
        s_ix, s_g, s_xb, s_rl, s_kp, s_d2, s_st = (m.sems(x, 2) for x in "ix g xb rl kp d2 st".split())
        s_xs, s_f, s_hn, s_t, s_h, s_v, s_sel, s_m, s_ag, s_b, s_o, s_ch, s_cho, s_turn, s_end, s_pturn = (
            m.sem(x) for x in "xs f hn t h v sel m ag b o ch cho turn end pturn".split())
        block = ctx.enter_context(nc.Block())
        split = lambda t: t.rearrange("r (p j) -> r p j", j=J)

        @block.sync
        def _(sp):
            def load(n, k, q, old):
                if old:
                    sp.wait_ge(s_g[k], 16 * J * q)
                sp.dma_start(ix[k][:, :], words(T["PSRC"], n)).then_inc(s_ix[k], 16)
                if old:
                    sp.wait_ge(s_xs, n - 1)
                sp.dma_start(xb[k][:, :, :], rows(T["XSD"], n)[:, :, 0:D]).then_inc(s_xb[k], 16)

            def relations(n, k, q, old):
                if old:
                    sp.wait_ge(s_sel, 4 * (n - 1))
                sp.dma_start(rl[k][:, :], line(T["REL"], n, P)).then_inc(s_rl[k], 16)

            def keeps(n, k, q, old):
                if old:
                    sp.wait_ge(s_ag, n - 1)
                sp.dma_start(kp[k][:, :], line(T["KEEP"], n, D)).then_inc(s_kp[k], 16)

            def before(n, k, q, old):
                if old:
                    sp.wait_ge(s_o, n - 1)
                sp.dma_start(d2[k][:, :, :], rows(T["D2"], n)).then_inc(s_d2[k], 16)
            flow(sp, [(0, load), (4, before), (3, keeps), (1, relations)])

        @block.gpsimd
        def _(pool):
            def gather(n, k, q, old):
                hold(pool, s_turn, (s_ix[k], 16 * (q + 1)))
                if old:
                    hold(pool, s_turn, (s_xs, n - 1))
                for j in range(J):
                    nc.gpsimd.indirect_dma_start(
                        dg[k][:, j, :], None, T["D2"],
                        bass.IndirectOffsetOnAxis(ap=ix[k][:, j:j + 1], axis=0)).then_inc(s_g[k], 16)
            flow(pool, [(0, gather)])

        @block.vector
        def _(dve):
            v = nc.vector
            for k in two:
                last = v.memset(ag[k][:, :], 0.0)
            last.then_inc(s_end, 1)
            dve.wait_ge(s_end, 1)
            ch, cho = Chain(dve, s_ch, 1 + LN_OPS), Chain(dve, s_cho, 1)
            b2 = C["bias2"][:, :].unsqueeze(1).to_broadcast([P, J, D])

            def norm(n, k, q, old):
                ch.at(n)
                dve.wait_ge(s_g[k], 16 * J * (q + 1))
                dve.wait_ge(s_xb[k], 16 * (q + 1))
                if old:
                    dve.wait_ge(s_hn, n - 1)
                v.tensor_tensor(xs[k][:, :, :], dg[k][:, :, :], xb[k][:, :, :], ALU.add).then_inc(s_xs, 1)
                dve.wait_ge(s_xs, n + 1)
                ch(row_moments(nc, xs[k], bn))
                if later(n):
                    dve.wait_ge(s_hn, n)
                norm_factors(nc, ch, bn, sm, s_f)
                ch.done()

            def select(n, k, q, old):
                dve.wait_ge(s_rl[k], 16 * (q + 1))
                if old:
                    dve.wait_ge(s_m, n - 1)
                for g in range(4):
                    dve.wait_ge(s_v, n * 4 + g + 1)
                    v.scalar_tensor_tensor(sel[k][g][:, :], rl[k][:, :], C["relp"][:, g:g + 1], b_v[g][:, :],
                                           ALU.is_equal, ALU.mult).then_inc(s_sel, 1)

            def sums(n, k, q, old):
                dve.wait_ge(s_m, n + 1)
                dve.wait_ge(s_kp[k], 16 * (q + 1))
                if later(n):
                    dve.wait_ge(s_ag, n)
                if old:
                    dve.wait_ge(s_b, n - 1)
                v.tensor_tensor_scan(ag[k][:, :], kp[k][:, :], b_m[k][0:D, :], ag[1 - k][:, CH - 1:CH],
                                     ALU.mult, ALU.add).then_inc(s_ag, 1)

            def result(n, k, q, old):
                cho.at(n)
                dve.wait_ge(s_d2[k], 16 * (q + 1))
                cho(v.tensor_tensor(d2b[k][:, :, :], d2[k][:, :, :], b2, ALU.add))
                dve.wait_ge(s_b, n + 1)
                if old:
                    dve.wait_ge(s_st[k], 16 * q)
                v.tensor_tensor(o[k][:, :, :], d2b[k][:, :, :],
                                b_back[:, 0:J * D].rearrange("p (j d) -> p j d", j=J), ALU.add).then_inc(s_o, 1)
                cho.done()
            flow(dve, [(5, result), (4, sums), (1, norm), (2, select)])

        @block.tensor
        def _(pe):
            def turn(n, k, q, old):
                hold(pe, s_pturn, (s_hn, n + 1))
                if later(n):
                    hold(pe, s_pturn, (s_h, n))
                for j in range(J):
                    last = nc.tensor.transpose(split(b_turn[0:D, :])[:, :, j], hn[k][:, j, :], C["ident"][:, :])
                last.then_inc(s_t, 1)

            def vectors(n, k, q, old):
                pe.wait_ge(s_h, n + 1)
                for g in range(4):
                    if later(n):
                        pe.wait_ge(s_sel, n * 4 + (g - 3))
                    nc.tensor.matmul(b_v[g][:, :], C["wft"][:, g, :], hT[k][:, :], start=True, stop=True).then_inc(s_v, 1)

            def compose(n, k, q, old):
                if old:
                    pe.wait_ge(s_ag, n - 1)
                for g in range(4):
                    pe.wait_ge(s_sel, n * 4 + g + 1)
                    last = nc.tensor.matmul(b_m[k][0:D, :], C["cstk"][:, :], sel[k][g][:, :],
                                            start=(g == 0), stop=(g == 3))
                last.then_inc(s_m, 1)

            def turn_back(n, k, q, old):
                hold(pe, s_pturn, (s_ag, n + 1))
                if later(n):
                    hold(pe, s_pturn, (s_o, n))
                for j in range(J):
                    last = nc.tensor.transpose(b_back[:, j * D:(j + 1) * D], split(ag[k][:, :])[:, :, j],
                                               C["ident"][0:D, 0:D])
                last.then_inc(s_b, 1)
            flow(pe, [(2, turn), (3, compose), (2, vectors), (4, turn_back)])

        @block.scalar
        def _(act):
            f = nc.scalar.activation

            def normed(n, k, q, old):
                act.wait_ge(s_f, n + 1)
                if old:
                    act.wait_ge(s_t, n - 1)
                for j in range(J):
                    last = f(hn[k][:, j, :], xs[k][:, j, :], ACT.Relu, bias=sm[:, 5, j:j + 1], scale=sm[:, 4, j:j + 1])
                last.then_inc(s_hn, 1)

            def turned(n, k, q, old):
                act.wait_ge(s_t, n + 1)
                if old:
                    act.wait_ge(s_v, 4 * (n - 1))
                f(hT[k][:, :], b_turn[0:D, :], ACT.Copy).then_inc(s_h, 1)

            def store(n, k, q, old):
                act.wait_ge(s_o, n + 1)
                act.dma_start(rows(T["D3"], n), o[k][:, :, :]).then_inc(s_st[k], 16)
            flow(act, [(2, turned), (1, normed), (5, store)])
            for k in two:
                act.wait_ge(s_st[k], 16 * (NCH // 2))
            act.dma_start(srow[:, :], T["D2"][SENT:SENT + 1, :]).then_inc(s_st[0], 16)
            act.wait_ge(s_st[0], 16 * (NCH // 2) + 16)
            f(C["c3row"][:, :], srow[:, :], ACT.Copy).then_inc(s_end, 1)
            act.wait_ge(s_end, 2)

    with ExitStack() as ctx:
        m = Mem(nc, ctx, "fs")
        s_a, s_d = m.sem("a"), m.sem("d")
        block = ctx.enter_context(nc.Block())

        @block.vector
        def _(dve):
            nc.vector.tensor_tensor(C["c3row"][:, :], C["c3row"][:, :], C["bias2"][0:1, :], ALU.add).then_inc(s_a, 1)

        @block.sync
        def _(sp):
            sp.wait_ge(s_a, 1)
            sp.dma_start(T["D3"][SENT:SENT + 1, :], C["c3row"][:, :]).then_inc(s_d, 16)
            sp.wait_ge(s_d, 16)
            sp.dma_start(C["c3"][:, :], T["D3"][SENT].unsqueeze(0).partition_broadcast(P)).then_inc(s_d, 16)
            sp.wait_ge(s_d, 32)



def batch_block(nc, T, C):
    F = 56
    NC = EF // F
    with ExitStack() as ctx:
        m = Mem(nc, ctx, "bn")
        em = m.sb("em", [P, EF])
        ag = [m.sb(f"ag{i}", [P, F, D]) for i in range(2)]
        q = [m.sb(f"q{i}", [P, F, D]) for i in range(2)]
        sq = [m.sb(f"sq{i}", [P, F, D]) for i in range(2)]
        part = m.sb("part", [P, 2, NC, D])
        tot = m.sb("tot", [P, 2, D])
        t = m.sb("t", [P, 6, D])
        ps = m.ps("ps", [P, 2 * D])
        s_em, s_q, s_sq, s_r, s_ch, s_pe = (m.sem(x) for x in "em q sq r ch pe".split())
        s_ld = m.sems("ld", 2)
        block = ctx.enter_context(nc.Block())
        ag_v = T["AG"].rearrange("(p f) d -> p f d", f=EF)

        @block.sync
        def _(sp):
            sp.dma_start(em[:, :], T["ENDM"].rearrange("(p f) -> p f", f=EF)).then_inc(s_em, 16)
            for c in range(NC):
                if c >= 2:
                    sp.wait_ge(s_q, c - 1)
                sp.dma_start(ag[c % 2][:, :, :], ag_v[:, c * F:(c + 1) * F, :]).then_inc(s_ld[c % 2], 16)

        @block.scalar
        def _(act):
            for c in range(NC):
                act.wait_ge(s_q, c + 1)
                if c >= 2:
                    act.wait_ge(s_r, c - 1)
                nc.scalar.activation(sq[c % 2][:, :, :], q[c % 2][:, :, :], ACT.Square).then_inc(s_sq, 1)

        @block.tensor
        def _(pe):
            pe.wait_ge(s_r, NC + 1)
            nc.tensor.matmul(ps[:, :], C["ones_sq"][:, :], tot[:, :, :].rearrange("p s d -> p (s d)"),
                             start=True, stop=True).then_inc(s_pe, 1)

        @block.vector
        def _(dve):
            v = nc.vector
            ch = Chain(dve, s_ch, 0)
            ch.at(0)
            dve.wait_ge(s_em, 16)
            by_d = lambda x: x.rearrange("p f d -> p d f")

            def squares(c):
                dve.wait_ge(s_sq, c + 1)
                v.tensor_reduce(part[:, 1, c, :], by_d(sq[c % 2][:, :, :]), X, ALU.add).then_inc(s_r, 1)

            for c in range(NC):
                dve.wait_ge(s_ld[c % 2], 16 * (c // 2 + 1))
                if c >= 2:
                    dve.wait_ge(s_sq, c - 1)
                v.tensor_tensor(q[c % 2][:, :, :], ag[c % 2][:, :, :], bcast(em[:, c * F:(c + 1) * F], D), ALU.mult
                                ).then_inc(s_q, 1)
                dve.wait_ge(s_q, c + 1)
                ch(v.tensor_reduce(part[:, 0, c, :], by_d(q[c % 2][:, :, :]), X, ALU.add))
                if c >= 1:
                    squares(c - 1)
            squares(NC - 1)
            dve.wait_ge(s_r, NC)
            v.tensor_reduce(tot[:, :, :], part[:, :, :, :].rearrange("p s c d -> p s d c"), X, ALU.add).then_inc(s_r, 1)
            dve.wait_ge(s_pe, 1)
            mean, ex2, var, y, t1, t2 = (t[:, i, :] for i in range(6))
            v.tensor_scalar(mean, ps[:, 0:D], 1.0 / N, None, ALU.mult)
            ch(v.tensor_scalar(ex2, ps[:, D:2 * D], 1.0 / N, EPS, ALU.mult, ALU.add))
            ch(v.tensor_tensor(t1, mean, mean, ALU.mult))
            ch(v.tensor_tensor(var, ex2, t1, ALU.subtract))
            ch(v.tensor_scalar(t1.bitcast(I32), var.bitcast(I32), 1, None, ALU.logical_shift_right))
            ch(v.tensor_scalar(y.bitcast(I32), t1.bitcast(I32), -1.0, RSQRT_SEED, ALU.mult, ALU.add))
            for _ in range(4):
                ch(v.tensor_tensor(t1, y, y, ALU.mult))
                ch(v.scalar_tensor_tensor(t2, t1, -0.5, var, ALU.mult, ALU.mult))
                ch(v.scalar_tensor_tensor(y, t2, 1.5, y, ALU.add, ALU.mult))
            ch(v.tensor_tensor(C["k1"][:, :], y, C["gamma"][:, :], ALU.mult))
            ch(v.tensor_tensor(t1, mean, C["bias3"][:, :], ALU.add))
            ch(v.tensor_tensor(t2, C["bias3"][:, :], t1, ALU.subtract))
            ch(v.tensor_tensor(t1, t2, C["k1"][:, :], ALU.mult))
            ch(v.tensor_tensor(C["k0"][:, :], t1, C["beta"][:, :], ALU.add))


def nodes_block(nc, a, out, C):
    G = 20
    NR = P * G
    NF = N // NR
    PT = (N - NF * NR) // G
    SL = 3
    assert NF % SL == 0 and (NF * P + PT) * G == N
    with ExitStack() as ctx:
        m = Mem(nc, ctx, "n")
        x, x3, h, t, gl, y = ([m.sb(f"{name}{k}", [P, G, D]) for k in range(SL)] for name in "x x3 h t gl y".split())
        bn = m.sb("bn", [P, G, 6])
        sm = m.sb("sm", [P, 6, G])
        s_ld, s_st = m.sems("ld", SL), m.sems("st", SL)
        s_x3, s_f, s_h, s_t, s_gl, s_y, s_ch = (m.sem(q) for q in "x3 f h t gl y ch".split())
        block = ctx.enter_context(nc.Block())
        parts = lambda n: PT if isinstance(n, int) and n == NF else P

        def rows_of(dram, n):
            return dram[bass.ds(n * NR, parts(n) * G), :].rearrange("(p g) d -> p g d", g=G)

        def every(eng, stages):
            flow(eng, stages, total=NF + 1, slots=SL)

        bc = lambda w, np_: C[w][0:np_, :].unsqueeze(1).to_broadcast([np_, G, D])

        @block.sync
        def _(sp):
            def load(n, k, q, old):
                if old:
                    sp.wait_ge(s_x3, n - SL + 1)
                sp.dma_start(x[k][0:parts(n), :, :], rows_of(a["x"], n)).then_inc(s_ld[k], 16)
            every(sp, [(0, load)])

        @block.gpsimd
        def _(pool):
            def shift(n, k, q, old):
                np_ = parts(n)
                pool.wait_ge(s_ld[k], 16 * (q + 1))
                if old:
                    pool.wait_ge(s_y, n - SL + 1)
                nc.gpsimd.tensor_tensor(x3[k][0:np_, :, :], x[k][0:np_, :, :], bc("c3", np_), ALU.add).then_inc(s_x3, 1)
            every(pool, [(1, shift)])

        @block.vector
        def _(dve):
            v = nc.vector
            ch = Chain(dve, s_ch, 1 + LN_OPS)

            def norm(n, k, q, old):
                np_ = parts(n)
                ch.at(n)
                dve.wait_ge(s_x3, n + 1)
                ch(row_moments(nc, x3[k][0:np_, :, :], bn[0:np_, :, :]))
                if later(n):
                    dve.wait_ge(s_h, n)
                norm_factors(nc, ch, bn[0:np_, :, :], sm[0:np_, :, :], s_f)
                ch.done()

            def batch(n, k, q, old):
                np_ = parts(n)
                dve.wait_ge(s_h, n + 1)
                if old:
                    dve.wait_ge(s_gl, n - SL + 1)
                v.tensor_tensor(t[k][0:np_, :, :], h[k][0:np_, :, :], bc("k0", np_), ALU.add).then_inc(s_t, 1)

            def result(n, k, q, old):
                np_ = parts(n)
                dve.wait_ge(s_gl, n + 1)
                if old:
                    dve.wait_ge(s_st[k], 16 * q)
                v.tensor_tensor(y[k][0:np_, :, :], gl[k][0:np_, :, :], x3[k][0:np_, :, :], ALU.add).then_inc(s_y, 1)
            every(dve, [(4, result), (3, batch), (1, norm)])

        @block.scalar
        def _(act):
            f = nc.scalar.activation

            def normed(n, k, q, old):
                np_ = parts(n)
                act.wait_ge(s_f, n + 1)
                if old:
                    act.wait_ge(s_t, n - SL + 1)
                for g in range(G):
                    last = f(h[k][0:np_, g, :], x3[k][0:np_, g, :], ACT.Relu,
                             bias=sm[0:np_, 5, g:g + 1], scale=sm[0:np_, 4, g:g + 1])
                last.then_inc(s_h, 1)

            def gelu(n, k, q, old):
                np_ = parts(n)
                act.wait_ge(s_t, n + 1)
                if old:
                    act.wait_ge(s_y, n - SL + 1)
                f(gl[k][0:np_, :, :], t[k][0:np_, :, :], ACT.Gelu).then_inc(s_gl, 1)

            def store(n, k, q, old):
                np_ = parts(n)
                act.wait_ge(s_y, n + 1)
                act.dma_start(rows_of(out, n), y[k][0:np_, :, :]).then_inc(s_st[k], 16)
            every(act, [(2, normed), (3, gelu), (4, store)])
            for k in range(SL):
                act.wait_ge(s_st[k], 16 * chunks_of(k, SL, NF + 1))


def targets_block(nc, T, out, C):
    with ExitStack() as ctx:
        m = Mem(nc, ctx, "o")
        SL = 4
        four = range(SL)
        ix = [m.sb(f"ix{k}", [P, J], I32) for k in four]
        ag, h, x3, t1, t2, t3, gl, y = ([m.sb(f"{n}{k}", [P, J, D]) for k in four] for n in
                                        "ag h x3 t1 t2 t3 gl y".split())
        s_ld, s_sc = m.sems("ld", SL), m.sems("sc", SL)
        s_t, s_gl, s_y, s_ch, s_turn, s_spturn = (m.sem(q) for q in "t gl y ch turn spturn".split())
        block = ctx.enter_context(nc.Block())

        @block.sync
        def _(sp):
            def load(n, k, q, old):
                if old:
                    hold(sp, s_spturn, (s_y, n - SL + 1), (s_sc[k], 16 * J * q))
                for dst, src in ((ix[k][:, :], words(T["SCAT"], n)), (ag[k][:, :, :], rows(T["AG"], n)),
                                 (h[k][:, :, :], rows(T["HN3"], n)), (x3[k][:, :, :], rows(T["X3"], n))):
                    sp.dma_start(dst, src).then_inc(s_ld[k], 16)
            flow(sp, [(0, load)], slots=SL)

        @block.vector
        def _(dve):
            v = nc.vector
            ch = Chain(dve, s_ch, 2)
            k1, k0 = (C[w][:, :].unsqueeze(1).to_broadcast([P, J, D]) for w in ("k1", "k0"))

            def batch(n, k, q, old):
                ch.at(n)
                dve.wait_ge(s_ld[k], 64 * (q + 1))
                ch(v.tensor_tensor(t1[k][:, :, :], ag[k][:, :, :], k1, ALU.mult))
                ch(v.tensor_tensor(t2[k][:, :, :], t1[k][:, :, :], h[k][:, :, :], ALU.add))
                v.tensor_tensor(t3[k][:, :, :], t2[k][:, :, :], k0, ALU.add).then_inc(s_t, 1)
                ch.done()

            def result(n, k, q, old):
                dve.wait_ge(s_gl, n + 1)
                if old:
                    dve.wait_ge(s_sc[k], 16 * J * q)
                v.tensor_tensor(y[k][:, :, :], gl[k][:, :, :], x3[k][:, :, :], ALU.add).then_inc(s_y, 1)
            flow(dve, [(3, result), (1, batch)], slots=SL)

        @block.scalar
        def _(act):
            def gelu(n, k, q, old):
                act.wait_ge(s_t, n + 1)
                nc.scalar.activation(gl[k][:, :, :], t3[k][:, :, :], ACT.Gelu).then_inc(s_gl, 1)
            flow(act, [(2, gelu)], slots=SL)

        @block.gpsimd
        def _(pool):
            def scatter(n, k, q, old):
                hold(pool, s_turn, (s_y, n + 1), (s_ld[k], 64 * (q + 1)))
                for j in range(J):
                    nc.gpsimd.indirect_dma_start(
                        out, bass.IndirectOffsetOnAxis(ap=ix[k][:, j:j + 1], axis=0), y[k][:, j, :], None,
                        bounds_check=N - 1, oob_is_err=False).then_inc(s_sc[k], 16)
            flow(pool, [(3, scatter)], slots=SL)
            for k in four:
                pool.wait_ge(s_sc[k], 16 * J * chunks_of(k, SL))



_INS = ['x', 'src', 'dst', 'edge_attr_t', 'w_comp_t', 'edge_type_4', 'edge_weight1', 'node_type_2',
        'L0_gnn_w1_l', 'L0_gnn_w1_r', 'L0_gnn_w1_e', 'L0_gnn_att1', 'L0_gnn_b1', 'L0_gnn_w2_l', 'L0_gnn_w2_r',
        'L0_gnn_w2_e', 'L0_gnn_att2', 'L0_gnn_b2', 'L0_gnn_wc', 'L0_gnn_bc', 'L0_gnn_ln_g', 'L0_gnn_ln_b',
        'L0_gnn_wr', 'L0_gnn_br', 'L0_gnn_lnr_g', 'L0_gnn_lnr_b', 'L1_gnn_W', 'L1_gnn_a', 'L2_gnn_weight',
        'L2_gnn_bias', 'L3_gnn_W_l', 'L3_gnn_b_l', 'L3_gnn_W_r', 'L3_gnn_b_r', 'L3_gnn_W_e',
        'L3_gnn_att', 'L3_gnn_bias', 'L3_gnn_gamma', 'L3_gnn_beta']



def program(nc, a, out):
    T = {}

    def table(name, shape, dt=F32):
        T[name] = nc.dram_tensor(f"t_{name}", shape, dt, kind="Internal").ap()

    for name in ("SRC", "DST", "SCAT", "POS", "PSRC", "PDST", "VSRC", "VDST"):
        table(name, [EP], I32)
    for name in ("START", "KEEP", "ENDM", "ET"):
        table(name, [EP])
    table("LP", [P * NTAB], I32)
    table("LPT", [P * NTAB], I32)
    T["EWP"] = nc.dram_tensor("t_EWP", [9, EP], BF16, kind="Internal").ap()
    table("EA", [18, EP])
    table("XSD", [EP, 2 * D])
    table("SSRC", [SORTED + 2])
    table("EID", [SORTED], I32)
    table("EL", [SORTED])
    table("AL", [SORTED])
    table("H1", [EP, P])
    table("HR", [EP, D])
    for name in ("D1", "D2", "D3", "D1D", "HS", "AG", "X3", "HN3"):
        table(name, [EP, D])
    for name in ("SE", "SA", "REL"):
        table(name, [EP])
    with ExitStack() as ctx:
        m = Mem(nc, ctx, "c")
        C = {name: m.sb(name, shape) for name, shape in (
            ("ident", [P, P]), ("sel8", [8, P]), ("sel2", [2, P]), ("sel4", [4, D]), ("att1b", [P, 8]),
            ("att2b", [P, 2]), ("att3b", [D, 4]), ("ones_row", [1, P]), ("wz1", [P, P]), ("we1", [1, P]),
            ("wl2", [P, P]), ("wr2", [P, P]), ("we2", [1, P]), ("wz3", [P, P]), ("we3", [18, P]), ("b1", [P, 1]),
            ("b2", [D, 1]),
            ("b1row", [1, P]), ("brow", [1, P]), ("cstk", [P, D]), ("ones_sq", [P, P]),
            ("lng", [P, D]), ("lnb", [P, D]), ("lrg", [P, D]), ("lrb", [P, D]), ("gamma", [P, D]), ("beta", [P, D]),
            ("bias3", [P, D]), ("bias2", [P, D]), ("wca", [D + 1, D]), ("wra", [D + 1, D]), ("w1", [D, D]),
            ("a1", [D, 2]), ("wflat", [P, 4, D]), ("w1t", [D, D]), ("wb", [P, P]), ("wft", [D, 4, P]),
            ("relp", [P, 4]), ("c3row", [1, D]), ("c3", [P, D]), ("k1", [P, D]), ("k0", [P, D]), ("bl3", [D, 1]))}
        for name in ("we1p", "we2p"):
            C[name] = m.sb(name, [9, P], BF16)
        setup_block(nc, a, T, C)
        weights_block(nc, T, C)
        index_block(nc, a, T, C)
        gat_block(nc, a, T, C, "a", 8, P, False)
        positions_block(nc, T)
        gat_block(nc, a, T, C, "b", 2, P, True)
        mlp_block(nc, T, C)
        logit_block(nc, T, C)
        permute_block(nc, T, "ps", True)
        softmax_block(nc, T, C)
        permute_block(nc, T, "pb", False)
        mix_block(nc, T, C)
        relation_block(nc, T, C)
        gat_block(nc, a, T, C, "g", 4, D, False)
        batch_block(nc, T, C)
        nodes_block(nc, a, out, C)
        targets_block(nc, T, out, C)


def kernel(**inputs):
    import numpy as _np
    import concourse.bacc as _bacc
    from concourse import mybir as _mybir
    from concourse.bass_utils import run_bass_kernel_spmd as _run

    nc = _bacc.Bacc("TRN2", target_bir_lowering=False, num_devices=1)
    inputs = dict(inputs)
    inputs["edge_attr_t"] = _np.asarray(inputs["edge_attr_16"]).T
    inputs["w_comp_t"] = _np.asarray(inputs["L2_gnn_w_comp"]).T
    arrays, args = {}, {}
    for name in _INS:
        v = _np.ascontiguousarray(inputs[name])
        arrays[f"in_{name}"] = v
        args[name] = nc.dram_tensor(f"in_{name}", v.shape, _mybir.dt.from_np(v.dtype), kind="ExternalInput").ap()
    out = nc.dram_tensor("out", (N, D), F32, kind="ExternalOutput").ap()
    program(nc, args, out)
    r = _run(nc, [arrays], core_ids=[0])
    return r.results[0]["out"]
```
